# Optimizing a Trainium2 kernel written in Bass

```python
import numpy as np
import jax
import jax.numpy as jnp

def _softmax(x, axis=-1):
    return jax.nn.softmax(x, axis=axis)

def _gelu(x):
    return jax.nn.gelu(x, approximate=True)

def _silu(x):
    return jax.nn.silu(x)

def _sigmoid(x):
    return jax.nn.sigmoid(x)

def _layernorm(x, axis=-1, eps=1e-05):
    m = jnp.mean(x, axis=axis, keepdims=True)
    v = jnp.var(x, axis=axis, keepdims=True)
    return (x - m) / jnp.sqrt(v + eps)

def _scatter_add(tgt, idx, src, axis=0):
    return tgt.at[idx].add(src)

def _segment_sum(src, seg, n):
    return jax.ops.segment_sum(src, seg, n)
kernel_name = 'mk_hybrid_d1_jaxref_r4_88188e'

def setup_inputs(seed: int=0):
    np.random.seed(seed)
    _w = jnp.asarray

    def _L0_attn_a_setup():
        import jax, jax.numpy as jnp
        import numpy as np
        EPS = 1e-05
        key = jax.random.key(seed)
        ks = jax.random.split(key, 16)
        B, T, D = (8, 512, 256)
        Hh, KD, VD, LR, GLR = (4, 128, 256, 32, 64)
        s = 0.02
        w = lambda k, shape: jax.random.normal(k, shape, jnp.float32) * s
        return {'hidden_states': jax.random.normal(ks[0], (B, T, D), jnp.float32), 'mu_x': w(ks[1], (D,)), 'W_x1': w(ks[2], (5 * LR, D)), 'W_x2': w(ks[3], (D, 5 * LR)), 'x_bias': jnp.zeros((5, D), jnp.float32), 'W_r': w(ks[4], (KD, D)), 'W_k': w(ks[5], (KD, D)), 'W_v': w(ks[6], (VD, D)), 'W_g': w(ks[7], (VD, D)), 'A_w': w(ks[8], (GLR, D)), 'B_w': w(ks[9], (KD, GLR)), 'b_w': jnp.zeros((KD,), jnp.float32), 'bonus': w(ks[10], (Hh, KD // Hh)), 'gn_weight': jnp.ones((VD,), jnp.float32), 'gn_bias': jnp.zeros((VD,), jnp.float32), 'W_o': w(ks[11], (D, VD))}
    _L0_attn_a_in = _L0_attn_a_setup()

    def _L0_attn_b_setup():
        import jax, jax.numpy as jnp
        import numpy as np
        import math

        def _alibi_slopes(n_heads):

            def pow2(n):
                start = 2 ** (-2 ** (-(math.log2(n) - 3)))
                return [start ** i for i in range(n)]
            if math.log2(n_heads).is_integer():
                slopes = pow2(n_heads)
            else:
                closest = 2 ** math.floor(math.log2(n_heads))
                slopes = pow2(closest) + _alibi_slopes(2 * closest).tolist()[0::2][:n_heads - closest]
            return np.asarray(slopes, dtype=np.float32)
        key = jax.random.key(seed)
        ks = jax.random.split(key, 4)
        B, L, D = (2, 512, 256)
        s = 1.0 / math.sqrt(D)
        return {'x': jax.random.normal(ks[0], (B, L, D), jnp.float32), 'Wqkv': jax.random.normal(ks[1], (D, 3 * D), jnp.float32) * s, 'bqkv': jnp.zeros((3 * D,), jnp.float32), 'Wout': jax.random.normal(ks[2], (D, D), jnp.float32) * s, 'bout': jnp.zeros((D,), jnp.float32)}
    _L0_attn_b_in = _L0_attn_b_setup()

    def _L0_ffn_setup():
        import jax, jax.numpy as jnp
        import numpy as np

        def _bitlinear(x, w_latent):
            scale = jax.lax.stop_gradient(jnp.clip(jnp.mean(jnp.abs(w_latent), axis=1, keepdims=True), 1e-05, None))
            tern = jnp.clip(jnp.round(w_latent / scale), -1.0, 1.0)
            w = w_latent + jax.lax.stop_gradient(tern - w_latent)
            return x @ (w * scale).T
        key = jax.random.key(seed)
        ks = jax.random.split(key, 6)
        dim, hidden, rank = (256, 1024, 16)
        B, S = (4, 1024)
        x = jax.random.normal(ks[0], (B, S, dim), dtype=jnp.float32)
        w_fc = 0.02 * jax.random.normal(ks[1], (hidden, dim), dtype=jnp.float32)
        w_proj = 0.02 * jax.random.normal(ks[2], (dim, hidden), dtype=jnp.float32)
        u = 0.02 * jax.random.normal(ks[3], (hidden, rank), dtype=jnp.float32)
        v = 0.02 * jax.random.normal(ks[4], (rank, dim), dtype=jnp.float32)
        fast_b = jax.random.normal(ks[5], (rank, rank), dtype=jnp.float32)
        gate = jnp.float32(0.05)
        return {'x': x, 'fast_b': fast_b, 'w_fc': w_fc, 'w_proj': w_proj, 'u': u, 'v': v, 'gate': gate}
    _L0_ffn_in = _L0_ffn_setup()
    _d = {'L0_attn_a_hidden_states': _L0_attn_a_in['hidden_states'], 'L0_attn_a_mu_x': _L0_attn_a_in['mu_x'], 'L0_attn_a_W_x1': _L0_attn_a_in['W_x1'], 'L0_attn_a_W_x2': _L0_attn_a_in['W_x2'], 'L0_attn_a_x_bias': _L0_attn_a_in['x_bias'], 'L0_attn_a_W_r': _L0_attn_a_in['W_r'], 'L0_attn_a_W_k': _L0_attn_a_in['W_k'], 'L0_attn_a_W_v': _L0_attn_a_in['W_v'], 'L0_attn_a_W_g': _L0_attn_a_in['W_g'], 'L0_attn_a_A_w': _L0_attn_a_in['A_w'], 'L0_attn_a_B_w': _L0_attn_a_in['B_w'], 'L0_attn_a_b_w': _L0_attn_a_in['b_w'], 'L0_attn_a_bonus': _L0_attn_a_in['bonus'], 'L0_attn_a_gn_weight': _L0_attn_a_in['gn_weight'], 'L0_attn_a_gn_bias': _L0_attn_a_in['gn_bias'], 'L0_attn_a_W_o': _L0_attn_a_in['W_o'], 'L0_attn_b_Wqkv': _L0_attn_b_in['Wqkv'], 'L0_attn_b_bqkv': _L0_attn_b_in['bqkv'], 'L0_attn_b_Wout': _L0_attn_b_in['Wout'], 'L0_attn_b_bout': _L0_attn_b_in['bout'], 'L0_ffn_fast_b': _L0_ffn_in['fast_b'], 'L0_ffn_w_fc': _L0_ffn_in['w_fc'], 'L0_ffn_w_proj': _L0_ffn_in['w_proj'], 'L0_ffn_u': _L0_ffn_in['u'], 'L0_ffn_v': _L0_ffn_in['v'], 'L0_ffn_gate': _L0_ffn_in['gate']}
    _x0 = _d['L0_attn_a_hidden_states']
    _d['L0_attn_a_hidden_states'] = jax.random.normal(jax.random.fold_in(jax.random.key(seed), 1), (8, 1024, 256), dtype=_x0.dtype)
    del _x0
    return _d

def reference(L0_attn_a_hidden_states, L0_attn_a_mu_x, L0_attn_a_W_x1, L0_attn_a_W_x2, L0_attn_a_x_bias, L0_attn_a_W_r, L0_attn_a_W_k, L0_attn_a_W_v, L0_attn_a_W_g, L0_attn_a_A_w, L0_attn_a_B_w, L0_attn_a_b_w, L0_attn_a_bonus, L0_attn_a_gn_weight, L0_attn_a_gn_bias, L0_attn_a_W_o, L0_attn_b_Wqkv, L0_attn_b_bqkv, L0_attn_b_Wout, L0_attn_b_bout, L0_ffn_fast_b, L0_ffn_w_fc, L0_ffn_w_proj, L0_ffn_u, L0_ffn_v, L0_ffn_gate):

    def _L0_attn_a_ref(hidden_states, mu_x, W_x1, W_x2, x_bias, W_r, W_k, W_v, W_g, A_w, B_w, b_w, bonus, gn_weight, gn_bias, W_o):
        import jax, jax.numpy as jnp
        import numpy as np
        EPS = 1e-05
        B, T, D = hidden_states.shape
        Hh = bonus.shape[0]
        x = hidden_states
        shifted = jnp.pad(x, ((0, 0), (1, 0), (0, 0)))[:, :T]
        delta = shifted - x
        lr = W_x1.shape[0] // 5
        z = jnp.tanh((x + delta * mu_x) @ W_x1.T).reshape(B, T, 5, lr)
        mus = jnp.einsum('blnr,dnr->blnd', z, W_x2.reshape(D, 5, lr)) + x_bias
        r_mu, w_mu, k_mu, v_mu, g_mu = (mus[:, :, i] for i in range(5))
        r = (x + delta * r_mu) @ W_r.T
        w = jnp.tanh((x + delta * w_mu) @ A_w.T) @ B_w.T + b_w
        k = (x + delta * k_mu) @ W_k.T
        v = (x + delta * v_mu) @ W_v.T
        g = (x + delta * g_mu) @ W_g.T
        K = W_r.shape[0] // Hh
        V = W_v.shape[0] // Hh
        r = r.reshape(B, T, Hh, K)
        k = k.reshape(B, T, Hh, K)
        w = -jnp.exp(w.reshape(B, T, Hh, K))
        v = v.reshape(B, T, Hh, V)
        u = bonus

        def step(S, inp):
            q_t, k_t, v_t, w_t = inp
            kv = k_t[..., :, None] * v_t[..., None, :]
            o_t = jnp.einsum('bhk,bhkv->bhv', q_t, S + u[None, :, :, None] * kv)
            S = jnp.exp(w_t)[..., None] * S + kv
            return (S, o_t)
        S0 = jnp.zeros((B, Hh, K, V), dtype=x.dtype)
        xs = (jnp.swapaxes(r, 0, 1), jnp.swapaxes(k, 0, 1), jnp.swapaxes(v, 0, 1), jnp.swapaxes(w, 0, 1))
        _, o = jax.lax.scan(step, S0, xs)
        o = jnp.swapaxes(o, 0, 1)
        mean = o.mean(-1, keepdims=True)
        var = o.var(-1, keepdims=True)
        o = (o - mean) / jnp.sqrt(var + EPS)
        o = o.reshape(B, T, Hh * V) * gn_weight + gn_bias
        o = o * jax.nn.silu(g)
        return o @ W_o.T

    def _L0_attn_b_ref(x, Wqkv, bqkv, Wout, bout):
        import jax, jax.numpy as jnp
        import numpy as np
        import math

        def _alibi_slopes(n_heads):

            def pow2(n):
                start = 2 ** (-2 ** (-(math.log2(n) - 3)))
                return [start ** i for i in range(n)]
            if math.log2(n_heads).is_integer():
                slopes = pow2(n_heads)
            else:
                closest = 2 ** math.floor(math.log2(n_heads))
                slopes = pow2(closest) + _alibi_slopes(2 * closest).tolist()[0::2][:n_heads - closest]
            return np.asarray(slopes, dtype=np.float32)
        n_heads = 16
        B, L, D = x.shape
        head_dim = D // n_heads
        qkv = (x @ Wqkv + bqkv).reshape(B, L, 3, n_heads, head_dim)
        q, k, v = (qkv[:, :, 0], qkv[:, :, 1], qkv[:, :, 2])
        scores = jnp.einsum('bqhd,bkhd->bhqk', q, k) / math.sqrt(head_dim)
        pos = jnp.arange(L)
        bias = -jnp.abs(pos[None, :] - pos[:, None]).astype(jnp.float32)
        slopes = jnp.asarray(_alibi_slopes(n_heads))
        scores = scores + slopes[None, :, None, None] * bias[None, None]
        probs = jax.nn.softmax(scores, axis=-1)
        out = jnp.einsum('bhqk,bkhd->bqhd', probs, v).reshape(B, L, D)
        return out @ Wout + bout

    def _L0_ffn_ref(x, fast_b, w_fc, w_proj, u, v, gate):
        import jax, jax.numpy as jnp
        import numpy as np

        def _bitlinear(x, w_latent):
            scale = jax.lax.stop_gradient(jnp.clip(jnp.mean(jnp.abs(w_latent), axis=1, keepdims=True), 1e-05, None))
            tern = jnp.clip(jnp.round(w_latent / scale), -1.0, 1.0)
            w = w_latent + jax.lax.stop_gradient(tern - w_latent)
            return x @ (w * scale).T
        h = _bitlinear(x, w_fc) + gate * (x @ v.T @ fast_b.T @ u.T)
        r = jnp.maximum(h, 0.0)
        return _bitlinear(r * r, w_proj)
    x = L0_attn_a_hidden_states
    x = x + _L0_attn_a_ref(_layernorm(x, axis=-1), L0_attn_a_mu_x, L0_attn_a_W_x1, L0_attn_a_W_x2, L0_attn_a_x_bias, L0_attn_a_W_r, L0_attn_a_W_k, L0_attn_a_W_v, L0_attn_a_W_g, L0_attn_a_A_w, L0_attn_a_B_w, L0_attn_a_b_w, L0_attn_a_bonus, L0_attn_a_gn_weight, L0_attn_a_gn_bias, L0_attn_a_W_o)
    x = x + _L0_ffn_ref(_layernorm(x, axis=-1), L0_ffn_fast_b, L0_ffn_w_fc, L0_ffn_w_proj, L0_ffn_u, L0_ffn_v, L0_ffn_gate)
    x = x + _L0_attn_b_ref(_layernorm(x, axis=-1), L0_attn_b_Wqkv, L0_attn_b_bqkv, L0_attn_b_Wout, L0_attn_b_bout)
    x = x + _L0_ffn_ref(_layernorm(x, axis=-1), L0_ffn_fast_b, L0_ffn_w_fc, L0_ffn_w_proj, L0_ffn_u, L0_ffn_v, L0_ffn_gate)
    return x

_drawn_inputs = setup_inputs


def setup_inputs(seed=0):
    import zlib

    import numpy as np

    out = dict(_drawn_inputs(seed))
    spreads = {'L0_attn_a_x_bias': (0.0, 0.379),
     'L0_attn_a_b_w': (0.0, 0.8),
     'L0_attn_a_gn_weight': (1.0, 0.6),
     'L0_attn_a_gn_bias': (0.0, 0.8),
     'L0_attn_b_bqkv': (0.0, 0.28),
     'L0_attn_b_bout': (0.0, 0.1)}
    factors = {'L0_attn_a_mu_x': 8.0,
     'L0_attn_a_W_x1': 7.776,
     'L0_attn_a_W_x2': 7.727,
     'L0_attn_a_A_w': 8.0,
     'L0_attn_a_B_w': 8.0,
     'L0_attn_a_bonus': 8.0,
     'L0_ffn_fast_b': 8.0,
     'L0_ffn_u': 8.0,
     'L0_ffn_v': 8.0}
    for name, (base, spread) in spreads.items():
        noise = np.random.default_rng([zlib.crc32(name.encode()), seed]).standard_normal(out[name].shape)
        drawn = base * np.exp(spread * noise) if base else spread * noise
        out[name] = jnp.asarray(drawn.astype(out[name].dtype))
    for name, factor in factors.items():
        out[name] = (out[name] * factor).astype(out[name].dtype)
    return out
```

```python
import math
from contextlib import ExitStack

import numpy as np
from concourse import mybir

F32 = mybir.dt.float32
F32R = mybir.dt.float32r
ALU = mybir.AluOpType
ACT = mybir.ActivationFunctionType
AX = mybir.AxisListType

P = 128
BATCH, SEQ, DIM = 8, 1024, 256
KT = DIM // P
TOKENS = BATCH * SEQ
TILES = TOKENS // P
BANK = 512
CHUNK = BANK
CT = CHUNK // P
CHUNKS = TOKENS // CHUNK
EPS = 1e-5

HEADS_A, KD, VD, LOWRANK, GATERANK, MIXES = 4, 128, 256, 32, 64, 5
HK, HV = KD // HEADS_A, VD // HEADS_A
SUB = 32
DIAG = 6
TREE = 7

HIDDEN, RANK = 1024, 16
HT = HIDDEN // P

HEADS, HD, GROUP = 16, 16, 4
GROUPS = HEADS // GROUP
QB = SEQ // P
HALVES = SEQ // BANK
MAIN = 3 * HD
BIASROWS = 4 * QB
SHIFTROW = 96
STACK = SHIFTROW + 2


def round12(a):
    m, e = np.frexp(np.asarray(a, np.float64))
    return np.ldexp(np.rint(m * 4096) / 4096, e).astype(np.float32)


def hi_lo(a):
    hi = round12(a)
    return hi, round12(a - hi)


def slopes():
    start = 2 ** (-2 ** (-(math.log2(HEADS) - 3)))
    return np.asarray([start ** i for i in range(HEADS)], dtype=np.float32)


SLOPE_LO = [h for h in range(HEADS) if hi_lo(slopes()[h])[1] != 0]


def constants():
    c = {"c_ident": np.eye(P, dtype=np.float32)}
    s, t = np.arange(P)[:, None] % SUB, np.arange(SUB)[None, :]
    parts = [s == t]
    for level in range(DIAG - 1):
        m = 1 << level
        parts.append((s // (2 * m) == t // (2 * m)) & (s // m % 2 == 0) & (t // m % 2 == 1))
    c["c_mask"] = np.stack(parts, 1).astype(np.float32).reshape(P, DIAG * SUB)
    q = np.arange(SEQ)
    picked = (q[None, :] // P == np.arange(QB)[:, None]).astype(np.float32)
    c["c_qbias"] = np.concatenate([picked * (q % P)] * 2 + [picked] * 2).astype(np.float32)
    i, j = np.arange(QB)[:, None], q[None, :] // P
    sign = np.sign(i - j)
    near = np.arange(P)
    kbias, diag = [], []
    for h, slope in enumerate(slopes().astype(np.float64)):
        a, b = hi_lo(-slope * sign), hi_lo(slope * (sign * (q % P) - P * np.abs(i - j)))
        kbias.append(np.concatenate([a[0], a[1], b[0], b[1]]))
        d = hi_lo(-slope * np.abs(near[:, None] - near[None, :]))
        diag += [d[0]] + [d[1]] * (h in SLOPE_LO)
    c["c_kbias"] = np.stack(kbias)
    c["c_diag"] = np.stack(diag, 1)
    return {k: np.ascontiguousarray(v) for k, v in c.items()}


class Queue:

    def __init__(self, sem):
        self.sem, self.items, self.count, self.reached = sem, [], 0, {}

    def do(self, issue):
        self.items.append([issue, None, 0])

    def wait(self, *tokens):
        for sem, value in tokens:
            if self.reached.get(sem.name, 0) < value:
                self.reached[sem.name] = value
                self.items.append([None, sem, value])

    def mark(self):
        last = self.items[-1]
        if last[1] is None:
            self.count += 1
            last[1], last[2] = self.sem, 1
            self.marked = (self.sem, self.count)
        return self.marked

    def emit(self, engine):
        for issue, sem, value in self.items:
            if issue is None:
                engine.wait_ge(sem, value)
            elif sem is None:
                issue(engine)
            else:
                issue(engine).then_inc(sem, value)
        self.items = []


class Lane:

    def __init__(self, sem):
        self.sem, self.count = sem, 0

    def start(self, queue, out, in_):
        self.count += 16
        queue.items.append([lambda e: e.dma_start(out, in_), self.sem, 16])
        return (self.sem, self.count)


class Slot:

    def __init__(self, buf):
        self.buf, self.read = buf, ()


class Ring:
    def __init__(self, bufs):
        self.slots, self.n = [Slot(b) for b in bufs], 0

    def take(self):
        self.n += 1
        return self.slots[(self.n - 1) % len(self.slots)]


def matmul(pe, out, lhsT, rhs, start=True, stop=True, tile=None):
    if tile is None:
        pe.do(lambda e: e.matmul(out, lhsT, rhs, start=start, stop=stop))
    else:
        pe.do(lambda e: e.matmul(out, lhsT, rhs, start=start, stop=stop, tile_position=tile))


def transpose(pe, out, in_, ident):
    pe.do(lambda e: e.transpose(out, in_, ident))


def activation(act, out, in_, func, bias=0.0, scale=1.0):
    act.do(lambda e: e.activation(out, in_, func, bias=bias, scale=scale))


def copy(q, out, in_):
    q.do(lambda e: e.tensor_copy(out, in_))


def act_copy(act, out, in_):
    act.do(lambda e: e.activation(out, in_, ACT.Copy))


def tensor2(q, out, a, b, op):
    q.do(lambda e: e.tensor_tensor(out, a, b, op))


def scalar2(q, out, in_, s1, s2, op0, op1):
    q.do(lambda e: e.tensor_scalar(out, in_, s1, s2, op0, op1))


def scalar1(q, out, in_, s1, op0):
    q.do(lambda e: e.tensor_scalar(out, in_, s1, None, op0))


def fused(dve, out, in0, scalar, in1, op0, op1):
    dve.do(lambda e: e.scalar_tensor_tensor(out=out, in0=in0, scalar=scalar, in1=in1, op0=op0, op1=op1))


def reduce(dve, out, in_, op, negate=False, absolute=False):
    dve.do(lambda e: e.tensor_reduce(out, in_, axis=AX.X, op=op, negate=negate, apply_absolute_value=absolute))


def memset(q, out, value):
    q.do(lambda e: e.memset(out, value))


def spread(ap, n):
    return ap.unsqueeze(len(ap.shape)).to_broadcast(list(ap.shape) + [n])


def words(ap):
    return ap.bitcast(F32)


def together(*steps):
    steps = [s for s in steps if s is not None]
    while steps:
        for s in list(steps):
            if next(s, steps) is steps:
                steps.remove(s)


class Core:
    def __init__(self, nc, ctx):
        self.nc = nc
        sem = lambda n: ctx.enter_context(nc.semaphore(n))
        self.pe, self.act, self.dve = Queue(sem("pe_done")), Queue(sem("act_done")), Queue(sem("dve_done"))
        self.pool, self.sp = Queue(sem("pool_done")), Queue(sem("sp_done"))
        self.banks = ctx.enter_context(nc.psum_tensor("banks", [P, 8, BANK], F32))

    def run(self):
        with self.nc.Block() as block:
            block.sync(self.sp.emit)
            block.tensor(self.pe.emit)
            block.scalar(self.act.emit)
            block.vector(self.dve.emit)
            block.gpsimd(self.pool.emit)


class Normalizer:

    def __init__(self, core, sb, name, tiles):
        self.core, self.tiles = core, tiles
        self.stats = sb(f"{name}_stats", [P, tiles, 6])
        self.mean_var = sb(f"{name}_mean_var", [P, tiles, 2])
        self.rstd = sb(f"{name}_rstd", [P, tiles])
        self.minus_half = sb(f"{name}_minus_half", [P, tiles])
        memset(core.pool, self.minus_half[:, :], -0.5)
        self.ready = core.pool.mark()
        self.applied = ()

    def statistics(self, x, first, arrived):
        dve, pool = self.core.dve, self.core.pool
        dve.wait(*arrived, *self.applied)
        for i in range(self.tiles):
            dve.do(lambda e, i=i: e.bn_stats(self.stats[:, i, :], x[:, first + i, :]))
        dve.wait(dve.mark())
        for i in range(self.tiles):
            dve.do(lambda e, i=i: e.bn_aggr(self.mean_var[:, i, :], self.stats[:, i, :]))
        pool.wait(self.ready, dve.mark())
        scalar1(pool, self.rstd[:, :], self.mean_var[:, :, 1], EPS, ALU.add)
        pool.wait(pool.mark())
        tensor2(pool, self.rstd[:, :], self.rstd[:, :], self.minus_half[:, :], ALU.pow)
        return pool.mark()

    def scale(self, out, x, first, i):
        scalar2(self.core.dve, out, x[:, first + i, :], self.mean_var[:, i, 0:1], self.rstd[:, i:i + 1],
                ALU.subtract, ALU.mult)


def recurrent_mixer(core, x, x_dram, d):
    nc, pe, act, dve, pool, sp, banks = core.nc, core.pe, core.act, core.dve, core.pool, core.sp, core.banks
    with ExitStack() as ctx:
        sb = lambda n, s, dt=F32: ctx.enter_context(nc.sbuf_tensor("a_" + n, s, dt))
        lane = lambda n: Lane(ctx.enter_context(nc.semaphore("a_" + n)))
        C2 = 2 * SUB

        ident, mask = sb("ident", [P, P]), sb("mask", [P, DIAG * SUB])
        mu_x, x_bias = sb("mu_x", [P, KT]), sb("x_bias", [P, MIXES, KT])
        w_x1 = sb("w_x1", [P, KT, 2 * P])
        w_x2 = sb("w_x2", [P, MIXES, DIM])
        w_r, w_k = sb("w_r", [P, KT, KD]), sb("w_k", [P, KT, KD])
        w_v, w_g, w_o = sb("w_v", [P, KT, VD]), sb("w_g", [P, KT, VD]), sb("w_o", [P, KT, DIM])
        w_a, w_b = sb("w_a", [P, KT, GATERANK]), sb("w_b", [GATERANK, KD])
        b_w, bonus = sb("b_w", [P, 1]), sb("bonus", [P, 1])
        gn_w, gn_b = sb("gn_w", [P, VD]), sb("gn_b", [P, VD])

        xn = Ring([sb(f"xn{i}", [P, DIM]) for i in range(4)])
        xn_t = [sb(f"xn_t{i}", [P, KT, 1 + CHUNK]) for i in range(2)]
        delta = sb("delta", [P, KT, CHUNK])
        z = sb("z", [P, 2, CHUNK])
        mix = Ring([sb(f"mix{i}", [P, KT, CHUNK]) for i in range(2)])
        gate_low = sb("gate_low", [GATERANK, CHUNK])
        w_exp = sb("w_exp", [P, CHUNK])
        decay = [sb(f"decay{i}", [P, 2 * CHUNK]) for i in range(2)]
        q = [sb(f"q{i}", [P, CHUNK]) for i in range(2)]
        k = [sb(f"k{i}", [P, CHUNK]) for i in range(2)]
        q_up = [None] + [sb(f"q_up{l}", [P, CHUNK]) for l in range(1, TREE + 1)]
        k_up = [None] + [sb(f"k_up{l}", [P, CHUNK]) for l in range(1, TREE + 1)]
        k_bonus = sb("k_bonus", [P, CHUNK])
        v = [sb(f"v{i}", [P, CT, VD]) for i in range(2)]
        g_tanh = sb("g_tanh", [P, CT, VD])
        gate = [sb(f"gate{i}", [P, CT, VD]) for i in range(2)]
        masked = sb("masked", [P, HEADS_A, DIAG * SUB])
        diag = sb("diag", [P, HEADS_A, SUB])
        pair = Ring([sb(f"pair{i}", [P, HEADS_A, P]) for i in range(2)])
        k_tok = Ring([sb(f"k_tok{i}", [P, P]) for i in range(2)])
        state = [sb(f"state{i}", [P, VD]) for i in range(2)]
        o = sb("o", [P, CT, VD])
        o_sq = sb("o_sq", [P, CT, VD])
        o_t = sb("o_t", [P, KT, CHUNK])
        sums, rstd, half = sb("sums", [P, CT * HEADS_A]), sb("rstd", [P, CT * HEADS_A]), sb("half", [P, CT * HEADS_A])

        weights, x_lanes = lane("weights"), [lane(f"x{c}") for c in range(CHUNKS)]
        for w in (w_x1, w_x2):
            memset(pool, w[:], 0.0)
        sp.wait(pool.mark())
        tiled = lambda ap: ap.rearrange("(k p) n -> p k n", p=P)
        column = lambda ap: ap.rearrange("(p a) -> p a", a=1)
        x_view = x_dram.rearrange("b (t p) c -> p (b t) c", p=P)
        x_here = []

        def load_x(c):
            x_here.append(x_lanes[c].start(sp, x[:, c * CT:(c + 1) * CT, :], x_view[:, c * CT:(c + 1) * CT, :]))

        load_x(0)
        weights.start(sp, ident[:, :], d["c_ident"])
        weights.start(sp, mu_x[:, :], d["mu_x"])
        weights.start(sp, w_x1[:, :, 0:MIXES * LOWRANK], tiled(d["W_x1"]))
        for n in range(MIXES):
            r = n * LOWRANK % P
            weights.start(sp, w_x2[r:r + LOWRANK, n, :], d["W_x2"][n * LOWRANK:(n + 1) * LOWRANK, :])
        weights.start(sp, x_bias[:, :, :], d["x_bias"])
        for t, name in ((w_r, "W_r"), (w_k, "W_k"), (w_v, "W_v"), (w_g, "W_g"), (w_o, "W_o"), (w_a, "A_w")):
            weights.start(sp, t[:, :, :], tiled(d[name]))
        weights.start(sp, w_b[:, :], d["B_w"])
        weights.start(sp, b_w[:, :], column(d["b_w"]))
        weights.start(sp, bonus[:, :], column(d["bonus"].rearrange("h k -> (h k)")))
        weights.start(sp, mask[:, :], d["c_mask"])
        weights.start(sp, gn_w[:, :], d["gn_weight"].partition_broadcast(P))
        loaded = weights.start(sp, gn_b[:, :], d["gn_bias"].partition_broadcast(P))
        for c in range(1, CHUNKS):
            load_x(c)
        for s in pair.slots:
            memset(pool, s.buf[:], 0.0)
        for s in state:
            memset(pool, s[:, :], 0.0)
        memset(pool, half[:, :], -0.5)
        zeroed = pool.mark()
        norm = Normalizer(core, sb, "norm", CT)
        for e in (pe, act, dve, pool):
            e.wait(loaded, zeroed)

        bank = lambda i: banks[:, i, :]
        front, back = Ring([bank(0), bank(1)]), Ring([bank(2), bank(3)])
        products = Slot(banks[:, 4:8, :])
        done = {}
        got = lambda what, c: done.get((what, c), ())

        def prepare(c):
            par, first = c % 2, c * CT
            xt, q0, k0, dec = xn_t[par], q[par], k[par], decay[par]
            rstd_done = norm.statistics(x, first, [x_here[c]])
            dve.wait(rstd_done)
            slots = []
            for i in range(CT):
                s = xn.take()
                dve.wait(*s.read)
                norm.scale(s.buf[:, :], x, first, i)
                slots.append((s, dve.mark()))
            norm.applied = (dve.mark(),)
            yield
            for kt in range(KT):
                b = front.take()
                pe.wait(*b.read)
                for i, (s, scaled) in enumerate(slots):
                    pe.wait(scaled)
                    transpose(pe, b.buf[:, i * P:(i + 1) * P], s.buf[:, kt * P:(kt + 1) * P], ident[:, :])
                    s.read = (pe.mark(),)
                act.wait(pe.mark(), *got("mixed", c - 2), *got("carried", c - 1))
                act_copy(act, xt[:, kt, 1:], b.buf)
                b.read = (act.mark(),)
            xt_done = act.mark()
            if c % (SEQ // CHUNK) == 0:
                pool.wait(*got("mixed", c - 2))
                memset(pool, xt[:, :, 0:1], 0.0)
            else:
                pool.wait(*got("xt", c - 1), *got("mixed", c - 2))
                copy(pool, xt[:, :, 0:1], xn_t[1 - par][:, :, CHUNK:CHUNK + 1])
            carried = pool.mark()
            done["carried", c], done["xt", c] = (carried,), (xt_done,)
            yield
            dve.wait(xt_done, carried, *got("mixed", c - 1))
            tensor2(dve, delta[:, :, :], xt[:, :, 0:CHUNK], xt[:, :, 1:], ALU.subtract)
            mixed_x = mix.take()
            dve.wait(dve.mark(), *mixed_x.read)
            for kt in range(KT):
                fused(dve, mixed_x.buf[:, kt, :], delta[:, kt, :], mu_x[:, kt:kt + 1], xt[:, kt, 1:], ALU.mult, ALU.add)
            mixed_done = dve.mark()
            for m in range(2):
                b = front.take()
                pe.wait(mixed_done, *b.read)
                for kt in range(KT):
                    matmul(pe, b.buf, w_x1[:, kt, m * P:(m + 1) * P], mixed_x.buf[:, kt, :], kt == 0, kt == KT - 1)
                act.wait(pe.mark(), *got("mus", c - 1))
                activation(act, z[:, m, :], b.buf, ACT.Tanh)
                b.read = (act.mark(),)
            mixed_x.read = (pe.mark(),)
            z_done = act.mark()
            yield

            def mix_in(n):
                s = mix.take()
                for kt in range(KT):
                    b = front.take()
                    pe.wait(z_done, *b.read)
                    matmul(pe, b.buf, w_x2[:, n, kt * P:(kt + 1) * P], z[:, n * LOWRANK // P, :])
                    dve.wait(pe.mark(), *s.read)
                    fused(dve, s.buf[:, kt, :], b.buf, x_bias[:, n, kt:kt + 1], delta[:, kt, :], ALU.add, ALU.mult)
                    b.read = (dve.mark(),)
                pool.wait(dve.mark())
                tensor2(pool, s.buf[:, :, :], s.buf[:, :, :], xt[:, :, 1:], ALU.add)
                return s, pool.mark()

            def project(w, s, mixed, rows=P):
                b = front.take()
                pe.wait(mixed, *b.read)
                for kt in range(KT):
                    matmul(pe, b.buf[0:rows, :], w[:, kt, :], s.buf[:, kt, :], kt == 0, kt == KT - 1)
                s.read = (pe.mark(),)
                return b, pe.mark()

            s, mixed = mix_in(1)
            yield
            b, projected = project(w_a, s, mixed, GATERANK)
            act.wait(projected, *got("w", c - 1))
            activation(act, gate_low[:, :], b.buf[0:GATERANK, :], ACT.Tanh)
            b.read = (act.mark(),)
            b = front.take()
            pe.wait(act.mark(), *b.read)
            matmul(pe, b.buf, w_b[:, :], gate_low[:, :])
            done["w", c] = (pe.mark(),)
            act.wait(pe.mark(), act.mark())
            activation(act, w_exp[:, :], b.buf, ACT.Exp, bias=b_w[:, 0:1])
            b.read = (act.mark(),)
            act.wait(act.mark(), *got("recurred", c - 2))
            activation(act, dec[:, 0:CHUNK], w_exp[:, :], ACT.Exp, scale=-1.0)
            done["decay", c] = (act.mark(),)
            yield
            for n, w, t, what in ((0, w_r, q0, "q"), (2, w_k, k0, "k")):
                s, mixed = mix_in(n)
                yield
                b, projected = project(w, s, mixed)
                act.wait(projected, *got("recurred", c - 2))
                act_copy(act, t[:, :], b.buf)
                b.read = (act.mark(),)
                done[what, c] = (act.mark(),)
                yield
            for n, w in ((3, w_v), (4, w_g)):
                s, mixed = mix_in(n)
                yield
                for half_chunk in range(CT // 2):
                    b = front.take()
                    pe.wait(mixed, *b.read)
                    for i in range(2):
                        tok = (2 * half_chunk + i) * P
                        for kt in range(KT):
                            matmul(pe, b.buf[:, i * VD:(i + 1) * VD], s.buf[:, kt, tok:tok + P], w[:, kt, :],
                                   kt == 0, kt == KT - 1)
                    s.read = (pe.mark(),)
                    two = slice(2 * half_chunk, 2 * half_chunk + 2)
                    bank2 = b.buf.rearrange("p (t n) -> p t n", t=2)
                    if n == 3:
                        act.wait(pe.mark(), *got("recurred", c - 2))
                        act_copy(act, v[par][:, two, :], bank2)
                        b.read = (act.mark(),)
                    else:
                        act.wait(pe.mark(), *got("gated", c - 1))
                        activation(act, g_tanh[:, two, :], bank2, ACT.Tanh, scale=0.5)
                        dve.wait(act.mark(), *got("out", c - 2))
                        fused(dve, gate[par][:, two, :], g_tanh[:, two, :], 1.0, bank2, ALU.add, ALU.mult)
                        b.read = (dve.mark(),)
                if n == 3:
                    done["v", c] = (act.mark(),)
                    yield
            done["mus", c] = (pe.mark(),)
            done["gated", c] = (dve.mark(),)
            done["mixed", c] = (pool.mark(), dve.mark())

        def recur(c):
            par, first = c % 2, c * CT
            qs, ks = [q[par]] + q_up[1:], [k[par]] + k_up[1:]
            dec = decay[par]
            offset = [0]
            for l in range(TREE):
                offset.append(offset[-1] + (CHUNK >> l))
            totals = [dec[:, offset[l]:offset[l] + (CHUNK >> l)] for l in range(TREE + 1)]
            previous = got("recurred", c - 1)
            dve.wait(*got("k", c), *got("q", c), *got("decay", c), *previous)
            act.wait(*got("k", c), *got("q", c), *previous)
            pool.wait(*got("k", c), *got("decay", c), *previous)
            scalar1(pool, k_bonus[:, :], ks[0][:, :], bonus[:, 0:1], ALU.mult)
            ready = [pool.mark()]
            for l in range(TREE):
                blocks = lambda ap: ap.rearrange("p (n two m) -> p n two m", two=2, m=1 << l)
                tot = totals[l].rearrange("p (n two) -> p n two", two=2)
                tensor2(dve, blocks(qs[l + 1][:, :])[:, :, 1, :], blocks(qs[l][:, :])[:, :, 1, :],
                        spread(tot[:, :, 0], 1 << l), ALU.mult)
                tensor2(dve, totals[l + 1], tot[:, :, 0], tot[:, :, 1], ALU.mult)
                stepped = dve.mark()
                tensor2(pool, blocks(ks[l + 1][:, :])[:, :, 0, :], blocks(ks[l][:, :])[:, :, 0, :],
                        spread(tot[:, :, 1], 1 << l), ALU.mult)
                key = pool.mark()
                act_copy(act, blocks(qs[l + 1][:, :])[:, :, 0, :], blocks(qs[l][:, :])[:, :, 0, :])
                act_copy(act, blocks(ks[l + 1][:, :])[:, :, 1, :], blocks(ks[l][:, :])[:, :, 1, :])
                kept = act.mark()
                for e in (dve, pool, act):
                    e.wait(stepped, key, kept)
                ready.append(stepped)
                yield
            levelled = [stepped, key, kept, ready[0]]
            pe.wait(*levelled, *got("v", c))
            for i in range(CT):
                tok = i * P
                first_of_sequence = (c * CT + i) % QB == 0
                now, then = (c * CT + i) % 2, (c * CT + i + 1) % 2
                pe.wait(*products.read)
                for part in range(DIAG):
                    kk, qq = (k_bonus, qs[0]) if part == 0 else (ks[part - 1], qs[part - 1])
                    for j in range(P // SUB):
                        t0 = tok + j * SUB
                        for h in range(HEADS_A):
                            r = h * HK
                            matmul(pe, products.buf[j * SUB:(j + 1) * SUB, h, part * SUB:(part + 1) * SUB],
                                   kk[r:r + HK, t0:t0 + SUB], qq[r:r + HK, t0:t0 + SUB], tile=(r, j * SUB))
                off = DIAG * SUB
                for j in (0, 2):
                    t0 = tok + j * SUB
                    for h in range(HEADS_A):
                        r = h * HK
                        matmul(pe, products.buf[j * SUB:(j + 1) * SUB, h, off:off + SUB],
                               ks[5][r:r + HK, t0:t0 + SUB], qs[5][r:r + HK, t0 + SUB:t0 + C2], tile=(r, j * SUB))
                for h in range(HEADS_A):
                    r = h * HK
                    matmul(pe, products.buf[0:C2, h, off + SUB:off + SUB + C2],
                           ks[6][r:r + HK, tok:tok + C2], qs[6][r:r + HK, tok + C2:tok + P], tile=(r, 0))
                multiplied = pe.mark()
                b = back.take()
                pe.wait(*b.read)
                transpose(pe, b.buf[:, 0:P], ks[TREE][:, tok:tok + P], ident[:, :])
                kt_slot = k_tok.take()
                act.wait(pe.mark(), *kt_slot.read)
                act_copy(act, kt_slot.buf[:, :], b.buf[:, 0:P])
                k_turned = act.mark()
                b.read = (k_turned,)
                s = pair.take()
                dve.wait(multiplied, *got("summed", 0))
                tensor2(dve, masked[:, :, :], products.buf[:, :, 0:off],
                        mask[:, :].unsqueeze(1).to_broadcast([P, HEADS_A, off]), ALU.mult)
                dve.wait(dve.mark(), *got("placed", 0))
                reduce(dve, diag[:, :, :], masked[:, :, :].rearrange("p h (l t) -> p h t l", l=DIAG), ALU.add)
                summed = dve.mark()
                done["summed", 0] = (summed,)
                act.wait(multiplied, summed, *s.read)
                act_copy(act, s.buf[0:SUB, :, SUB:C2], products.buf[0:SUB, :, off:off + SUB])
                act_copy(act, s.buf[C2:C2 + SUB, :, C2 + SUB:P], products.buf[C2:C2 + SUB, :, off:off + SUB])
                act_copy(act, s.buf[0:C2, :, C2:P], products.buf[0:C2, :, off + SUB:off + SUB + C2])
                products.read = (summed, act.mark())
                for j in range(P // SUB):
                    act_copy(act, s.buf[j * SUB:(j + 1) * SUB, :, j * SUB:(j + 1) * SUB],
                             diag[j * SUB:(j + 1) * SUB, :, :])
                placed = act.mark()
                done["placed", 0] = (placed,)
                yield
                b = back.take()
                pe.wait(*b.read, *got("state", 0))
                if not first_of_sequence:
                    matmul(pe, b.buf[:, 0:VD], qs[TREE][:, tok:tok + P], state[now][:, :], True, False)
                pe.wait(placed)
                for h in range(HEADS_A):
                    matmul(pe, b.buf[:, h * HV:(h + 1) * HV], s.buf[:, h, :], v[par][:, i, h * HV:(h + 1) * HV],
                           first_of_sequence, first_of_sequence or h == HEADS_A - 1)
                s.read = (pe.mark(),)
                act.wait(pe.mark(), *got("o_read", c - 1))
                act_copy(act, o[:, i, :], b.buf[:, 0:VD])
                o_read_out = act.mark()
                b.read = (o_read_out,)
                b = back.take()
                pe.wait(k_turned, *b.read)
                for h in range(HEADS_A):
                    r = h * HK
                    matmul(pe, b.buf[r:r + HK, 0:HV], kt_slot.buf[:, r:r + HK], v[par][:, i, h * HV:(h + 1) * HV],
                           tile=(0, r))
                kt_slot.read = (pe.mark(),)
                dve.wait(pe.mark())
                for h in range(HEADS_A):
                    r, cols = h * HK, slice(h * HV, (h + 1) * HV)
                    if first_of_sequence:
                        copy(dve, state[then][r:r + HK, cols], b.buf[r:r + HK, 0:HV])
                    else:
                        fused(dve, state[then][r:r + HK, cols], state[now][r:r + HK, cols],
                              totals[TREE][r:r + HK, i:i + 1], b.buf[r:r + HK, 0:HV], ALU.mult, ALU.add)
                b.read = (dve.mark(),)
                done["state", 0] = (dve.mark(),)
                dve.wait(dve.mark())
                yield
            done["recurred", c] = (pe.mark(), dve.mark(), act.mark())
            groups = lambda ap: ap.rearrange("p t (h n) -> p (t h) n", n=HV)
            dve.wait(o_read_out)
            reduce(dve, sums[:, :], groups(o[:, :, :]), ALU.add)
            dve.wait(dve.mark())
            scalar1(dve, sums[:, :], sums[:, :], 1.0 / HV, ALU.mult)
            dve.wait(dve.mark())
            tensor2(dve, groups(o[:, :, :]), groups(o[:, :, :]), spread(sums[:, :], HV), ALU.subtract)
            act.wait(dve.mark(), *got("squares", c - 1))
            activation(act, o_sq[:, :, :], o[:, :, :], ACT.Square)
            yield
            dve.wait(act.mark(), *got("rstd_read", c - 1))
            reduce(dve, rstd[:, :], groups(o_sq[:, :, :]), ALU.add)
            done["squares", c] = (dve.mark(),)
            pool.wait(dve.mark())
            scalar2(pool, rstd[:, :], rstd[:, :], 1.0 / HV, EPS, ALU.mult, ALU.add)
            pool.wait(pool.mark())
            tensor2(pool, rstd[:, :], rstd[:, :], half[:, :], ALU.pow)
            dve.wait(pool.mark())
            tensor2(dve, groups(o[:, :, :]), groups(o[:, :, :]), spread(rstd[:, :], HV), ALU.mult)
            done["rstd_read", c] = (dve.mark(),)
            yield
            wide = lambda ap: ap.unsqueeze(1).to_broadcast([P, CT, VD])
            pool.wait(dve.mark(), *got("gated", c))
            tensor2(pool, o[:, :, :], o[:, :, :], wide(gn_w[:, :]), ALU.mult)
            pool.wait(pool.mark())
            tensor2(pool, o[:, :, :], o[:, :, :], wide(gn_b[:, :]), ALU.add)
            dve.wait(pool.mark())
            fused(dve, o[:, :, :], o[:, :, :], 0.5, gate[par][:, :, :], ALU.mult, ALU.mult)
            out_ready = dve.mark()
            yield
            pe.wait(out_ready)
            for kt in range(KT):
                b = back.take()
                pe.wait(*b.read)
                for i in range(CT):
                    transpose(pe, b.buf[:, i * P:(i + 1) * P], o[:, i, kt * P:(kt + 1) * P], ident[:, :])
                act.wait(pe.mark(), *got("projected", c - 1))
                act_copy(act, o_t[:, kt, :], b.buf)
                b.read = (act.mark(),)
            done["o_read", c] = (pe.mark(),)
            turned = act.mark()
            for i in range(CT):
                b = back.take()
                pe.wait(turned, *b.read)
                for kt in range(KT):
                    matmul(pe, b.buf[:, 0:DIM], o_t[:, kt, i * P:(i + 1) * P], w_o[:, kt, :], kt == 0, kt == KT - 1)
                dve.wait(pe.mark())
                tensor2(dve, x[:, first + i, :], x[:, first + i, :], b.buf[:, 0:DIM], ALU.add)
                b.read = (dve.mark(),)
                if i % 2:
                    yield
            done["projected", c] = (pe.mark(),)
            done["out", c] = (dve.mark(),)

        together(prepare(0))
        for c in range(CHUNKS):
            together(prepare(c + 1) if c + 1 < CHUNKS else None, recur(c))
        core.run()


def feed_forward(core, x, d, tag, out_dram=None):
    nc, pe, act, dve, pool, sp, banks = core.nc, core.pe, core.act, core.dve, core.pool, core.sp, core.banks
    with ExitStack() as ctx:
        sb = lambda n, s, dt=F32: ctx.enter_context(nc.sbuf_tensor(f"{tag}_{n}", s, dt))
        lane = lambda n: Lane(ctx.enter_context(nc.semaphore(f"{tag}_{n}")))
        COPIES = 3
        ROWS = COPIES * SUB
        ident = sb("ident", [P, P])
        fc = sb("fc", [P, HT, DIM])
        proj = sb("proj", [P, KT, HIDDEN])
        u, v, fast_b = sb("u", [P, HT, RANK]), sb("v", [RANK, DIM]), sb("fast_b", [RANK, RANK])
        gate = sb("gate", [P, 1])
        fc_t, proj_t = sb("fc_t", [P, KT, HIDDEN], F32R), sb("proj_t", [P, HT, DIM], F32R)
        scale_fc, gate_fc = sb("scale_fc", [P, HT]), sb("gate_fc", [P, HT])
        scale_proj, scale_row = sb("scale_proj", [P, KT]), sb("scale_row", [P, DIM])
        upper, lower = sb("upper", [P, HT]), sb("lower", [P, HT])
        below = Ring([sb(f"below{i}", [P, P]) for i in range(2)])
        tern = Ring([sb(f"tern{i}", [P, P]) for i in range(2)])
        ones, diagonal = sb("ones", [P, P]), sb("diagonal", [P, P])
        u3 = sb("u3", [P, HT, ROWS])
        u3_t = sb("u3_t", [ROWS, HIDDEN], F32R)
        low_in = sb("low_in", [P, KT, ROWS])
        low_hi, low_lo = sb("low_hi", [P, KT, ROWS], F32R), sb("low_lo", [P, KT, ROWS], F32R)

        xn = Ring([sb(f"xn{i}", [P, DIM]) for i in range(4)])
        x_hi = Ring([sb(f"x_hi{i}", [P, KT, CHUNK], F32R) for i in range(1)])
        x_lo = sb("x_lo", [P, KT, CHUNK], F32R)
        low = sb("low", [ROWS, CHUNK], F32R)
        relu = Ring([sb(f"relu{i}", [P, CHUNK]) for i in range(2)])
        square = Ring([sb(f"square{i}", [P, CHUNK]) for i in range(2)])
        r_hi = [sb(f"r_hi{i}", [P, HT, CHUNK], F32R) for i in range(2)]
        r_lo = [sb(f"r_lo{i}", [P, HT, CHUNK], F32R) for i in range(2)]
        scaled_out = Ring([sb(f"scaled_out{i}", [P, DIM]) for i in range(2)])

        bank = lambda i: banks[:, i, :]
        front, back = Ring([bank(i) for i in range(5)]), Ring([bank(i) for i in range(5, 8)])
        norm = Normalizer(core, sb, "norm", CT)

        weights = lane("weights")
        weights.start(sp, ident[:, :], d["c_ident"])
        weights.start(sp, fc[:, :, :], d["w_fc"].rearrange("(m p) n -> p m n", p=P))
        weights.start(sp, proj[:, :, :], d["w_proj"].rearrange("(m p) n -> p m n", p=P))
        weights.start(sp, u[:, :, :], d["u"].rearrange("(m p) n -> p m n", p=P))
        weights.start(sp, v[:, :], d["v"])
        weights.start(sp, fast_b[:, :], d["fast_b"])
        loaded = weights.start(sp, gate[:, :], d["gate"].to_broadcast([P, 1]))
        memset(pool, ones[:, :], 1.0)
        memset(pool, u3[:, :, :], 0.0)
        memset(pool, low_in[:, :, :], 0.0)
        zeroed = pool.mark()
        for e in (pe, act, dve, pool):
            e.wait(loaded, zeroed)

        def ternary(w, rows, cols, scale, out_t):
            reduce(dve, scale[:, 0:rows], w[:, :, :], ALU.add, absolute=True)
            dve.wait(dve.mark())
            scalar2(dve, scale[:, 0:rows], scale[:, 0:rows], 1.0 / (cols * P), 1e-5, ALU.mult, ALU.max)
            dve.wait(dve.mark())
            scalar1(dve, upper[:, 0:rows], scale[:, 0:rows], 0.5, ALU.mult)
            scalar1(dve, lower[:, 0:rows], scale[:, 0:rows], -0.5, ALU.mult)
            dve.wait(dve.mark())
            for m in range(rows):
                for n in range(cols):
                    part = w[:, m, n * P:(n + 1) * P]
                    lt, s, b = below.take(), tern.take(), front.take()
                    scalar1(dve, lt.buf[:, :], part, lower[:, m:m + 1], ALU.is_lt)
                    dve.wait(dve.mark(), *s.read)
                    fused(dve, s.buf[:, :], part, upper[:, m:m + 1], lt.buf[:, :], ALU.is_gt, ALU.subtract)
                    pe.wait(dve.mark(), *b.read)
                    transpose(pe, b.buf[:, 0:P], s.buf[:, :], ident[:, :])
                    s.read = (pe.mark(),)
                    act.wait(pe.mark())
                    act_copy(act, out_t[:, n, m * P:(m + 1) * P], b.buf[:, 0:P])
                    b.read = (act.mark(),)

        ternary(fc, HT, KT, scale_fc, fc_t)
        dve.do(lambda e: e.reciprocal(gate_fc[:, :], scale_fc[:, :]))
        dve.wait(dve.mark())
        scalar1(dve, gate_fc[:, :], gate_fc[:, :], gate[:, 0:1], ALU.mult)
        dve.wait(dve.mark())
        tensor2(dve, u[:, :, :], u[:, :, :], spread(gate_fc[:, :], RANK), ALU.mult)
        dve.wait(dve.mark())
        for i in range(COPIES):
            copy(dve, u3[:, :, i * SUB:i * SUB + RANK], u[:, :, :])
        u3_done = dve.mark()
        for m in range(HT):
            b, cols = front.take(), slice(m * P, (m + 1) * P)
            pe.wait(u3_done, *b.read)
            transpose(pe, b.buf[0:ROWS, 0:P], u3[:, m, :], ident[:, :])
            dve.wait(pe.mark())
            copy(dve, u3_t[:, cols], b.buf[0:ROWS, 0:P])
            dve.wait(dve.mark())
            last = slice(ROWS - SUB, ROWS)
            tensor2(dve, u3_t[last, cols], b.buf[last, 0:P], u3_t[last, cols].bitcast(F32), ALU.subtract)
            b.read = (dve.mark(),)
        for kt in range(KT):
            b = front.take()
            pe.wait(*b.read)
            matmul(pe, b.buf[:, 0:RANK], v[:, kt * P:(kt + 1) * P], fast_b[:, :])
            dve.wait(pe.mark())
            for i in range(COPIES):
                copy(dve, low_in[:, kt, i * SUB:i * SUB + RANK], b.buf[:, 0:RANK])
            b.read = (dve.mark(),)
        dve.wait(dve.mark())
        copy(dve, low_hi[:, :, :], low_in[:, :, :])
        dve.wait(dve.mark())
        tensor2(dve, low_lo[:, :, :], low_in[:, :, :], low_hi[:, :, :].bitcast(F32), ALU.subtract)
        ternary(proj, KT, HT, scale_proj, proj_t)
        for kt in range(KT):
            b = front.take()
            dve.wait(*( () if kt == 0 else (pe.mark(),)))
            scalar1(dve, diagonal[:, :], ident[:, :], scale_proj[:, kt:kt + 1], ALU.mult)
            pe.wait(dve.mark(), *b.read)
            matmul(pe, b.buf[:, 0:P], ones[:, :], diagonal[:, :])
            act.wait(pe.mark())
            act_copy(act, scale_row[:, kt * P:(kt + 1) * P], b.buf[:, 0:P])
            b.read = (act.mark(),)
        pe.wait(act.mark(), dve.mark())
        dve.wait(act.mark())

        done = {}
        got = lambda what, c: done.get((what, c), ())
        stored = [lane(f"out{i}") for i in range(2)] if out_dram is not None else []
        out_view = out_dram.rearrange("b (t p) c -> p (b t) c", p=P) if out_dram is not None else None

        def up(c):
            par, first = c % 2, c * CT
            rstd_done = norm.statistics(x, first, ())
            dve.wait(rstd_done)
            slots = []
            for i in range(CT):
                s = xn.take()
                dve.wait(*s.read)
                norm.scale(s.buf[:, :], x, first, i)
                slots.append((s, dve.mark()))
            norm.applied = (dve.mark(),)
            yield
            xh = x_hi.take()
            for kt in range(KT):
                b = front.take()
                pe.wait(*b.read)
                for i, (s, scaled) in enumerate(slots):
                    pe.wait(scaled)
                    transpose(pe, b.buf[:, i * P:(i + 1) * P], s.buf[:, kt * P:(kt + 1) * P], ident[:, :])
                    s.read = (pe.mark(),)
                act.wait(pe.mark(), *xh.read)
                act_copy(act, xh.buf[:, kt, :], b.buf)
                dve.wait(act.mark(), *xh.read)
                tensor2(dve, x_lo[:, kt, :], b.buf, xh.buf[:, kt, :].bitcast(F32), ALU.subtract)
                b.read = (dve.mark(),)
            x_done = dve.mark()
            yield
            b = front.take()
            pe.wait(x_done, *b.read)
            passes = [(kt, w, s) for kt in range(KT) for w, s in ((low_hi, xh.buf), (low_hi, x_lo), (low_lo, xh.buf))]
            for n, (kt, w, s) in enumerate(passes):
                matmul(pe, b.buf[0:ROWS, :], w[:, kt, :], s[:, kt, :], n == 0, n == len(passes) - 1)
            act.wait(pe.mark(), *xh.read)
            act_copy(act, low[:, :], b.buf[0:ROWS, :])
            dve.wait(act.mark())
            tensor2(dve, low[SUB:2 * SUB, :], b.buf[SUB:2 * SUB, :], low[SUB:2 * SUB, :].bitcast(F32), ALU.subtract)
            b.read = (dve.mark(),)
            low_done = dve.mark()
            for m in range(HT):
                b, cols = front.take(), slice(m * P, (m + 1) * P)
                pe.wait(*b.read)
                for kt in range(KT):
                    matmul(pe, b.buf, fc_t[:, kt, cols], xh.buf[:, kt, :], kt == 0, False)
                    matmul(pe, b.buf, fc_t[:, kt, cols], x_lo[:, kt, :], False, False)
                pe.wait(low_done)
                matmul(pe, b.buf, u3_t[:, cols], low[:, :], False, True)
                r, sq = relu.take(), square.take()
                act.wait(pe.mark(), *r.read)
                activation(act, r.buf[:, :], b.buf, ACT.Relu, scale=scale_fc[:, m:m + 1])
                b.read = (act.mark(),)
                act.wait(act.mark(), *sq.read)
                activation(act, sq.buf[:, :], r.buf[:, :], ACT.Square)
                dve.wait(act.mark(), *got("down", c - 2))
                copy(dve, r_hi[par][:, m, :], sq.buf[:, :])
                dve.wait(dve.mark())
                tensor2(dve, r_lo[par][:, m, :], sq.buf[:, :], r_hi[par][:, m, :].bitcast(F32), ALU.subtract)
                sq.read = (dve.mark(),)
                yield
            xh.read = (pe.mark(),)
            done["up", c] = (dve.mark(),)

        def down(c):
            par, first = c % 2, c * CT
            pe.wait(*got("up", c))
            for i in range(CT):
                b = back.take()
                pe.wait(*b.read)
                for m in range(HT):
                    for r in (r_hi, r_lo):
                        matmul(pe, b.buf[:, 0:DIM], r[par][:, m, i * P:(i + 1) * P], proj_t[:, m, :],
                               m == 0 and r is r_hi, m == HT - 1 and r is r_lo)
                    if m == HT // 2:
                        yield
                s = scaled_out.take()
                dve.wait(pe.mark(), *s.read)
                tensor2(dve, s.buf[:, :], b.buf[:, 0:DIM], scale_row[:, :], ALU.mult)
                b.read = (dve.mark(),)
                pool.wait(dve.mark())
                tensor2(pool, x[:, first + i, :], x[:, first + i, :], s.buf[:, :], ALU.add)
                s.read = (pool.mark(),)
                yield
            done["down", c] = (pe.mark(),)
            if out_dram is not None:
                sp.wait(pool.mark())
                stored[c % 2].start(sp, out_view[:, first:first + CT, :], x[:, first:first + CT, :])

        together(up(0))
        for c in range(CHUNKS):
            together(up(c + 1) if c + 1 < CHUNKS else None, down(c))
        for s in stored:
            sp.wait((s.sem, s.count))
        core.run()


def attention(core, x, d):
    nc, pe, act, dve, pool, sp, banks = core.nc, core.pe, core.act, core.dve, core.pool, core.sp, core.banks
    with ExitStack() as ctx:
        sb = lambda n, s, dt=F32: ctx.enter_context(nc.sbuf_tensor("b_" + n, s, dt))
        lane = lambda n: Lane(ctx.enter_context(nc.semaphore("b_" + n)))
        GW = GROUP * HD
        VW = HD + 1
        SLOT = P // GROUP

        ident, ident_r = sb("ident", [P, P]), sb("ident_r", [P, P], F32R)
        tables = sb("tables", [P, HEADS + len(SLOPE_LO), P], F32R)
        w_qk = sb("w_qk", [P, KT, GROUPS, 2 * GW])
        w_v, w_out = sb("w_v", [P, KT, DIM]), sb("w_out", [P, KT, DIM])
        b_qk, scale_qk = sb("b_qk", [P, GROUPS]), sb("scale_qk", [P, 1])
        b_v, b_out = sb("b_v", [P, DIM]), sb("b_out", [P, DIM])
        q_stack = sb("q_stack", [STACK, 2 * GROUP, SEQ], F32R)
        k_stack = sb("k_stack", [STACK, 2 * GROUP, SEQ], F32R)
        xn = Ring([sb(f"xn{i}", [P, DIM]) for i in range(2)])
        xn_t = sb("xn_t", [P, KT, SEQ])
        qk = Ring([sb("qk", [P, BANK])])
        qk_hi, qk_lo = sb("qk_hi", [P, SEQ], F32R), sb("qk_lo", [P, SEQ], F32R)
        v = sb("v", [P, QB, HEADS, VW])
        half_max = sb("half_max", [P, GROUP * QB, HALVES])
        row_max = sb("row_max", [P, 2, GROUP * QB])
        shift = sb("shift", [2 * GROUP * QB, P], F32R)
        p_t = Ring([sb(f"p_t{i}", [P, 2, BANK]) for i in range(3)])
        pv = sb("pv", [P, BANK])
        recip = sb("recip", [P, CT * GROUP])
        att = sb("att", [P, QB, DIM])
        att_t = sb("att_t", [P, KT, P])
        shift_dram = [nc.dram_tensor(f"b_shift_dram{i}", (2, GROUP, SEQ), F32R, kind="Internal").ap() for i in range(2)]

        scores = Ring([banks[:, 0:2, :], banks[:, 2:4, :]])
        values = Slot(banks[:, 4, :])
        misc = Ring([banks[:, i, :] for i in (5, 6, 7)])
        norm = Normalizer(core, sb, "norm", QB)

        weights, tables_lane = lane("weights"), lane("tables")
        memset(pool, words(q_stack[:, :, :]), 0.0)
        memset(dve, words(k_stack[:, :, :]), 0.0)
        dve.wait(dve.mark())
        memset(dve, words(k_stack[SHIFTROW:STACK, :, :]), 1.0)
        pool.wait(pool.mark(), dve.mark())
        for s in range(2 * GROUP):
            tables_lane.start(pool, q_stack[MAIN:MAIN + BIASROWS, s, :], d["c_qbias"])
        tables_lane.start(pool, tables[:, :, :], d["c_diag"])
        k_bias = nc.dram_tensor("b_k_bias", (HEADS, BIASROWS, SEQ), F32R, kind="Internal").ap()
        cast = tables_lane.start(pool, k_bias, d["c_kbias"])
        weights.start(sp, ident[:, :], d["c_ident"])
        for kt in range(KT):
            rows = d["Wqkv"][kt * P:(kt + 1) * P, :]
            for part in range(2):
                weights.start(sp, w_qk[:, kt, :, part * GW:(part + 1) * GW],
                              rows[:, part * DIM:(part + 1) * DIM].rearrange("p (g n) -> p g n", g=GROUPS))
            weights.start(sp, w_v[:, kt, :], rows[:, 2 * DIM:3 * DIM])
        weights.start(sp, w_out[:, :, :], d["Wout"].rearrange("(k p) n -> p k n", p=P))
        for g in range(GROUPS):
            for part in range(2):
                lo = part * DIM + g * GW
                weights.start(sp, b_qk[part * GW:(part + 1) * GW, g:g + 1],
                              d["bqkv"][lo:lo + GW].rearrange("(p a) -> p a", a=1))
        weights.start(sp, b_v[:, :], d["bqkv"][2 * DIM:3 * DIM].partition_broadcast(P))
        loaded = weights.start(sp, b_out[:, :], d["bout"].partition_broadcast(P))
        memset(dve, scale_qk[0:GW, :], HD ** -0.5)
        memset(dve, scale_qk[GW:P, :], 1.0)
        memset(dve, v[:, :, :, HD:VW], 1.0)
        filled = pool.mark()
        memset(dve, values.buf, 0.0)
        for e in (pe, act, dve, pool, sp):
            e.wait(loaded, cast, filled, dve.mark())
        copy(dve, ident_r[:, :], ident[:, :])
        pe.wait(dve.mark())

        done = {}
        got = lambda what, g: done.get((what, g), ())
        stack_lane = [lane(f"stack{i}") for i in range(2)]
        shift_out, shift_in = lane("shift_out"), lane("shift_in")

        def table(h):
            at = h + sum(other < h for other in SLOPE_LO)
            return [tables[:, at + i, :] for i in range(1 + (h in SLOPE_LO))]

        def add_block_bias(out, h):
            parts = table(h)
            for n, t in enumerate(parts):
                matmul(pe, out, ident_r[:, :], t, False, n == len(parts) - 1)

        def front(g):
            b, hg, slot0 = g // GROUPS, g % GROUPS, g % 2 * GROUP
            if hg == 0:
                rstd_done = norm.statistics(x, b * QB, ())
                dve.wait(rstd_done)
                for i in range(0, QB, 2):
                    m = misc.take()
                    pe.wait(*m.read)
                    for j in range(2):
                        s = xn.take()
                        dve.wait(*s.read)
                        norm.scale(s.buf[:, :], x, b * QB, i + j)
                        pe.wait(dve.mark())
                        for kt in range(KT):
                            at = (kt * 2 + j) * P
                            transpose(pe, m.buf[:, at:at + P], s.buf[:, kt * P:(kt + 1) * P], ident[:, :])
                        s.read = (pe.mark(),)
                    act.wait(pe.mark(), *got("xn_read", b - 1))
                    act_copy(act, xn_t[:, :, i * P:(i + 2) * P], m.buf.rearrange("p (k n) -> p k n", k=KT))
                    m.read = (act.mark(),)
                    yield
                norm.applied = (dve.mark(),)
                done["xn", b] = (act.mark(),)
                pe.wait(act.mark())
            for half in range(HALVES):
                m, s, cols = misc.take(), qk.take(), slice(half * BANK, (half + 1) * BANK)
                pe.wait(*m.read)
                for kt in range(KT):
                    matmul(pe, m.buf, w_qk[:, kt, hg, :], xn_t[:, kt, cols], kt == 0, kt == KT - 1)
                dve.wait(pe.mark(), *s.read)
                scalar2(dve, s.buf[:, :], m.buf, b_qk[:, hg:hg + 1], scale_qk[:, 0:1], ALU.add, ALU.mult)
                m.read = (dve.mark(),)
                act.wait(dve.mark(), *got("stacked", g - 1))
                act_copy(act, qk_hi[:, cols], s.buf[:, :])
                pool.wait(act.mark(), *got("stacked", g - 1))
                tensor2(pool, qk_lo[:, cols], s.buf[:, :], qk_hi[:, cols].bitcast(F32), ALU.subtract)
                s.read = (pool.mark(),)
                yield
            done["qk", g] = (pe.mark(),)
            if hg == GROUPS - 1:
                done["projected", b] = (pe.mark(),)
            sp.wait(act.mark(), pool.mark(), *got("scored", g - 2))
            for i in range(GROUP):
                s, rows_q = slot0 + i, slice(i * HD, (i + 1) * HD)
                rows_k = slice(GW + i * HD, GW + (i + 1) * HD)
                for at, (qpart, kpart) in enumerate(((qk_hi, qk_hi), (qk_hi, qk_lo), (qk_lo, qk_hi))):
                    to = slice(at * HD, (at + 1) * HD)
                    stack_lane[g % 2].start(sp, words(q_stack[to, s, :]), words(qpart[rows_q, :]))
                    stack_lane[g % 2].start(sp, words(k_stack[to, s, :]), words(kpart[rows_k, :]))
                stacked = stack_lane[g % 2].start(sp, words(k_stack[MAIN:MAIN + BIASROWS, s, :]), words(k_bias[hg * GROUP + i]))
            done["stacked", g] = (stacked,)
            pe.wait(stacked)
            yield
            for i in range(GROUP):
                for qb in range(QB):
                    s = slot0 + i
                    for half in range(HALVES):
                        m = misc.take()
                        pe.wait(*m.read)
                        here = qb // CT == half
                        matmul(pe, m.buf, q_stack[0:SHIFTROW, s, qb * P:(qb + 1) * P],
                               k_stack[0:SHIFTROW, s, half * BANK:(half + 1) * BANK], True, not here)
                        if here:
                            at = qb % CT * P
                            add_block_bias(m.buf[:, at:at + P], hg * GROUP + i)
                        dve.wait(pe.mark(), *got("max", g - 1))
                        reduce(dve, half_max[:, i * QB + qb, half:half + 1], m.buf, ALU.max, negate=True)
                        m.read = (dve.mark(),)
                    if qb % 2:
                        yield
            dve.wait(dve.mark(), *got("turned", g - 1))
            reduce(dve, row_max[:, 0, :], half_max[:, :, :], ALU.min)
            done["max", g] = (dve.mark(),)
            dve.wait(dve.mark())
            copy(dve, row_max[:, 1, :], row_max[:, 0, :])
            m = misc.take()
            pe.wait(dve.mark(), *m.read)
            rows = 2 * GROUP * QB
            transpose(pe, m.buf[0:rows, 0:P], row_max[:, :, :].rearrange("p a n -> p (a n)"), ident[:, :])
            done["turned", g] = (pe.mark(),)
            act.wait(pe.mark(), *got("shift_out", g - 1))
            act_copy(act, shift[:, :], m.buf[0:rows, 0:P])
            dve.wait(act.mark())
            lo = slice(rows // 2, rows)
            tensor2(dve, shift[lo, :], m.buf[lo, 0:P], shift[lo, :].bitcast(F32), ALU.subtract)
            m.read = (dve.mark(),)
            sp.wait(dve.mark(), *got("shift_in", g - 2))
            out = shift_out.start(sp, words(shift_dram[g % 2].rearrange("a h (b n) -> (a h b) n", n=P)), words(shift[:, :]))
            done["shift_out", g] = (out,)
            sp.wait(out)
            done["shift_in", g] = (shift_in.start(sp, words(q_stack[SHIFTROW:STACK, slot0:slot0 + GROUP, :]), words(shift_dram[g % 2])),)

        def back(g):
            b, hg, slot0 = g // GROUPS, g % GROUPS, g % 2 * GROUP
            if hg == 0:
                for i in range(QB):
                    m = misc.take()
                    pe.wait(*m.read)
                    for kt in range(KT):
                        matmul(pe, m.buf[:, 0:DIM], xn_t[:, kt, i * P:(i + 1) * P], w_v[:, kt, :],
                               kt == 0, kt == KT - 1)
                    dve.wait(pe.mark())
                    by_head = lambda ap: ap.rearrange("p (h n) -> p h n", n=HD)
                    tensor2(dve, v[:, i, :, 0:HD], by_head(m.buf[:, 0:DIM]), by_head(b_v[:, :]), ALU.add)
                    m.read = (dve.mark(),)
                    yield
                pe.wait(dve.mark())
                done["v_made", b] = (pe.mark(),)
            pe.wait(*got("shift_in", g))
            for half in range(HALVES):
                qcols, pending = slice(half * BANK, (half + 1) * BANK), []

                def weigh(kb, halves_of_group):
                    if kb == 0:
                        pe.wait(*values.read)
                    for slot, exped in halves_of_group:
                        pe.wait(exped)
                    for i in range(GROUP):
                        slot = halves_of_group[i // 2][0]
                        matmul(pe, values.buf[i * SLOT:i * SLOT + VW, :], v[:, kb, hg * GROUP + i, :],
                               slot.buf[:, i % 2, :], kb == 0, kb == QB - 1, tile=(0, i * SLOT))
                    for slot, _ in halves_of_group:
                        slot.read = (pe.mark(),)

                for kb in range(QB):
                    made = []
                    for pair in range(2):
                        sc = scores.take()
                        pe.wait(*sc.read)
                        for j in range(2):
                            i = pair * 2 + j
                            here = kb // CT == half
                            matmul(pe, sc.buf[:, j, :], k_stack[0:STACK, slot0 + i, kb * P:(kb + 1) * P],
                                   q_stack[0:STACK, slot0 + i, qcols], True, not here)
                            if here:
                                at = kb % CT * P
                                add_block_bias(sc.buf[:, j, at:at + P], hg * GROUP + i)
                        if pair == 0 and pending:
                            scored = pe.mark()
                            weigh(*pending.pop())
                        else:
                            scored = pe.mark()
                        s = p_t.take()
                        act.wait(scored, *s.read)
                        activation(act, s.buf[:, :, :], sc.buf, ACT.Exp)
                        sc.read = (act.mark(),)
                        made.append((s, act.mark()))
                    pending.append((kb, made))
                    yield
                weigh(*pending.pop())
                if half == HALVES - 1:
                    done["scored", g] = (pe.mark(),)
                act.wait(pe.mark(), *got("pv_read", 0))
                act_copy(act, pv[:, :], values.buf)
                values.read = (act.mark(),)
                m = misc.take()
                pe.wait(act.mark(), *m.read)
                for i in range(CT):
                    transpose(pe, m.buf[:, i * P:(i + 1) * P], pv[:, i * P:(i + 1) * P], ident[:, :])
                done["pv_read", 0] = (pe.mark(),)
                slots = m.buf.rearrange("p (t h n) -> p t h n", t=CT, h=GROUP)
                dve.wait(pe.mark(), *got("att_read", b - 1), *got("normalized", 0))
                dve.do(lambda e, slots=slots: e.reciprocal(recip[:, :].rearrange("p (t h) -> p t h", t=CT), slots[:, :, :, HD]))
                dve.wait(dve.mark())
                tensor2(dve, att[:, half * CT:(half + 1) * CT, hg * GW:(hg + 1) * GW].rearrange("p t (h n) -> p t h n", n=HD),
                        slots[:, :, :, 0:HD], spread(recip[:, :].rearrange("p (t h) -> p t h", t=CT), HD), ALU.mult)
                m.read = done["normalized", 0] = (dve.mark(),)
                yield
            if hg == GROUPS - 1:
                pe.wait(dve.mark())
                for i in range(QB):
                    m = misc.take()
                    pe.wait(*m.read)
                    for kt in range(KT):
                        transpose(pe, m.buf[:, kt * P:(kt + 1) * P], att[:, i, kt * P:(kt + 1) * P], ident[:, :])
                    act.wait(pe.mark(), *got("att_t_read", 0))
                    act_copy(act, att_t[:, :, :], m.buf[:, 0:DIM].rearrange("p (k n) -> p k n", k=KT))
                    m.read = (act.mark(),)
                    done["att_read", b] = (pe.mark(),)
                    m = misc.take()
                    pe.wait(act.mark(), *m.read)
                    for kt in range(KT):
                        matmul(pe, m.buf[:, 0:DIM], att_t[:, kt, :], w_out[:, kt, :], kt == 0, kt == KT - 1)
                    done["att_t_read", 0] = (pe.mark(),)
                    tile = x[:, b * QB + i, :]
                    dve.wait(pe.mark())
                    tensor2(dve, tile, tile, m.buf[:, 0:DIM], ALU.add)
                    m.read = (dve.mark(),)
                    pool.wait(dve.mark())
                    tensor2(pool, tile, tile, b_out[:, :], ALU.add)
                    yield

        n = BATCH * GROUPS
        together(front(0))
        for g in range(n):
            if g % GROUPS == 0:
                done["xn_read", g // GROUPS] = ()
            together(front(g + 1) if g + 1 < n else None, back(g))
            done["xn_read", g // GROUPS] = got("projected", g // GROUPS) + got("v_made", g // GROUPS)
        core.run()


def build(nc, d, out):
    with ExitStack() as ctx:
        core = Core(nc, ctx)
        x = ctx.enter_context(nc.sbuf_tensor("x", [P, TILES, DIM], F32))
        recurrent_mixer(core, x, d["hidden_states"], d)
        feed_forward(core, x, d, "ffn1")
        attention(core, x, d)
        feed_forward(core, x, d, "ffn2", out)


BY_PARTITION = ("mu_x", "x_bias")
TRANSPOSED = ("W_x1", "W_x2", "W_r", "W_k", "W_v", "W_g", "A_w", "B_w", "W_o", "fast_b")


def lay_out(name, a):
    a = np.asarray(a)
    if name in TRANSPOSED:
        a = a.T
    if name in BY_PARTITION:
        a = np.moveaxis(a.reshape(a.shape[:-1] + (-1, P)), -1, 0)
    return np.ascontiguousarray(a.reshape(1, 1) if a.ndim == 0 else a)


def kernel(**inputs):
    import concourse.bacc as bacc
    from concourse.bass_utils import run_bass_kernel_spmd

    nc = bacc.Bacc("TRN2", target_bir_lowering=False, num_devices=1)
    arrays, d = {}, {}
    for name, a in list(inputs.items()) + list(constants().items()):
        short = name.replace("L0_attn_a_", "").replace("L0_attn_b_", "").replace("L0_ffn_", "")
        a = lay_out(short, a)
        arrays[short] = a
        d[short] = nc.dram_tensor(short, a.shape, mybir.dt.from_np(a.dtype), kind="ExternalInput").ap()
    out = nc.dram_tensor("out", (BATCH, SEQ, DIM), F32, kind="ExternalOutput").ap()
    build(nc, d, out)
    return run_bass_kernel_spmd(nc, [arrays], core_ids=[0]).results[0]["out"]
```

```python
import math
from contextlib import ExitStack

import numpy as np
from concourse import mybir

F32 = mybir.dt.float32
BF16 = mybir.dt.bfloat16
F32R = mybir.dt.float32r
ALU = mybir.AluOpType
ACT = mybir.ActivationFunctionType
AX = mybir.AxisListType

P = 128
BATCH, SEQ, DIM = 8, 1024, 256
KT = DIM // P
TOKENS = BATCH * SEQ
TILES = TOKENS // P
BANK = 512
CHUNK = BANK
CT = CHUNK // P
CHUNKS = TOKENS // CHUNK
EPS = 1e-5

HEADS_A, KD, VD, LOWRANK, GATERANK, MIXES = 4, 128, 256, 32, 64, 5
HK, HV = KD // HEADS_A, VD // HEADS_A
SUB = 32
DIAG = 6
TREE = 7

HIDDEN, RANK = 1024, 16
HT = HIDDEN // P

HEADS, HD, GROUP = 16, 16, 4
GROUPS = HEADS // GROUP
QB = SEQ // P
HALVES = SEQ // BANK
MAIN = 3 * HD
BIASROWS = 4 * QB
SHIFTROW = 96
STACK = SHIFTROW + 2


def rounded(a, bits):
    m, e = np.frexp(np.asarray(a, np.float64))
    return np.ldexp(np.rint(m * 2 ** bits) / 2 ** bits, e).astype(np.float32)


def hi_lo(a):
    hi = rounded(a, 12)
    return hi, rounded(a - hi, 12)


def thirds(a):
    parts = [rounded(a, 8)]
    while len(parts) < 3 and np.any(parts[0] != a):
        parts.append(rounded(a - sum(p.astype(np.float64) for p in parts), 8))
    return parts


def slopes():
    start = 2 ** (-2 ** (-(math.log2(HEADS) - 3)))
    return np.asarray([start ** i for i in range(HEADS)], dtype=np.float32)


def block_bias(h):
    near = np.arange(P)
    return thirds(-float(slopes()[h]) * np.abs(near[:, None] - near[None, :]))


def constants():
    c = {"c_ident": np.eye(P, dtype=np.float32)}
    s, t = np.arange(P)[:, None] % SUB, np.arange(SUB)[None, :]
    parts = [s == t]
    for level in range(DIAG - 1):
        m = 1 << level
        parts.append((s // (2 * m) == t // (2 * m)) & (s // m % 2 == 0) & (t // m % 2 == 1))
    c["c_mask"] = np.stack(parts, 1).astype(np.float32).reshape(P, DIAG * SUB)
    q = np.arange(SEQ)
    picked = (q[None, :] // P == np.arange(QB)[:, None]).astype(np.float32)
    c["c_qrows"] = np.concatenate([picked * (q % P)] * 2 + [picked] * 2 +
                                  [np.zeros((SHIFTROW - MAIN - BIASROWS, SEQ))]).astype(np.float32)
    c["c_krows"] = np.repeat([0.0, 1.0], [SHIFTROW - MAIN - BIASROWS, STACK - SHIFTROW])[:, None] \
        .repeat(SEQ, 1).astype(np.float32)
    i, j = np.arange(QB)[:, None], q[None, :] // P
    sign = np.sign(i - j)
    kbias = []
    for slope in slopes().astype(np.float64):
        a, b = hi_lo(-slope * sign), hi_lo(slope * (sign * (q % P) - P * np.abs(i - j)))
        kbias.append(np.concatenate([a[0], a[1], b[0], b[1]]))
    c["c_kbias"] = np.stack(kbias)
    c["c_block"] = np.stack([part for h in range(HEADS) for part in block_bias(h)], 1)
    return {k: np.ascontiguousarray(v) for k, v in c.items()}


class Queue:

    def __init__(self, sem):
        self.sem, self.items, self.count, self.reached = sem, [], 0, {}

    def do(self, issue):
        self.items.append([issue, None, 0])

    def wait(self, *tokens):
        for sem, value in tokens:
            if self.reached.get(sem.name, 0) < value:
                self.reached[sem.name] = value
                self.items.append([None, sem, value])

    def mark(self):
        last = self.items[-1]
        if last[1] is None:
            self.count += 1
            last[1], last[2] = self.sem, 1
            self.marked = (self.sem, self.count)
        return self.marked

    def emit(self, engine):
        for issue, sem, value in self.items:
            if issue is None:
                engine.wait_ge(sem, value)
            elif sem is None:
                issue(engine)
            else:
                issue(engine).then_inc(sem, value)
        self.items = []


class Lane:

    def __init__(self, sem):
        self.sem, self.count = sem, 0

    def start(self, queue, out, in_):
        self.count += 16
        queue.items.append([lambda e: e.dma_start(out, in_), self.sem, 16])
        return (self.sem, self.count)


class Slot:

    def __init__(self, buf):
        self.buf, self.read = buf, ()


class Ring:
    def __init__(self, bufs):
        self.slots, self.n = [Slot(b) for b in bufs], 0

    def take(self):
        self.n += 1
        return self.slots[(self.n - 1) % len(self.slots)]


def matmul(pe, out, lhsT, rhs, start=True, stop=True, tile=None):
    if tile is None:
        pe.do(lambda e: e.matmul(out, lhsT, rhs, start=start, stop=stop))
    else:
        pe.do(lambda e: e.matmul(out, lhsT, rhs, start=start, stop=stop, tile_position=tile))


def transpose(pe, out, in_, ident):
    pe.do(lambda e: e.transpose(out, in_, ident))


def activation(act, out, in_, func, bias=0.0, scale=1.0):
    act.do(lambda e: e.activation(out, in_, func, bias=bias, scale=scale))


def copy(q, out, in_):
    q.do(lambda e: e.tensor_copy(out, in_))


def act_copy(act, out, in_):
    act.do(lambda e: e.activation(out, in_, ACT.Copy))


def tensor2(q, out, a, b, op):
    q.do(lambda e: e.tensor_tensor(out, a, b, op))


def scalar2(q, out, in_, s1, s2, op0, op1):
    q.do(lambda e: e.tensor_scalar(out, in_, s1, s2, op0, op1))


def scalar1(q, out, in_, s1, op0):
    q.do(lambda e: e.tensor_scalar(out, in_, s1, None, op0))


def fused(dve, out, in0, scalar, in1, op0, op1):
    dve.do(lambda e: e.scalar_tensor_tensor(out=out, in0=in0, scalar=scalar, in1=in1, op0=op0, op1=op1))


def reduce(dve, out, in_, op, negate=False, absolute=False):
    dve.do(lambda e: e.tensor_reduce(out, in_, axis=AX.X, op=op, negate=negate, apply_absolute_value=absolute))


def memset(q, out, value):
    q.do(lambda e: e.memset(out, value))


def spread(ap, n):
    return ap.unsqueeze(len(ap.shape)).to_broadcast(list(ap.shape) + [n])


def token_tiles(dram):
    return dram.rearrange("b (t p) c -> p (b t) c", p=P)


def words(ap):
    return ap.bitcast(F32)


class Pipeline:

    def __init__(self):
        self.steps = {}

    def together(self, *stages):
        running = [[s[0], s[1], 0, s[2] if len(s) > 2 else 1.0] for s in stages if s is not None]
        while running:
            stage = min(running, key=lambda r: (r[2] + 0.5) / (self.steps.get(r[0], 16) * r[3]))
            if next(stage[1], running) is running:
                self.steps[stage[0]] = max(stage[2], 1)
                running.remove(stage)
            stage[2] += 1


class Core:
    def __init__(self, nc, ctx):
        self.nc = nc
        sem = lambda n: ctx.enter_context(nc.semaphore(n))
        self.pe, self.act, self.dve = Queue(sem("pe_done")), Queue(sem("act_done")), Queue(sem("dve_done"))
        self.pool, self.sp = Queue(sem("pool_done")), Queue(sem("sp_done"))
        self.banks = ctx.enter_context(nc.psum_tensor("banks", [P, 8, BANK], F32))

    def run(self):
        with self.nc.Block() as block:
            block.sync(self.sp.emit)
            block.tensor(self.pe.emit)
            block.scalar(self.act.emit)
            block.vector(self.dve.emit)
            block.gpsimd(self.pool.emit)


class Normalizer:

    def __init__(self, core, sb, name, tiles):
        self.core, self.tiles = core, tiles
        self.stats = sb(f"{name}_stats", [P, tiles, 6])
        self.mean_var = sb(f"{name}_mean_var", [P, tiles, 2])
        self.rstd = sb(f"{name}_rstd", [P, tiles])
        self.minus_half = sb(f"{name}_minus_half", [P, tiles])
        memset(core.pool, self.minus_half[:, :], -0.5)
        self.ready = core.pool.mark()
        self.applied = ()

    def statistics(self, x, arrived):
        dve, pool = self.core.dve, self.core.pool
        dve.wait(*arrived, *self.applied)
        for i in range(self.tiles):
            dve.do(lambda e, i=i: e.bn_stats(self.stats[:, i, :], x[:, i, :]))
        dve.wait(dve.mark())
        for i in range(self.tiles):
            dve.do(lambda e, i=i: e.bn_aggr(self.mean_var[:, i, :], self.stats[:, i, :]))
        pool.wait(self.ready, dve.mark())
        scalar1(pool, self.rstd[:, :], self.mean_var[:, :, 1], EPS, ALU.add)
        pool.wait(pool.mark())
        tensor2(pool, self.rstd[:, :], self.rstd[:, :], self.minus_half[:, :], ALU.pow)
        return pool.mark()

    def scale(self, out, x, i):
        scalar2(self.core.dve, out, x[:, i, :], self.mean_var[:, i, 0:1], self.rstd[:, i:i + 1],
                ALU.subtract, ALU.mult)


def recurrent_mixer(core, x_in, x_out, d):
    nc, pe, act, dve, pool, sp, banks = core.nc, core.pe, core.act, core.dve, core.pool, core.sp, core.banks
    with ExitStack() as ctx:
        sb = lambda n, s, dt=F32: ctx.enter_context(nc.sbuf_tensor("a_" + n, s, dt))
        lane = lambda n: Lane(ctx.enter_context(nc.semaphore("a_" + n)))
        C2 = 2 * SUB
        X_BUFS = 5

        ident, mask = sb("ident", [P, P]), sb("mask", [P, DIAG * SUB])
        mu_x, x_bias = sb("mu_x", [P, KT]), sb("x_bias", [P, MIXES, KT])
        w_x1 = sb("w_x1", [P, KT, 2 * P])
        w_x2 = sb("w_x2", [P, MIXES, DIM])
        w_r, w_k = sb("w_r", [P, KT, KD]), sb("w_k", [P, KT, KD])
        w_v, w_g, w_o = sb("w_v", [P, KT, VD]), sb("w_g", [P, KT, VD]), sb("w_o", [P, KT, DIM])
        w_a, w_b = sb("w_a", [P, KT, GATERANK]), sb("w_b", [GATERANK, KD])
        b_w, bonus = sb("b_w", [P, 1]), sb("bonus", [P, 1])
        gn_w, gn_b = sb("gn_w", [P, VD]), sb("gn_b", [P, VD])

        xs = [sb(f"x{i}", [P, CT, DIM]) for i in range(X_BUFS)]
        xn = Ring([sb(f"xn{i}", [P, DIM]) for i in range(4)])
        xn_t = [sb(f"xn_t{i}", [P, KT, 1 + CHUNK]) for i in range(2)]
        delta = sb("delta", [P, KT, CHUNK])
        z = sb("z", [P, 2, CHUNK])
        mix = Ring([sb(f"mix{i}", [P, KT, CHUNK]) for i in range(2)])
        gate_low = sb("gate_low", [GATERANK, CHUNK])
        w_exp = sb("w_exp", [P, CHUNK])
        decay = [sb(f"decay{i}", [P, 2 * CHUNK]) for i in range(2)]
        q = [sb(f"q{i}", [P, CHUNK]) for i in range(2)]
        k = [sb(f"k{i}", [P, CHUNK]) for i in range(2)]
        q_up = [None] + [sb(f"q_up{l}", [P, CHUNK]) for l in range(1, TREE + 1)]
        k_up = [None] + [sb(f"k_up{l}", [P, CHUNK]) for l in range(1, TREE + 1)]
        k_bonus = sb("k_bonus", [P, CHUNK])
        v = [sb(f"v{i}", [P, CT, VD]) for i in range(2)]
        g_tanh = sb("g_tanh", [P, CT, VD])
        gate = [sb(f"gate{i}", [P, CT, VD]) for i in range(3)]
        masked = sb("masked", [P, HEADS_A, DIAG * SUB])
        diag = sb("diag", [P, HEADS_A, SUB])
        pair = Ring([sb(f"pair{i}", [P, HEADS_A, P]) for i in range(2)])
        k_tok = Ring([sb(f"k_tok{i}", [P, P]) for i in range(2)])
        state = [sb(f"state{i}", [P, VD]) for i in range(2)]
        o_bufs = [sb(f"o{i}", [P, CT, VD]) for i in range(2)]
        o_sq = sb("o_sq", [P, CT, VD])
        o_t = sb("o_t", [P, KT, CHUNK])
        sums, rstd, half = sb("sums", [P, CT * HEADS_A]), sb("rstd", [P, CT * HEADS_A]), sb("half", [P, CT * HEADS_A])

        weights = lane("weights")
        loads, stores = [lane(f"load{i}") for i in range(X_BUFS)], [lane(f"store{i}") for i in range(X_BUFS)]
        for w in (w_x1, w_x2):
            memset(pool, w[:], 0.0)
        sp.wait(pool.mark())
        tiled = lambda ap: ap.rearrange("(k p) n -> p k n", p=P)
        column = lambda ap: ap.rearrange("(p a) -> p a", a=1)
        done = {}
        got = lambda what, c: done.get((what, c), ())

        def load_x(c):
            if c < CHUNKS:
                sp.wait(*got("stored", c - X_BUFS))
                done["x", c] = (loads[c % X_BUFS].start(sp, xs[c % X_BUFS][:, :, :],
                                                        token_tiles(x_in)[:, c * CT:(c + 1) * CT, :]),)

        load_x(0)
        weights.start(sp, ident[:, :], d["c_ident"])
        weights.start(sp, mu_x[:, :], d["mu_x"])
        weights.start(sp, w_x1[:, :, 0:MIXES * LOWRANK], tiled(d["W_x1"]))
        for n in range(MIXES):
            r = n * LOWRANK % P
            weights.start(sp, w_x2[r:r + LOWRANK, n, :], d["W_x2"][n * LOWRANK:(n + 1) * LOWRANK, :])
        weights.start(sp, x_bias[:, :, :], d["x_bias"])
        for t, name in ((w_r, "W_r"), (w_k, "W_k"), (w_v, "W_v"), (w_g, "W_g"), (w_o, "W_o"), (w_a, "A_w")):
            weights.start(sp, t[:, :, :], tiled(d[name]))
        weights.start(sp, w_b[:, :], d["B_w"])
        weights.start(sp, b_w[:, :], column(d["b_w"]))
        weights.start(sp, bonus[:, :], column(d["bonus"].rearrange("h k -> (h k)")))
        weights.start(sp, mask[:, :], d["c_mask"])
        weights.start(sp, gn_w[:, :], d["gn_weight"].partition_broadcast(P))
        loaded = weights.start(sp, gn_b[:, :], d["gn_bias"].partition_broadcast(P))
        load_x(1)
        for s in pair.slots:
            memset(pool, s.buf[:], 0.0)
        for s in state:
            memset(pool, s[:, :], 0.0)
        memset(pool, half[:, :], -0.5)
        zeroed = pool.mark()
        norm = Normalizer(core, sb, "norm", CT)
        for e in (pe, act, dve, pool):
            e.wait(loaded, zeroed)

        bank = lambda i: banks[:, i, :]
        front, back = Ring([bank(0), bank(1)]), Ring([bank(2), bank(3)])
        products = Slot(banks[:, 4:8, :])
        def prepare(c):
            par, x = c % 2, xs[c % X_BUFS]
            xt, q0, k0, dec = xn_t[par], q[par], k[par], decay[par]
            load_x(c + 2)
            rstd_done = norm.statistics(x, got("x", c))
            dve.wait(rstd_done)
            slots = []
            for i in range(CT):
                s = xn.take()
                dve.wait(*s.read)
                norm.scale(s.buf[:, :], x, i)
                slots.append((s, dve.mark()))
            norm.applied = (dve.mark(),)
            yield
            for kt in range(KT):
                b = front.take()
                pe.wait(*b.read)
                for i, (s, scaled) in enumerate(slots):
                    pe.wait(scaled)
                    transpose(pe, b.buf[:, i * P:(i + 1) * P], s.buf[:, kt * P:(kt + 1) * P], ident[:, :])
                    s.read = (pe.mark(),)
                act.wait(pe.mark(), *got("mixed", c - 2), *got("carried", c - 1))
                act_copy(act, xt[:, kt, 1:], b.buf)
                b.read = (act.mark(),)
            xt_done = act.mark()
            if c % (SEQ // CHUNK) == 0:
                pool.wait(*got("mixed", c - 2))
                memset(pool, xt[:, :, 0:1], 0.0)
            else:
                pool.wait(*got("xt", c - 1), *got("mixed", c - 2))
                copy(pool, xt[:, :, 0:1], xn_t[1 - par][:, :, CHUNK:CHUNK + 1])
            carried = pool.mark()
            done["carried", c], done["xt", c] = (carried,), (xt_done,)
            yield
            dve.wait(xt_done, carried, *got("mixed", c - 1))
            tensor2(dve, delta[:, :, :], xt[:, :, 0:CHUNK], xt[:, :, 1:], ALU.subtract)
            mixed_x = mix.take()
            dve.wait(dve.mark(), *mixed_x.read)
            for kt in range(KT):
                fused(dve, mixed_x.buf[:, kt, :], delta[:, kt, :], mu_x[:, kt:kt + 1], xt[:, kt, 1:], ALU.mult, ALU.add)
            mixed_done = dve.mark()
            for m in range(2):
                b = front.take()
                pe.wait(mixed_done, *b.read)
                for kt in range(KT):
                    matmul(pe, b.buf, w_x1[:, kt, m * P:(m + 1) * P], mixed_x.buf[:, kt, :], kt == 0, kt == KT - 1)
                act.wait(pe.mark(), *got("mus", c - 1))
                activation(act, z[:, m, :], b.buf, ACT.Tanh)
                b.read = (act.mark(),)
            mixed_x.read = (pe.mark(),)
            z_done = act.mark()
            yield

            def mix_in(n):
                s = mix.take()
                for kt in range(KT):
                    b = front.take()
                    pe.wait(z_done, *b.read)
                    matmul(pe, b.buf, w_x2[:, n, kt * P:(kt + 1) * P], z[:, n * LOWRANK // P, :])
                    dve.wait(pe.mark(), *s.read)
                    fused(dve, s.buf[:, kt, :], b.buf, x_bias[:, n, kt:kt + 1], delta[:, kt, :], ALU.add, ALU.mult)
                    b.read = (dve.mark(),)
                pool.wait(dve.mark())
                tensor2(pool, s.buf[:, :, :], s.buf[:, :, :], xt[:, :, 1:], ALU.add)
                return s, pool.mark()

            def project(w, s, mixed, rows=P):
                b = front.take()
                pe.wait(mixed, *b.read)
                for kt in range(KT):
                    matmul(pe, b.buf[0:rows, :], w[:, kt, :], s.buf[:, kt, :], kt == 0, kt == KT - 1)
                s.read = (pe.mark(),)
                return b, pe.mark()

            s, mixed = mix_in(1)
            yield
            b, projected = project(w_a, s, mixed, GATERANK)
            act.wait(projected, *got("w", c - 1))
            activation(act, gate_low[:, :], b.buf[0:GATERANK, :], ACT.Tanh)
            b.read = (act.mark(),)
            b = front.take()
            pe.wait(act.mark(), *b.read)
            matmul(pe, b.buf, w_b[:, :], gate_low[:, :])
            done["w", c] = (pe.mark(),)
            act.wait(pe.mark(), act.mark())
            activation(act, w_exp[:, :], b.buf, ACT.Exp, bias=b_w[:, 0:1])
            b.read = (act.mark(),)
            act.wait(act.mark(), *got("recurred", c - 2))
            activation(act, dec[:, 0:CHUNK], w_exp[:, :], ACT.Exp, scale=-1.0)
            done["decay", c] = (act.mark(),)
            yield
            for n, w, t, what in ((0, w_r, q0, "q"), (2, w_k, k0, "k")):
                s, mixed = mix_in(n)
                yield
                b, projected = project(w, s, mixed)
                act.wait(projected, *got("recurred", c - 2))
                act_copy(act, t[:, :], b.buf)
                b.read = (act.mark(),)
                done[what, c] = (act.mark(),)
                yield
            for n, w in ((3, w_v), (4, w_g)):
                s, mixed = mix_in(n)
                yield
                for half_chunk in range(CT // 2):
                    b = front.take()
                    pe.wait(mixed, *b.read)
                    for i in range(2):
                        tok = (2 * half_chunk + i) * P
                        for kt in range(KT):
                            matmul(pe, b.buf[:, i * VD:(i + 1) * VD], s.buf[:, kt, tok:tok + P], w[:, kt, :],
                                   kt == 0, kt == KT - 1)
                    s.read = (pe.mark(),)
                    two = slice(2 * half_chunk, 2 * half_chunk + 2)
                    bank2 = b.buf.rearrange("p (t n) -> p t n", t=2)
                    if n == 3:
                        act.wait(pe.mark(), *got("recurred", c - 2))
                        act_copy(act, v[par][:, two, :], bank2)
                        b.read = (act.mark(),)
                    else:
                        act.wait(pe.mark(), *got("gated", c - 1))
                        activation(act, g_tanh[:, two, :], bank2, ACT.Tanh, scale=0.5)
                        dve.wait(act.mark(), *got("gate_read", c - 3))
                        fused(dve, gate[c % 3][:, two, :], g_tanh[:, two, :], 1.0, bank2, ALU.add, ALU.mult)
                        b.read = (dve.mark(),)
                if n == 3:
                    done["v", c] = (act.mark(),)
                    yield
            done["mus", c] = (pe.mark(),)
            done["gated", c] = (dve.mark(),)
            done["mixed", c] = (pool.mark(), dve.mark())

        def recur(c):
            par, o = c % 2, o_bufs[c % 2]
            qs, ks = [q[par]] + q_up[1:], [k[par]] + k_up[1:]
            dec = decay[par]
            offset = [0]
            for l in range(TREE):
                offset.append(offset[-1] + (CHUNK >> l))
            totals = [dec[:, offset[l]:offset[l] + (CHUNK >> l)] for l in range(TREE + 1)]
            previous = got("recurred", c - 1)
            dve.wait(*got("k", c), *got("q", c), *got("decay", c), *previous)
            act.wait(*got("k", c), *got("q", c), *previous)
            pool.wait(*got("k", c), *got("decay", c), *previous)
            scalar1(pool, k_bonus[:, :], ks[0][:, :], bonus[:, 0:1], ALU.mult)
            ready = [pool.mark()]
            for l in range(TREE):
                blocks = lambda ap: ap.rearrange("p (n two m) -> p n two m", two=2, m=1 << l)
                tot = totals[l].rearrange("p (n two) -> p n two", two=2)
                tensor2(dve, blocks(qs[l + 1][:, :])[:, :, 1, :], blocks(qs[l][:, :])[:, :, 1, :],
                        spread(tot[:, :, 0], 1 << l), ALU.mult)
                tensor2(dve, totals[l + 1], tot[:, :, 0], tot[:, :, 1], ALU.mult)
                stepped = dve.mark()
                tensor2(pool, blocks(ks[l + 1][:, :])[:, :, 0, :], blocks(ks[l][:, :])[:, :, 0, :],
                        spread(tot[:, :, 1], 1 << l), ALU.mult)
                key = pool.mark()
                act_copy(act, blocks(qs[l + 1][:, :])[:, :, 0, :], blocks(qs[l][:, :])[:, :, 0, :])
                act_copy(act, blocks(ks[l + 1][:, :])[:, :, 1, :], blocks(ks[l][:, :])[:, :, 1, :])
                kept = act.mark()
                for e in (dve, pool, act):
                    e.wait(stepped, key, kept)
                ready.append(stepped)
                yield
            levelled = [stepped, key, kept, ready[0]]
            pe.wait(*levelled, *got("v", c))

            def pair_products(i):
                tok = i * P
                pe.wait(*products.read)
                for part in range(DIAG):
                    kk, qq = (k_bonus, qs[0]) if part == 0 else (ks[part - 1], qs[part - 1])
                    for j in range(P // SUB):
                        t0 = tok + j * SUB
                        for h in range(HEADS_A):
                            r = h * HK
                            matmul(pe, products.buf[j * SUB:(j + 1) * SUB, h, part * SUB:(part + 1) * SUB],
                                   kk[r:r + HK, t0:t0 + SUB], qq[r:r + HK, t0:t0 + SUB], tile=(r, j * SUB))
                off = DIAG * SUB
                for j in (0, 2):
                    t0 = tok + j * SUB
                    for h in range(HEADS_A):
                        r = h * HK
                        matmul(pe, products.buf[j * SUB:(j + 1) * SUB, h, off:off + SUB],
                               ks[5][r:r + HK, t0:t0 + SUB], qs[5][r:r + HK, t0 + SUB:t0 + C2], tile=(r, j * SUB))
                for h in range(HEADS_A):
                    r = h * HK
                    matmul(pe, products.buf[0:C2, h, off + SUB:off + SUB + C2],
                           ks[6][r:r + HK, tok:tok + C2], qs[6][r:r + HK, tok + C2:tok + P], tile=(r, 0))
                multiplied = pe.mark()
                b = back.take()
                pe.wait(*b.read)
                transpose(pe, b.buf[:, 0:P], ks[TREE][:, tok:tok + P], ident[:, :])
                turned, keys, s = pe.mark(), k_tok.take(), pair.take()
                dve.wait(multiplied, *got("summed", 0))
                tensor2(dve, masked[:, :, :], products.buf[:, :, 0:off],
                        mask[:, :].unsqueeze(1).to_broadcast([P, HEADS_A, off]), ALU.mult)
                act.wait(multiplied, dve.mark(), *s.read)
                act_copy(act, s.buf[0:SUB, :, SUB:C2], products.buf[0:SUB, :, off:off + SUB])
                act_copy(act, s.buf[C2:C2 + SUB, :, C2 + SUB:P], products.buf[C2:C2 + SUB, :, off:off + SUB])
                act_copy(act, s.buf[0:C2, :, C2:P], products.buf[0:C2, :, off + SUB:off + SUB + C2])
                products.read = (dve.mark(), act.mark())
                act.wait(turned, *keys.read)
                act_copy(act, keys.buf[:, :], b.buf[:, 0:P])
                b.read = (act.mark(),)
                k_turned = act.mark()
                dve.wait(dve.mark(), *got("placed", 0))
                reduce(dve, diag[:, :, :], masked[:, :, :].rearrange("p h (l t) -> p h t l", l=DIAG), ALU.add)
                done["summed", 0] = (dve.mark(),)
                act.wait(dve.mark())
                for j in range(P // SUB):
                    act_copy(act, s.buf[j * SUB:(j + 1) * SUB, :, j * SUB:(j + 1) * SUB],
                             diag[j * SUB:(j + 1) * SUB, :, :])
                done["placed", 0] = (act.mark(),)
                return keys, k_turned, s, act.mark()

            def advance(i, keys, k_turned, s, placed):
                tok = i * P
                first_of_sequence = (c * CT + i) % QB == 0
                now, then = (c * CT + i) % 2, (c * CT + i + 1) % 2
                b = back.take()
                pe.wait(k_turned, *b.read)
                for h in range(HEADS_A):
                    r = h * HK
                    matmul(pe, b.buf[r:r + HK, 0:HV], keys.buf[:, r:r + HK], v[par][:, i, h * HV:(h + 1) * HV],
                           tile=(0, r))
                keys.read = (pe.mark(),)
                kv_done, kv = pe.mark(), b
                b = back.take()
                pe.wait(*b.read, *got("state", 0))
                if not first_of_sequence:
                    matmul(pe, b.buf[:, 0:VD], qs[TREE][:, tok:tok + P], state[now][:, :], True, False)
                dve.wait(kv_done, *got("state_read", 0), *got("state", 0))
                for h in range(HEADS_A):
                    r, cols = h * HK, slice(h * HV, (h + 1) * HV)
                    if first_of_sequence:
                        copy(dve, state[then][r:r + HK, cols], kv.buf[r:r + HK, 0:HV])
                    else:
                        fused(dve, state[then][r:r + HK, cols], state[now][r:r + HK, cols],
                              totals[TREE][r:r + HK, i:i + 1], kv.buf[r:r + HK, 0:HV], ALU.mult, ALU.add)
                kv.read = (dve.mark(),)
                done["state", 0] = (dve.mark(),)
                pe.wait(placed)
                for h in range(HEADS_A):
                    matmul(pe, b.buf[:, h * HV:(h + 1) * HV], s.buf[:, h, :], v[par][:, i, h * HV:(h + 1) * HV],
                           first_of_sequence, first_of_sequence or h == HEADS_A - 1)
                s.read = done["state_read", 0] = (pe.mark(),)
                act.wait(pe.mark(), *got("o_read", c - 2))
                act_copy(act, o[:, i, :], b.buf[:, 0:VD])
                b.read = (act.mark(),)

            ahead = pair_products(0)
            yield
            for i in range(CT):
                current = ahead
                if i + 1 < CT:
                    ahead = pair_products(i + 1)
                    yield
                advance(i, *current)
                yield
            done["o", c] = (act.mark(),)
            done["recurred", c] = (pe.mark(), dve.mark(), act.mark())

        def finish(c):
            o, x = o_bufs[c % 2], xs[c % X_BUFS]
            groups = lambda ap: ap.rearrange("p t (h n) -> p (t h) n", n=HV)
            dve.wait(*got("o", c), *got("rstd_read", c - 1))
            reduce(dve, sums[:, :], groups(o[:, :, :]), ALU.add)
            dve.wait(dve.mark())
            scalar1(dve, sums[:, :], sums[:, :], 1.0 / HV, ALU.mult)
            dve.wait(dve.mark())
            tensor2(dve, groups(o[:, :, :]), groups(o[:, :, :]), spread(sums[:, :], HV), ALU.subtract)
            act.wait(dve.mark(), *got("squares", c - 1))
            activation(act, o_sq[:, :, :], o[:, :, :], ACT.Square)
            yield
            dve.wait(act.mark(), *got("rstd_read", c - 1))
            reduce(dve, rstd[:, :], groups(o_sq[:, :, :]), ALU.add)
            done["squares", c] = (dve.mark(),)
            pool.wait(dve.mark())
            scalar2(pool, rstd[:, :], rstd[:, :], 1.0 / HV, EPS, ALU.mult, ALU.add)
            pool.wait(pool.mark())
            tensor2(pool, rstd[:, :], rstd[:, :], half[:, :], ALU.pow)
            dve.wait(pool.mark())
            tensor2(dve, groups(o[:, :, :]), groups(o[:, :, :]), spread(rstd[:, :], HV), ALU.mult)
            done["rstd_read", c] = (dve.mark(),)
            yield
            wide = lambda ap: ap.unsqueeze(1).to_broadcast([P, CT, VD])
            pool.wait(dve.mark(), *got("gated", c))
            tensor2(pool, o[:, :, :], o[:, :, :], wide(gn_w[:, :]), ALU.mult)
            pool.wait(pool.mark())
            tensor2(pool, o[:, :, :], o[:, :, :], wide(gn_b[:, :]), ALU.add)
            dve.wait(pool.mark())
            fused(dve, o[:, :, :], o[:, :, :], 0.5, gate[c % 3][:, :, :], ALU.mult, ALU.mult)
            done["gate_read", c] = (dve.mark(),)
            out_ready = dve.mark()
            yield
            pe.wait(out_ready)
            for kt in range(KT):
                b = back.take()
                pe.wait(*b.read)
                for i in range(CT):
                    transpose(pe, b.buf[:, i * P:(i + 1) * P], o[:, i, kt * P:(kt + 1) * P], ident[:, :])
                act.wait(pe.mark(), *got("projected", c - 1))
                act_copy(act, o_t[:, kt, :], b.buf)
                b.read = (act.mark(),)
            done["o_read", c] = (pe.mark(),)
            turned = act.mark()
            for i in range(CT):
                b = back.take()
                pe.wait(turned, *b.read)
                for kt in range(KT):
                    matmul(pe, b.buf[:, 0:DIM], o_t[:, kt, i * P:(i + 1) * P], w_o[:, kt, :], kt == 0, kt == KT - 1)
                dve.wait(pe.mark())
                tensor2(dve, x[:, i, :], x[:, i, :], b.buf[:, 0:DIM], ALU.add)
                b.read = (dve.mark(),)
                if i % 2:
                    yield
            done["projected", c] = (pe.mark(),)
            sp.wait(dve.mark())
            done["stored", c] = (stores[c % X_BUFS].start(sp, token_tiles(x_out)[:, c * CT:(c + 1) * CT, :], x[:, :, :]),)

        pipeline = Pipeline()
        for c in range(-1, CHUNKS + 1):
            pipeline.together(("recur", recur(c)) if 0 <= c < CHUNKS else None,
                              ("finish", finish(c - 1)) if c > 0 else None,
                              ("prepare", prepare(c + 1)) if c + 1 < CHUNKS else None)
        for s in stores:
            sp.wait((s.sem, s.count))
        core.run()


def feed_forward(core, x_in, x_out, d, tag):
    nc, pe, act, dve, pool, sp, banks = core.nc, core.pe, core.act, core.dve, core.pool, core.sp, core.banks
    with ExitStack() as ctx:
        sb = lambda n, s, dt=F32: ctx.enter_context(nc.sbuf_tensor(f"{tag}_{n}", s, dt))
        lane = lambda n: Lane(ctx.enter_context(nc.semaphore(f"{tag}_{n}")))
        COPIES = 3
        ROWS = COPIES * SUB
        ident = sb("ident", [P, P])
        fc = sb("fc", [P, HT, DIM])
        proj = sb("proj", [P, KT, HIDDEN])
        u, v, fast_b = sb("u", [P, HT, RANK]), sb("v", [RANK, DIM]), sb("fast_b", [RANK, RANK])
        gate = sb("gate", [P, 1])
        fc_t, proj_t = sb("fc_t", [P, KT, HIDDEN], F32R), sb("proj_t", [P, HT, DIM], F32R)
        scale_fc, gate_fc = sb("scale_fc", [P, HT]), sb("gate_fc", [P, HT])
        scale_proj, scale_row = sb("scale_proj", [P, KT]), sb("scale_row", [P, DIM])
        upper, lower = sb("upper", [P, HT]), sb("lower", [P, HT])
        below = Ring([sb(f"below{i}", [P, P]) for i in range(2)])
        tern = Ring([sb(f"tern{i}", [P, P]) for i in range(2)])
        ones, diagonal = sb("ones", [P, P]), sb("diagonal", [P, P])
        u3 = sb("u3", [P, HT, ROWS])
        u3_t = sb("u3_t", [ROWS, HIDDEN], F32R)
        low_in = sb("low_in", [P, KT, ROWS])
        low_hi, low_lo = sb("low_hi", [P, KT, ROWS], F32R), sb("low_lo", [P, KT, ROWS], F32R)

        X_BUFS = 4
        xs = [sb(f"x{i}", [P, CT, DIM]) for i in range(X_BUFS)]
        xn = Ring([sb(f"xn{i}", [P, DIM]) for i in range(4)])
        x_hi = Ring([sb(f"x_hi{i}", [P, KT, CHUNK], F32R) for i in range(2)])
        x_lo_bufs = [sb(f"x_lo{i}", [P, KT, CHUNK], F32R) for i in range(2)]
        low = sb("low", [ROWS, CHUNK], F32R)
        relu = Ring([sb(f"relu{i}", [P, CHUNK]) for i in range(2)])
        square = Ring([sb(f"square{i}", [P, CHUNK]) for i in range(2)])
        r_hi = [sb(f"r_hi{i}", [P, HT, CHUNK], F32R) for i in range(2)]
        r_lo = [sb(f"r_lo{i}", [P, HT, CHUNK], F32R) for i in range(2)]
        scaled_out = Ring([sb(f"scaled_out{i}", [P, DIM]) for i in range(2)])

        bank = lambda i: banks[:, i, :]
        front, back = Ring([bank(i) for i in range(5)]), Ring([bank(i) for i in range(5, 8)])
        norm = Normalizer(core, sb, "norm", CT)

        weights = lane("weights")
        weights.start(sp, ident[:, :], d["c_ident"])
        weights.start(sp, fc[:, :, :], d["w_fc"].rearrange("(m p) n -> p m n", p=P))
        weights.start(sp, proj[:, :, :], d["w_proj"].rearrange("(m p) n -> p m n", p=P))
        weights.start(sp, u[:, :, :], d["u"].rearrange("(m p) n -> p m n", p=P))
        weights.start(sp, v[:, :], d["v"])
        weights.start(sp, fast_b[:, :], d["fast_b"])
        loaded = weights.start(sp, gate[:, :], d["gate"].to_broadcast([P, 1]))
        memset(pool, ones[:, :], 1.0)
        memset(pool, u3[:, :, :], 0.0)
        memset(pool, low_in[:, :, :], 0.0)
        zeroed = pool.mark()
        for e in (pe, act, dve, pool):
            e.wait(loaded, zeroed)

        def ternary(w, rows, cols, scale, out_t):
            reduce(dve, scale[:, 0:rows], w[:, :, :], ALU.add, absolute=True)
            dve.wait(dve.mark())
            scalar2(dve, scale[:, 0:rows], scale[:, 0:rows], 1.0 / (cols * P), 1e-5, ALU.mult, ALU.max)
            dve.wait(dve.mark())
            scalar1(dve, upper[:, 0:rows], scale[:, 0:rows], 0.5, ALU.mult)
            scalar1(dve, lower[:, 0:rows], scale[:, 0:rows], -0.5, ALU.mult)
            dve.wait(dve.mark())
            for m in range(rows):
                for n in range(cols):
                    part = w[:, m, n * P:(n + 1) * P]
                    lt, s, b = below.take(), tern.take(), front.take()
                    scalar1(dve, lt.buf[:, :], part, lower[:, m:m + 1], ALU.is_lt)
                    dve.wait(dve.mark(), *s.read)
                    fused(dve, s.buf[:, :], part, upper[:, m:m + 1], lt.buf[:, :], ALU.is_gt, ALU.subtract)
                    pe.wait(dve.mark(), *b.read)
                    transpose(pe, b.buf[:, 0:P], s.buf[:, :], ident[:, :])
                    s.read = (pe.mark(),)
                    act.wait(pe.mark())
                    act_copy(act, out_t[:, n, m * P:(m + 1) * P], b.buf[:, 0:P])
                    b.read = (act.mark(),)

        ternary(fc, HT, KT, scale_fc, fc_t)
        dve.do(lambda e: e.reciprocal(gate_fc[:, :], scale_fc[:, :]))
        dve.wait(dve.mark())
        scalar1(dve, gate_fc[:, :], gate_fc[:, :], gate[:, 0:1], ALU.mult)
        dve.wait(dve.mark())
        tensor2(dve, u[:, :, :], u[:, :, :], spread(gate_fc[:, :], RANK), ALU.mult)
        dve.wait(dve.mark())
        for i in range(COPIES):
            copy(dve, u3[:, :, i * SUB:i * SUB + RANK], u[:, :, :])
        u3_done = dve.mark()
        for m in range(HT):
            b, cols = front.take(), slice(m * P, (m + 1) * P)
            pe.wait(u3_done, *b.read)
            transpose(pe, b.buf[0:ROWS, 0:P], u3[:, m, :], ident[:, :])
            dve.wait(pe.mark())
            copy(dve, u3_t[:, cols], b.buf[0:ROWS, 0:P])
            dve.wait(dve.mark())
            last = slice(ROWS - SUB, ROWS)
            tensor2(dve, u3_t[last, cols], b.buf[last, 0:P], u3_t[last, cols].bitcast(F32), ALU.subtract)
            b.read = (dve.mark(),)
        for kt in range(KT):
            b = front.take()
            pe.wait(*b.read)
            matmul(pe, b.buf[:, 0:RANK], v[:, kt * P:(kt + 1) * P], fast_b[:, :])
            dve.wait(pe.mark())
            for i in range(COPIES):
                copy(dve, low_in[:, kt, i * SUB:i * SUB + RANK], b.buf[:, 0:RANK])
            b.read = (dve.mark(),)
        dve.wait(dve.mark())
        copy(dve, low_hi[:, :, :], low_in[:, :, :])
        dve.wait(dve.mark())
        tensor2(dve, low_lo[:, :, :], low_in[:, :, :], low_hi[:, :, :].bitcast(F32), ALU.subtract)
        ternary(proj, KT, HT, scale_proj, proj_t)
        for kt in range(KT):
            b = front.take()
            dve.wait(*( () if kt == 0 else (pe.mark(),)))
            scalar1(dve, diagonal[:, :], ident[:, :], scale_proj[:, kt:kt + 1], ALU.mult)
            pe.wait(dve.mark(), *b.read)
            matmul(pe, b.buf[:, 0:P], ones[:, :], diagonal[:, :])
            act.wait(pe.mark())
            act_copy(act, scale_row[:, kt * P:(kt + 1) * P], b.buf[:, 0:P])
            b.read = (act.mark(),)
        pe.wait(act.mark(), dve.mark())
        dve.wait(act.mark())

        done = {}
        got = lambda what, c: done.get((what, c), ())
        loads, stores = [lane(f"load{i}") for i in range(X_BUFS)], [lane(f"store{i}") for i in range(X_BUFS)]

        def load_x(c):
            if c < CHUNKS:
                sp.wait(*got("stored", c - X_BUFS))
                done["x", c] = (loads[c % X_BUFS].start(sp, xs[c % X_BUFS][:, :, :],
                                                        token_tiles(x_in)[:, c * CT:(c + 1) * CT, :]),)

        def up(c):
            par, x, x_lo = c % 2, xs[c % X_BUFS], x_lo_bufs[c % 2]
            load_x(c + 2)
            rstd_done = norm.statistics(x, got("x", c))
            dve.wait(rstd_done)
            slots = []
            for i in range(CT):
                s = xn.take()
                dve.wait(*s.read)
                norm.scale(s.buf[:, :], x, i)
                slots.append((s, dve.mark()))
            norm.applied = (dve.mark(),)
            yield
            xh = x_hi.take()
            for kt in range(KT):
                b = front.take()
                pe.wait(*b.read)
                for i, (s, scaled) in enumerate(slots):
                    pe.wait(scaled)
                    transpose(pe, b.buf[:, i * P:(i + 1) * P], s.buf[:, kt * P:(kt + 1) * P], ident[:, :])
                    s.read = (pe.mark(),)
                act.wait(pe.mark(), *xh.read)
                act_copy(act, xh.buf[:, kt, :], b.buf)
                dve.wait(act.mark(), *xh.read)
                tensor2(dve, x_lo[:, kt, :], b.buf, xh.buf[:, kt, :].bitcast(F32), ALU.subtract)
                b.read = (dve.mark(),)
            x_done = dve.mark()
            yield
            b = front.take()
            pe.wait(x_done, *b.read)
            passes = [(kt, w, s) for kt in range(KT) for w, s in ((low_hi, xh.buf), (low_hi, x_lo), (low_lo, xh.buf))]
            for n, (kt, w, s) in enumerate(passes):
                matmul(pe, b.buf[0:ROWS, :], w[:, kt, :], s[:, kt, :], n == 0, n == len(passes) - 1)
            act.wait(pe.mark(), *xh.read)
            act_copy(act, low[:, :], b.buf[0:ROWS, :])
            dve.wait(act.mark())
            tensor2(dve, low[SUB:2 * SUB, :], b.buf[SUB:2 * SUB, :], low[SUB:2 * SUB, :].bitcast(F32), ALU.subtract)
            b.read = (dve.mark(),)
            low_done = dve.mark()
            for m in range(HT):
                b, cols = front.take(), slice(m * P, (m + 1) * P)
                pe.wait(*b.read)
                for kt in range(KT):
                    matmul(pe, b.buf, fc_t[:, kt, cols], xh.buf[:, kt, :], kt == 0, False)
                    matmul(pe, b.buf, fc_t[:, kt, cols], x_lo[:, kt, :], False, False)
                pe.wait(low_done)
                matmul(pe, b.buf, u3_t[:, cols], low[:, :], False, True)
                r, sq = relu.take(), square.take()
                act.wait(pe.mark(), *r.read)
                activation(act, r.buf[:, :], b.buf, ACT.Relu, scale=scale_fc[:, m:m + 1])
                b.read = (act.mark(),)
                act.wait(act.mark(), *sq.read)
                activation(act, sq.buf[:, :], r.buf[:, :], ACT.Square)
                dve.wait(act.mark(), *got("down", c - 2))
                copy(dve, r_hi[par][:, m, :], sq.buf[:, :])
                dve.wait(dve.mark())
                tensor2(dve, r_lo[par][:, m, :], sq.buf[:, :], r_hi[par][:, m, :].bitcast(F32), ALU.subtract)
                sq.read = (dve.mark(),)
                yield
            xh.read = (pe.mark(),)
            done["up", c] = (dve.mark(),)

        def down(c):
            par, x = c % 2, xs[c % X_BUFS]
            pe.wait(*got("up", c))
            for i in range(CT):
                b = back.take()
                pe.wait(*b.read)
                for m in range(HT):
                    for r in (r_hi, r_lo):
                        matmul(pe, b.buf[:, 0:DIM], r[par][:, m, i * P:(i + 1) * P], proj_t[:, m, :],
                               m == 0 and r is r_hi, m == HT - 1 and r is r_lo)
                    if m == HT // 2:
                        yield
                s = scaled_out.take()
                dve.wait(pe.mark(), *s.read)
                tensor2(dve, s.buf[:, :], b.buf[:, 0:DIM], scale_row[:, :], ALU.mult)
                b.read = (dve.mark(),)
                pool.wait(dve.mark())
                tensor2(pool, x[:, i, :], x[:, i, :], s.buf[:, :], ALU.add)
                s.read = (pool.mark(),)
                yield
            done["down", c] = (pe.mark(),)
            sp.wait(pool.mark())
            done["stored", c] = (stores[c % X_BUFS].start(sp, token_tiles(x_out)[:, c * CT:(c + 1) * CT, :], x[:, :, :]),)

        load_x(0)
        load_x(1)
        pipeline = Pipeline()
        for c in range(-1, CHUNKS):
            pipeline.together(("down", down(c)) if c >= 0 else None, ("up", up(c + 1)) if c + 1 < CHUNKS else None)
        for s in stores:
            sp.wait((s.sem, s.count))
        core.run()


def attention(core, x_in, x_out, d):
    nc, pe, act, dve, pool, sp, banks = core.nc, core.pe, core.act, core.dve, core.pool, core.sp, core.banks
    with ExitStack() as ctx:
        sb = lambda n, s, dt=F32: ctx.enter_context(nc.sbuf_tensor("b_" + n, s, dt))
        lane = lambda n: Lane(ctx.enter_context(nc.semaphore("b_" + n)))
        GW = GROUP * HD
        VW = HD + 1
        SLOT = P // GROUP

        ident, ident_b = sb("ident", [P, P]), sb("ident_b", [P, P], BF16)
        first_table = np.cumsum([0] + [len(block_bias(h)) for h in range(HEADS)]).tolist()
        tables = sb("tables", [P, first_table[-1], P], BF16)
        w_qk = sb("w_qk", [P, KT, GROUPS, 2 * GW])
        w_v, w_out = sb("w_v", [P, KT, DIM]), sb("w_out", [P, KT, DIM])
        b_qk, scale_qk = sb("b_qk", [P, GROUPS]), sb("scale_qk", [P, 1])
        b_v, b_out = sb("b_v", [P, DIM]), sb("b_out", [P, DIM])
        SETS = 3
        q_stack = sb("q_stack", [STACK, SETS * GROUP, SEQ], F32R)
        k_stack = sb("k_stack", [STACK, SETS * GROUP, SEQ], F32R)
        X_BUFS = 2
        AHEAD = 1.3
        xs = [sb(f"x{i}", [P, QB, DIM]) for i in range(X_BUFS)]
        xn = Ring([sb(f"xn{i}", [P, DIM]) for i in range(2)])
        xn_ts = [sb(f"xn_t{i}", [P, KT, SEQ]) for i in range(2)]
        qk = Ring([sb("qk", [P, BANK])])
        qk_hi, qk_lo = sb("qk_hi", [P, SEQ], F32R), sb("qk_lo", [P, SEQ], F32R)
        vs = [sb(f"v{i}", [P, QB, HEADS, VW]) for i in range(2)]
        half_max = sb("half_max", [P, GROUP * QB, HALVES])
        row_max = sb("row_max", [P, 2, GROUP * QB])
        shift = sb("shift", [2 * GROUP * QB, P], F32R)
        p_t = Ring([sb(f"p_t{i}", [P, 2, BANK]) for i in range(4)])
        pv = sb("pv", [P, BANK])
        recip = sb("recip", [P, CT * GROUP])
        att = sb("att", [P, QB, DIM])
        att_t = Ring([sb(f"att_t{i}", [P, KT, P]) for i in range(2)])
        shift_dram = [nc.dram_tensor(f"b_shift_dram{i}", (2, GROUP, SEQ), F32R, kind="Internal").ap() for i in range(2)]

        scores = Ring([banks[:, 0:2, :], banks[:, 2:4, :]])
        values = Slot(banks[:, 4, :])
        misc = Ring([banks[:, i, :] for i in (5, 6, 7)])
        norm = Normalizer(core, sb, "norm", QB)

        weights, bias_lane, tables_lane = lane("weights"), lane("bias"), lane("tables")
        k_bias = nc.dram_tensor("b_k_bias", (HEADS, BIASROWS, SEQ), F32R, kind="Internal").ap()
        bias_cast = bias_lane.start(pool, k_bias, d["c_kbias"])
        every_slot = lambda ap: ap.unsqueeze(1).to_broadcast([ap.shape[0], SETS * GROUP, SEQ])
        tables_lane.start(pool, q_stack[MAIN:SHIFTROW, :, :], every_slot(d["c_qrows"]))
        tables_lane.start(pool, k_stack[MAIN + BIASROWS:STACK, :, :], every_slot(d["c_krows"]))
        tables_cast = tables_lane.start(pool, tables[:, :, :], d["c_block"])
        weights.start(sp, ident[:, :], d["c_ident"])
        for kt in range(KT):
            rows = d["Wqkv"][kt * P:(kt + 1) * P, :]
            for part in range(2):
                weights.start(sp, w_qk[:, kt, :, part * GW:(part + 1) * GW],
                              rows[:, part * DIM:(part + 1) * DIM].rearrange("p (g n) -> p g n", g=GROUPS))
            weights.start(sp, w_v[:, kt, :], rows[:, 2 * DIM:3 * DIM])
        weights.start(sp, w_out[:, :, :], d["Wout"].rearrange("(k p) n -> p k n", p=P))
        for g in range(GROUPS):
            for part in range(2):
                lo = part * DIM + g * GW
                weights.start(sp, b_qk[part * GW:(part + 1) * GW, g:g + 1],
                              d["bqkv"][lo:lo + GW].rearrange("(p a) -> p a", a=1))
        weights.start(sp, b_v[:, :], d["bqkv"][2 * DIM:3 * DIM].partition_broadcast(P))
        loaded = weights.start(sp, b_out[:, :], d["bout"].partition_broadcast(P))
        memset(dve, scale_qk[0:GW, :], HD ** -0.5)
        memset(dve, scale_qk[GW:P, :], 1.0)
        for v in vs:
            memset(dve, v[:, :, :, HD:VW], 1.0)
        filled = pool.mark()
        memset(dve, values.buf, 0.0)
        for e in (pe, act, dve, pool):
            e.wait(loaded, filled, dve.mark())
        copy(dve, ident_b[:, :], ident[:, :])
        pe.wait(dve.mark())

        done = {}
        got = lambda what, g: done.get((what, g), ())
        stack_lane = [lane(f"stack{i}") for i in range(SETS)]
        shift_out, shift_in = lane("shift_out"), [lane(f"shift_in{i}") for i in range(2)]

        loads, stores = [lane(f"load{i}") for i in range(X_BUFS)], [lane(f"store{i}") for i in range(X_BUFS)]

        def load_x(b):
            if b < BATCH:
                sp.wait(*got("stored", b - X_BUFS))
                done["x", b] = (loads[b % X_BUFS].start(sp, xs[b % X_BUFS][:, :, :],
                                                        token_tiles(x_in)[:, b * QB:(b + 1) * QB, :]),)

        def add_block_bias(out, h):
            for n in range(first_table[h], first_table[h + 1]):
                matmul(pe, out, ident_b[:, :], tables[:, n, :], False, n == first_table[h + 1] - 1)

        def normalize(b):
            x, xn_t = xs[b % X_BUFS], xn_ts[b % 2]
            rstd_done = norm.statistics(x, got("x", b))
            dve.wait(rstd_done)
            yield
            for i in range(0, QB, 2):
                scaled = []
                for j in range(2):
                    s = xn.take()
                    dve.wait(*s.read)
                    norm.scale(s.buf[:, :], x, i + j)
                    scaled.append((s, dve.mark()))
                yield
                m = misc.take()
                pe.wait(*m.read)
                for j, (s, done_scaling) in enumerate(scaled):
                    pe.wait(done_scaling)
                    for kt in range(KT):
                        at = (kt * 2 + j) * P
                        transpose(pe, m.buf[:, at:at + P], s.buf[:, kt * P:(kt + 1) * P], ident[:, :])
                    s.read = (pe.mark(),)
                act.wait(pe.mark(), *got("projected", b - 2), *got("v_made", b - 2))
                act_copy(act, xn_t[:, :, i * P:(i + 2) * P], m.buf.rearrange("p (k n) -> p k n", k=KT))
                m.read = (act.mark(),)
                yield
            norm.applied = (dve.mark(),)
            done["xn", b] = (act.mark(),)

        def make_values(b):
            xn_t, v = xn_ts[b % 2], vs[b % 2]
            by_head = lambda ap: ap.rearrange("p (h n) -> p h n", n=HD)
            pe.wait(*got("xn", b))
            for i in range(QB):
                m = misc.take()
                pe.wait(*m.read)
                for kt in range(KT):
                    matmul(pe, m.buf[:, 0:DIM], xn_t[:, kt, i * P:(i + 1) * P], w_v[:, kt, :],
                           kt == 0, kt == KT - 1)
                dve.wait(pe.mark(), *got("weighed", (b - 1) * GROUPS - 1))
                tensor2(dve, v[:, i, :, 0:HD], by_head(m.buf[:, 0:DIM]), by_head(b_v[:, :]), ALU.add)
                m.read = (dve.mark(),)
                yield
            done["v_made", b] = (pe.mark(), dve.mark())

        def make_stacks(g):
            b, hg, slot0 = g // GROUPS, g % GROUPS, g % SETS * GROUP
            xn_t = xn_ts[b % 2]
            pe.wait(*got("xn", b))
            for half in range(HALVES):
                m, s, cols = misc.take(), qk.take(), slice(half * BANK, (half + 1) * BANK)
                pe.wait(*m.read)
                for kt in range(KT):
                    matmul(pe, m.buf, w_qk[:, kt, hg, :], xn_t[:, kt, cols], kt == 0, kt == KT - 1)
                dve.wait(pe.mark(), *s.read)
                scalar2(dve, s.buf[:, :], m.buf, b_qk[:, hg:hg + 1], scale_qk[:, 0:1], ALU.add, ALU.mult)
                m.read = (dve.mark(),)
                act.wait(dve.mark(), *got("stacked", g - 1))
                act_copy(act, qk_hi[:, cols], s.buf[:, :])
                pool.wait(act.mark(), *got("stacked", g - 1))
                tensor2(pool, qk_lo[:, cols], s.buf[:, :], qk_hi[:, cols].bitcast(F32), ALU.subtract)
                s.read = (pool.mark(),)
                yield
            done["qk", g] = (pe.mark(),)
            if hg == GROUPS - 1:
                done["projected", b] = (pe.mark(),)
            sp.wait(bias_cast, act.mark(), pool.mark(), *got("scored", g - SETS))
            for i in range(GROUP):
                s, rows_q = slot0 + i, slice(i * HD, (i + 1) * HD)
                rows_k = slice(GW + i * HD, GW + (i + 1) * HD)
                for at, (qpart, kpart) in enumerate(((qk_hi, qk_hi), (qk_hi, qk_lo), (qk_lo, qk_hi))):
                    to = slice(at * HD, (at + 1) * HD)
                    stack_lane[g % SETS].start(sp, words(q_stack[to, s, :]), words(qpart[rows_q, :]))
                    stack_lane[g % SETS].start(sp, words(k_stack[to, s, :]), words(kpart[rows_k, :]))
                stacked = stack_lane[g % SETS].start(sp, words(k_stack[MAIN:MAIN + BIASROWS, s, :]), words(k_bias[hg * GROUP + i]))
            done["stacked", g] = (stacked,)

        def find_maxima(g):
            hg, slot0 = g % GROUPS, g % SETS * GROUP
            pe.wait(tables_cast, *got("stacked", g))
            for i in range(GROUP):
                for qb in range(QB):
                    s = slot0 + i
                    for half in range(HALVES):
                        m = misc.take()
                        pe.wait(*m.read)
                        here = qb // CT == half
                        matmul(pe, m.buf, q_stack[0:SHIFTROW, s, qb * P:(qb + 1) * P],
                               k_stack[0:SHIFTROW, s, half * BANK:(half + 1) * BANK], True, not here)
                        if here:
                            at = qb % CT * P
                            add_block_bias(m.buf[:, at:at + P], hg * GROUP + i)
                        dve.wait(pe.mark(), *got("max", g - 1))
                        reduce(dve, half_max[:, i * QB + qb, half:half + 1], m.buf, ALU.max, negate=True)
                        m.read = (dve.mark(),)
                    yield
            dve.wait(dve.mark(), *got("turned", g - 1))
            reduce(dve, row_max[:, 0, :], half_max[:, :, :], ALU.min)
            done["max", g] = (dve.mark(),)
            dve.wait(dve.mark())
            copy(dve, row_max[:, 1, :], row_max[:, 0, :])
            m = misc.take()
            pe.wait(dve.mark(), *m.read)
            rows = 2 * GROUP * QB
            transpose(pe, m.buf[0:rows, 0:P], row_max[:, :, :].rearrange("p a n -> p (a n)"), ident[:, :])
            done["turned", g] = (pe.mark(),)
            act.wait(pe.mark(), *got("shift_out", g - 1))
            act_copy(act, shift[:, :], m.buf[0:rows, 0:P])
            dve.wait(act.mark())
            lo = slice(rows // 2, rows)
            tensor2(dve, shift[lo, :], m.buf[lo, 0:P], shift[lo, :].bitcast(F32), ALU.subtract)
            m.read = (dve.mark(),)
            sp.wait(dve.mark(), *got("shift_in", g - 2))
            out = shift_out.start(sp, words(shift_dram[g % 2].rearrange("a h (b n) -> (a h b) n", n=P)), words(shift[:, :]))
            done["shift_out", g] = (out,)
            sp.wait(out)
            done["shift_in", g] = (shift_in[g % 2].start(sp, words(q_stack[SHIFTROW:STACK, slot0:slot0 + GROUP, :]), words(shift_dram[g % 2])),)

        weighing, tails = [], []

        def weigh():
            g, half, kb, made = weighing.pop(0)
            hg, v = g % GROUPS, vs[g // GROUPS % 2]
            if kb == 0:
                pe.wait(*values.read)
            pe.wait(*(exponentials for _, exponentials in made))
            for i in range(GROUP):
                slot = made[i // 2][0]
                matmul(pe, values.buf[i * SLOT:i * SLOT + VW, :], v[:, kb, hg * GROUP + i, :],
                       slot.buf[:, i % 2, :], kb == 0, kb == QB - 1, tile=(0, i * SLOT))
            for slot, _ in made:
                slot.read = (pe.mark(),)
            if kb == QB - 1:
                done["weighed", g] = (pe.mark(),)
                act.wait(pe.mark(), *got("pv_read", 0))
                act_copy(act, pv[:, :], values.buf)
                values.read = (act.mark(),)
                tails.append(conclude(g, half, act.mark()))

        def advance_tail():
            if tails and next(tails[0], tails) is tails:
                tails.pop(0)

        def conclude(g, half, copied):
            b, hg = g // GROUPS, g % GROUPS
            m = misc.take()
            pe.wait(copied, *m.read)
            for i in range(CT):
                transpose(pe, m.buf[:, i * P:(i + 1) * P], pv[:, i * P:(i + 1) * P], ident[:, :])
            done["pv_read", 0] = (pe.mark(),)
            slots = m.buf.rearrange("p (t h n) -> p t h n", t=CT, h=GROUP)
            dve.wait(pe.mark(), *got("att_read", b - 1), *got("normalized", 0))
            dve.do(lambda e: e.reciprocal(recip[:, :].rearrange("p (t h) -> p t h", t=CT), slots[:, :, :, HD]))
            dve.wait(dve.mark())
            tensor2(dve, att[:, half * CT:(half + 1) * CT, hg * GW:(hg + 1) * GW].rearrange("p t (h n) -> p t h n", n=HD),
                    slots[:, :, :, 0:HD], spread(recip[:, :].rearrange("p (t h) -> p t h", t=CT), HD), ALU.mult)
            m.read = done["normalized", 0] = (dve.mark(),)
            yield
            if (hg, half) != (GROUPS - 1, HALVES - 1):
                return
            pe.wait(*done["normalized", 0])
            turned = []
            for i in range(QB + 1):
                if i < QB:
                    m, t = misc.take(), att_t.take()
                    pe.wait(*m.read)
                    for kt in range(KT):
                        transpose(pe, m.buf[:, kt * P:(kt + 1) * P], att[:, i, kt * P:(kt + 1) * P], ident[:, :])
                    act.wait(pe.mark(), *t.read)
                    act_copy(act, t.buf[:, :, :], m.buf[:, 0:DIM].rearrange("p (k n) -> p k n", k=KT))
                    m.read = (act.mark(),)
                    done["att_read", b] = (pe.mark(),)
                    turned.append((t, act.mark()))
                    if i == 0:
                        continue
                t, copied = turned[i - 1]
                m = misc.take()
                pe.wait(copied, *m.read)
                for kt in range(KT):
                    matmul(pe, m.buf[:, 0:DIM], t.buf[:, kt, :], w_out[:, kt, :], kt == 0, kt == KT - 1)
                t.read = (pe.mark(),)
                tile = xs[b % X_BUFS][:, i - 1, :]
                dve.wait(pe.mark())
                tensor2(dve, tile, tile, m.buf[:, 0:DIM], ALU.add)
                m.read = (dve.mark(),)
                pool.wait(dve.mark())
                tensor2(pool, tile, tile, b_out[:, :], ALU.add)
                yield
            sp.wait(pool.mark())
            done["stored", b] = (stores[b % X_BUFS].start(sp, token_tiles(x_out)[:, b * QB:(b + 1) * QB, :],
                                                          xs[b % X_BUFS][:, :, :]),)
            load_x(b + 2)

        def attend(g):
            b, hg, slot0 = g // GROUPS, g % GROUPS, g % SETS * GROUP
            pe.wait(*got("shift_in", g), *got("v_made", b))
            for half in range(HALVES):
                qcols = slice(half * BANK, (half + 1) * BANK)
                for kb in range(QB):
                    made = []
                    for pair in range(GROUP // 2):
                        sc = scores.take()
                        pe.wait(*sc.read)
                        for j in range(2):
                            i = pair * 2 + j
                            here = kb // CT == half
                            matmul(pe, sc.buf[:, j, :], k_stack[0:STACK, slot0 + i, kb * P:(kb + 1) * P],
                                   q_stack[0:STACK, slot0 + i, qcols], True, not here)
                            if here:
                                at = kb % CT * P
                                add_block_bias(sc.buf[:, j, at:at + P], hg * GROUP + i)
                        s = p_t.take()
                        act.wait(pe.mark(), *s.read)
                        activation(act, s.buf[:, :, :], sc.buf, ACT.Exp)
                        sc.read = (act.mark(),)
                        made.append((s, act.mark()))
                        if pair == 0:
                            yield
                    if weighing:
                        weigh()
                    weighing.append((g, half, kb, made))
                    yield
                    advance_tail()
            done["scored", g] = (pe.mark(),)

        load_x(0)
        load_x(1)
        groups = BATCH * GROUPS
        pipeline = Pipeline()
        for g in range(1 - GROUPS, groups):
            b, last = (g - 1) // GROUPS + 1, g % GROUPS == GROUPS - 1
            pipeline.together(
                ("attend", attend(g)) if g >= 0 else None,
                ("maxima", find_maxima(g + 1), AHEAD) if 0 <= g + 1 < groups else None,
                ("stacks", make_stacks(g + 2), 3 * AHEAD) if 0 <= g + 2 < groups else None,
                ("values", make_values(b)) if last and b < BATCH else None,
                ("normalize", normalize(b)) if g % GROUPS == 1 and b < BATCH else None)
        weigh()
        while tails:
            advance_tail()
        for s in stores:
            sp.wait((s.sem, s.count))
        core.run()


def build(nc, d, out):
    with ExitStack() as ctx:
        core = Core(nc, ctx)
        between = [nc.dram_tensor(f"x{i}", (BATCH, SEQ, DIM), F32, kind="Internal").ap() for i in range(3)]
        recurrent_mixer(core, d["hidden_states"], between[0], d)
        feed_forward(core, between[0], between[1], d, "ffn1")
        attention(core, between[1], between[2], d)
        feed_forward(core, between[2], out, d, "ffn2")


BY_PARTITION = ("mu_x", "x_bias")
TRANSPOSED = ("W_x1", "W_x2", "W_r", "W_k", "W_v", "W_g", "A_w", "B_w", "W_o", "fast_b")


def lay_out(name, a):
    a = np.asarray(a)
    if name in TRANSPOSED:
        a = a.T
    if name in BY_PARTITION:
        a = np.moveaxis(a.reshape(a.shape[:-1] + (-1, P)), -1, 0)
    return np.ascontiguousarray(a.reshape(1, 1) if a.ndim == 0 else a)


def kernel(**inputs):
    import concourse.bacc as bacc
    from concourse.bass_utils import run_bass_kernel_spmd

    nc = bacc.Bacc("TRN2", target_bir_lowering=False, num_devices=1)
    arrays, d = {}, {}
    for name, a in list(inputs.items()) + list(constants().items()):
        short = name.replace("L0_attn_a_", "").replace("L0_attn_b_", "").replace("L0_ffn_", "")
        a = lay_out(short, a)
        arrays[short] = a
        d[short] = nc.dram_tensor(short, a.shape, mybir.dt.from_np(a.dtype), kind="ExternalInput").ap()
    out = nc.dram_tensor("out", (BATCH, SEQ, DIM), F32, kind="ExternalOutput").ap()
    build(nc, d, out)
    return run_bass_kernel_spmd(nc, [arrays], core_ids=[0]).results[0]["out"]
```

```python
import math
from contextlib import ExitStack

import numpy as np
from concourse import mybir

F32 = mybir.dt.float32
BF16 = mybir.dt.bfloat16
F32R = mybir.dt.float32r
ALU = mybir.AluOpType
ACT = mybir.ActivationFunctionType
AX = mybir.AxisListType

P = 128
BATCH, SEQ, DIM = 8, 1024, 256
KT = DIM // P
TOKENS = BATCH * SEQ
TILES = TOKENS // P
BANK = 512
CHUNK = BANK
CT = CHUNK // P
CHUNKS = TOKENS // CHUNK
EPS = 1e-5

HEADS_A, KD, VD, LOWRANK, GATERANK, MIXES = 4, 128, 256, 32, 64, 5
HK, HV = KD // HEADS_A, VD // HEADS_A
SUB = 32
DIAG = 5
TREE = 7

HIDDEN, RANK = 1024, 16
HT = HIDDEN // P

HEADS, HD, GROUP = 16, 16, 4
GROUPS = HEADS // GROUP
QB = SEQ // P
HALVES = SEQ // BANK
MAIN = 3 * HD
BIASROWS = 2 * QB
SHIFTROW = 96
STACK = SHIFTROW + 2


def slopes():
    start = 2 ** (-2 ** (-(math.log2(HEADS) - 3)))
    mantissa, exponent = np.frexp(np.asarray([start ** i for i in range(HEADS)], dtype=np.float32))
    return [(2 * float(m), 2.0 ** (int(e) - 1)) for m, e in zip(mantissa, exponent)]


def constants():
    c = {"c_ident": np.eye(P, dtype=np.float32)}
    s, t = np.arange(P)[:, None] % SUB, np.arange(SUB)[None, :]
    parts = []
    for level in range(DIAG):
        m = 1 << level
        parts.append((s // (2 * m) == t // (2 * m)) & (s // m % 2 == 0) & (t // m % 2 == 1))
    parts[0] |= s == t
    c["c_mask"] = np.stack(parts, 1).astype(np.float32).reshape(P, DIAG * SUB)
    q, power = np.arange(SEQ), np.asarray([power for _, power in slopes()])[:, None, None]
    picked = (q[None, :] // P == np.arange(QB)[:, None]).astype(np.float32)
    i, j = np.arange(QB)[:, None], q[None, :] // P
    sign, near = np.sign(i - j), np.arange(P)
    free = SHIFTROW - MAIN - BIASROWS
    c["c_qrows"] = np.concatenate([picked * (q % P), picked, np.zeros((free, SEQ))])
    c["c_krows"] = np.repeat([0.0, 1.0], [free, STACK - SHIFTROW])[:, None].repeat(SEQ, 1)
    c["c_kbias"] = np.concatenate([-power * sign, power * (sign * (q % P) - P * np.abs(i - j))], 1)
    c["c_block"] = -power[:, :, 0] * np.abs(near[:, None, None] - near)
    c["c_qkscale"] = np.concatenate([np.repeat([HD ** -0.5 / unit for unit, _ in slopes()[:GROUP]], HD),
                                     np.ones(GROUP * HD)])[:, None]
    c = {k: v.astype(np.float32) for k, v in c.items()}
    return {k: np.ascontiguousarray(v) for k, v in c.items()}


class Queue:

    def __init__(self, sem):
        self.sem, self.items, self.count, self.reached = sem, [], 0, {}

    def do(self, issue):
        self.items.append([issue, None, 0])

    def wait(self, *tokens):
        for sem, value in tokens:
            if self.reached.get(sem.name, 0) < value:
                self.reached[sem.name] = value
                self.items.append([None, sem, value])

    def mark(self):
        last = self.items[-1]
        if last[1] is None:
            self.count += 1
            last[1], last[2] = self.sem, 1
            self.marked = (self.sem, self.count)
        return self.marked

    def emit(self, engine):
        for issue, sem, value in self.items:
            if issue is None:
                engine.wait_ge(sem, value)
            elif sem is None:
                issue(engine)
            else:
                issue(engine).then_inc(sem, value)
        self.items = []


class Lane:

    def __init__(self, sem):
        self.sem, self.count = sem, 0

    def start(self, queue, out, in_):
        self.count += 16
        queue.items.append([lambda e: e.dma_start(out, in_), self.sem, 16])
        return (self.sem, self.count)


class Slot:

    def __init__(self, buf):
        self.buf, self.read = buf, ()


class Ring:
    def __init__(self, bufs):
        self.slots, self.n = [Slot(b) for b in bufs], 0

    def take(self):
        self.n += 1
        return self.slots[(self.n - 1) % len(self.slots)]


def matmul(pe, out, lhsT, rhs, start=True, stop=True, tile=None):
    if tile is None:
        pe.do(lambda e: e.matmul(out, lhsT, rhs, start=start, stop=stop))
    else:
        pe.do(lambda e: e.matmul(out, lhsT, rhs, start=start, stop=stop, tile_position=tile))


def transpose(pe, out, in_, ident):
    pe.do(lambda e: e.transpose(out, in_, ident))


def activation(act, out, in_, func, bias=0.0, scale=1.0):
    act.do(lambda e: e.activation(out, in_, func, bias=bias, scale=scale))


def copy(q, out, in_):
    q.do(lambda e: e.tensor_copy(out, in_))


def act_copy(act, out, in_):
    act.do(lambda e: e.activation(out, in_, ACT.Copy))


def tensor2(q, out, a, b, op):
    q.do(lambda e: e.tensor_tensor(out, a, b, op))


def scalar2(q, out, in_, s1, s2, op0, op1):
    q.do(lambda e: e.tensor_scalar(out, in_, s1, s2, op0, op1))


def scalar1(q, out, in_, s1, op0):
    q.do(lambda e: e.tensor_scalar(out, in_, s1, None, op0))


def fused(dve, out, in0, scalar, in1, op0, op1):
    dve.do(lambda e: e.scalar_tensor_tensor(out=out, in0=in0, scalar=scalar, in1=in1, op0=op0, op1=op1))


def reduce(dve, out, in_, op, negate=False, absolute=False):
    dve.do(lambda e: e.tensor_reduce(out, in_, axis=AX.X, op=op, negate=negate, apply_absolute_value=absolute))


def memset(q, out, value):
    q.do(lambda e: e.memset(out, value))


def spread(ap, n):
    return ap.unsqueeze(len(ap.shape)).to_broadcast(list(ap.shape) + [n])


def token_tiles(dram):
    return dram.rearrange("b (t p) c -> p (b t) c", p=P)


def words(ap):
    return ap.bitcast(F32)


class Pipeline:

    def __init__(self):
        self.steps = {}

    def together(self, *stages):
        running = [[s[0], s[1], 0, s[2] if len(s) > 2 else 1.0] for s in stages if s is not None]
        while running:
            stage = min(running, key=lambda r: (r[2] + 0.5) / (self.steps.get(r[0], 16) * r[3]))
            if next(stage[1], running) is running:
                self.steps[stage[0]] = max(stage[2], 1)
                running.remove(stage)
            stage[2] += 1


class Core:
    def __init__(self, nc, ctx):
        self.nc = nc
        sem = lambda n: ctx.enter_context(nc.semaphore(n))
        self.pe, self.act, self.dve = Queue(sem("pe_done")), Queue(sem("act_done")), Queue(sem("dve_done"))
        self.pool, self.sp = Queue(sem("pool_done")), Queue(sem("sp_done"))
        self.banks = ctx.enter_context(nc.psum_tensor("banks", [P, 8, BANK], F32))

    def run(self):
        with self.nc.Block() as block:
            block.sync(self.sp.emit)
            block.tensor(self.pe.emit)
            block.scalar(self.act.emit)
            block.vector(self.dve.emit)
            block.gpsimd(self.pool.emit)


class Normalizer:

    def __init__(self, core, sb, name, tiles):
        self.core, self.tiles = core, tiles
        self.stats = sb(f"{name}_stats", [P, tiles, 6])
        self.mean_var = sb(f"{name}_mean_var", [P, tiles, 2])
        self.rstd = sb(f"{name}_rstd", [P, tiles])
        self.minus_half = sb(f"{name}_minus_half", [P, tiles])
        memset(core.pool, self.minus_half[:, :], -0.5)
        self.ready = core.pool.mark()
        self.applied = ()

    def statistics(self, x, arrived):
        dve, pool = self.core.dve, self.core.pool
        dve.wait(*arrived, *self.applied)
        for i in range(self.tiles):
            dve.do(lambda e, i=i: e.bn_stats(self.stats[:, i, :], x[:, i, :]))
        dve.wait(dve.mark())
        for i in range(self.tiles):
            dve.do(lambda e, i=i: e.bn_aggr(self.mean_var[:, i, :], self.stats[:, i, :]))
        pool.wait(self.ready, dve.mark())
        scalar1(pool, self.rstd[:, :], self.mean_var[:, :, 1], EPS, ALU.add)
        pool.wait(pool.mark())
        tensor2(pool, self.rstd[:, :], self.rstd[:, :], self.minus_half[:, :], ALU.pow)
        return pool.mark()

    def scale(self, out, x, i):
        scalar2(self.core.dve, out, x[:, i, :], self.mean_var[:, i, 0:1], self.rstd[:, i:i + 1],
                ALU.subtract, ALU.mult)


def recurrent_mixer(core, x_in, x_out, d):
    nc, pe, act, dve, pool, sp, banks = core.nc, core.pe, core.act, core.dve, core.pool, core.sp, core.banks
    with ExitStack() as ctx:
        sb = lambda n, s, dt=F32: ctx.enter_context(nc.sbuf_tensor("a_" + n, s, dt))
        lane = lambda n: Lane(ctx.enter_context(nc.semaphore("a_" + n)))
        C2 = 2 * SUB
        X_BUFS = 5

        ident, mask = sb("ident", [P, P]), sb("mask", [P, DIAG * SUB])
        mu_x, x_bias = sb("mu_x", [P, KT]), sb("x_bias", [P, MIXES, KT])
        w_x1 = sb("w_x1", [P, KT, 2 * P])
        w_x2 = sb("w_x2", [P, MIXES, DIM])
        w_r, w_k = sb("w_r", [P, KT, KD]), sb("w_k", [P, KT, KD])
        w_v, w_g, w_o = sb("w_v", [P, KT, VD]), sb("w_g", [P, KT, VD]), sb("w_o", [P, KT, DIM])
        w_a, w_b = sb("w_a", [P, KT, GATERANK]), sb("w_b", [GATERANK, KD])
        b_w, bonus = sb("b_w", [P, 1]), sb("bonus", [P, 1])
        gn_w, gn_b = sb("gn_w", [P, VD]), sb("gn_b", [P, VD])

        xs = [sb(f"x{i}", [P, CT, DIM]) for i in range(X_BUFS)]
        xn = Ring([sb(f"xn{i}", [P, DIM]) for i in range(4)])
        xn_t = [sb(f"xn_t{i}", [P, KT, 1 + CHUNK]) for i in range(2)]
        deltas = [sb(f"delta{i}", [P, KT, CHUNK]) for i in range(2)]
        zs = [sb(f"z{i}", [P, 2, CHUNK]) for i in range(2)]
        mixed_x = sb("mixed_x", [P, KT, CHUNK])
        mix = Ring([sb(f"mix{i}", [P, KT, CHUNK]) for i in range(3)])
        gate_low = sb("gate_low", [GATERANK, CHUNK])
        decay = [sb(f"decay{i}", [P, 2 * CHUNK]) for i in range(2)]
        q = [sb(f"q{i}", [P, CHUNK]) for i in range(2)]
        k = [sb(f"k{i}", [P, CHUNK]) for i in range(2)]
        q_up = [[q[i]] + [sb(f"q_up{i}_{l}", [P, CHUNK]) for l in range(1, TREE + 1)] for i in range(2)]
        k_up = [[k[i]] + [sb(f"k_up{i}_{l}", [P, CHUNK]) for l in range(1, TREE + 1)] for i in range(2)]
        q_near = [sb(f"q_near{i}", [P, CHUNK]) for i in range(2)]
        k_near = [sb(f"k_near{i}", [P, CHUNK]) for i in range(2)]
        offset = np.cumsum([0] + [CHUNK >> l for l in range(TREE + 1)]).tolist()
        totals = [[decay[i][:, offset[l]:offset[l + 1]] for l in range(TREE + 1)] for i in range(2)]
        v = [sb(f"v{i}", [P, CT, VD]) for i in range(2)]
        gate = [sb(f"gate{i}", [P, CT, VD]) for i in range(3)]
        masked = sb("masked", [P, HEADS_A, DIAG * SUB])
        diag = sb("diag", [P, HEADS_A, SUB])
        pair = Ring([sb(f"pair{i}", [P, HEADS_A, P]) for i in range(2)])
        k_tok = Ring([sb(f"k_tok{i}", [P, P]) for i in range(2)])
        state = [sb(f"state{i}", [P, VD]) for i in range(2)]
        o_bufs = [sb(f"o{i}", [P, CT, VD]) for i in range(2)]
        o_t = sb("o_t", [P, KT, CHUNK])
        o_sq = o_t[:, :, :].rearrange("p k (a n) -> p (k a) n", n=VD)
        sums, rstd, half = sb("sums", [P, CT * HEADS_A]), sb("rstd", [P, CT * HEADS_A]), sb("half", [P, CT * HEADS_A])

        weights = lane("weights")
        loads, stores = [lane(f"load{i}") for i in range(X_BUFS)], [lane(f"store{i}") for i in range(X_BUFS)]
        for w in (w_x1, w_x2):
            memset(pool, w[:], 0.0)
        sp.wait(pool.mark())
        tiled = lambda ap: ap.rearrange("(k p) n -> p k n", p=P)
        column = lambda ap: ap.rearrange("(p a) -> p a", a=1)
        done = {}
        got = lambda what, c: done.get((what, c), ())

        def load_x(c):
            if c < CHUNKS:
                sp.wait(*got("stored", c - X_BUFS))
                done["x", c] = (loads[c % X_BUFS].start(sp, xs[c % X_BUFS][:, :, :],
                                                        token_tiles(x_in)[:, c * CT:(c + 1) * CT, :]),)

        load_x(0)
        weights.start(sp, ident[:, :], d["c_ident"])
        weights.start(sp, mu_x[:, :], d["mu_x"])
        weights.start(sp, w_x1[:, :, 0:MIXES * LOWRANK], tiled(d["W_x1"]))
        for n in range(MIXES):
            r = n * LOWRANK % P
            weights.start(sp, w_x2[r:r + LOWRANK, n, :], d["W_x2"][n * LOWRANK:(n + 1) * LOWRANK, :])
        weights.start(sp, x_bias[:, :, :], d["x_bias"])
        for t, name in ((w_r, "W_r"), (w_k, "W_k"), (w_v, "W_v"), (w_g, "W_g"), (w_o, "W_o"), (w_a, "A_w")):
            weights.start(sp, t[:, :, :], tiled(d[name]))
        weights.start(sp, w_b[:, :], d["B_w"])
        weights.start(sp, b_w[:, :], column(d["b_w"]))
        weights.start(sp, bonus[:, :], column(d["bonus"].rearrange("h k -> (h k)")))
        weights.start(sp, mask[:, :], d["c_mask"])
        weights.start(sp, gn_w[:, :], d["gn_weight"].partition_broadcast(P))
        loaded = weights.start(sp, gn_b[:, :], d["gn_bias"].partition_broadcast(P))
        for s in pair.slots:
            memset(pool, s.buf[:], 0.0)
        for s in state:
            memset(pool, s[:, :], 0.0)
        memset(pool, half[:, :], -0.5)
        zeroed = pool.mark()
        norm = Normalizer(core, sb, "norm", CT)
        for e in (pe, act, dve, pool):
            e.wait(loaded, zeroed)

        bank = lambda i: banks[:, i, :]
        front, back = Ring([bank(0), bank(1)]), Ring([bank(2), bank(3)])
        products = Slot(banks[:, 4:8, :])

        def normalize(c):
            par, x = c % 2, xs[c % X_BUFS]
            xt, delta, z = xn_t[par], deltas[par], zs[par]
            load_x(c + 1)
            rstd_done = norm.statistics(x, got("x", c))
            yield
            dve.wait(rstd_done)
            slots = []
            for i in range(CT):
                s = xn.take()
                dve.wait(*s.read)
                norm.scale(s.buf[:, :], x, i)
                slots.append((s, dve.mark()))
            norm.applied = (dve.mark(),)
            yield
            for kt in range(KT):
                b = front.take()
                pe.wait(*b.read)
                for i, (s, scaled) in enumerate(slots):
                    pe.wait(scaled)
                    transpose(pe, b.buf[:, i * P:(i + 1) * P], s.buf[:, kt * P:(kt + 1) * P], ident[:, :])
                    s.read = (pe.mark(),)
                act.wait(pe.mark(), *got("mixed", c - 2), *got("carried", c - 1))
                act_copy(act, xt[:, kt, 1:], b.buf)
                b.read = (act.mark(),)
                if kt == 0:
                    yield
            xt_done = act.mark()
            if c % (SEQ // CHUNK) == 0:
                pool.wait(*got("mixed", c - 2))
                memset(pool, xt[:, :, 0:1], 0.0)
            else:
                pool.wait(*got("xt", c - 1), *got("mixed", c - 2))
                copy(pool, xt[:, :, 0:1], xn_t[1 - par][:, :, CHUNK:CHUNK + 1])
            carried = pool.mark()
            done["carried", c], done["xt", c] = (carried,), (xt_done,)
            yield
            dve.wait(xt_done, carried, *got("mixed", c - 2))
            tensor2(dve, delta[:, :, :], xt[:, :, 0:CHUNK], xt[:, :, 1:], ALU.subtract)
            dve.wait(dve.mark(), *got("z", c - 1))
            for kt in range(KT):
                fused(dve, mixed_x[:, kt, :], delta[:, kt, :], mu_x[:, kt:kt + 1], xt[:, kt, 1:], ALU.mult, ALU.add)
            mixed_done = dve.mark()
            yield
            for m in range(2):
                b = front.take()
                pe.wait(mixed_done, *b.read)
                for kt in range(KT):
                    matmul(pe, b.buf, w_x1[:, kt, m * P:(m + 1) * P], mixed_x[:, kt, :], kt == 0, kt == KT - 1)
                act.wait(pe.mark(), *got("mus", c - 2))
                activation(act, z[:, m, :], b.buf, ACT.Tanh)
                b.read = (act.mark(),)
                yield
            done["z", c] = (pe.mark(), act.mark())

        def prepare(c):
            par = c % 2
            xt, delta, z, q0, k0, dec = xn_t[par], deltas[par], zs[par], q[par], k[par], decay[par]
            pe.wait(*got("z", c))

            def mix_in(n):
                s = mix.take()
                for kt in range(KT):
                    b = front.take()
                    pe.wait(*b.read)
                    matmul(pe, b.buf, w_x2[:, n, kt * P:(kt + 1) * P], z[:, n * LOWRANK // P, :])
                    dve.wait(pe.mark(), *s.read)
                    fused(dve, s.buf[:, kt, :], b.buf, x_bias[:, n, kt:kt + 1], delta[:, kt, :], ALU.add, ALU.mult)
                    b.read = (dve.mark(),)
                dve.wait(dve.mark())
                tensor2(dve, s.buf[:, :, :], s.buf[:, :, :], xt[:, :, 1:], ALU.add)
                return s, dve.mark()

            def project(w, s, mixed, rows=P):
                b = front.take()
                pe.wait(mixed, *b.read)
                for kt in range(KT):
                    matmul(pe, b.buf[0:rows, :], w[:, kt, :], s.buf[:, kt, :], kt == 0, kt == KT - 1)
                s.read = (pe.mark(),)
                return b, pe.mark()

            def feature_major(s, mixed, w, t, what):
                b, projected = project(w, s, mixed)
                act.wait(projected, *got("recurred", c - 2))
                act_copy(act, t[:, :], b.buf)
                b.read = (act.mark(),)
                done[what, c] = (act.mark(),)

            def token_major(s, mixed, w, take):
                for at in range(0, CT, 2):
                    b = front.take()
                    pe.wait(mixed, *b.read)
                    for i in range(2):
                        tok = (at + i) * P
                        for kt in range(KT):
                            matmul(pe, b.buf[:, i * VD:(i + 1) * VD], s.buf[:, kt, tok:tok + P], w[:, kt, :],
                                   kt == 0, kt == KT - 1)
                    s.read = (pe.mark(),)
                    b.read = take(slice(at, at + 2), b.buf.rearrange("p (t n) -> p t n", t=2))
                    yield

            def take_values(two, bank2):
                act.wait(pe.mark(), *got("recurred", c - 2))
                act_copy(act, v[par][:, two, :], bank2)
                return (act.mark(),)

            def take_gate(two, bank2):
                out = gate[c % 3][:, two, :]
                act.wait(pe.mark(), *got("gate_read", c - 3))
                activation(act, out, bank2, ACT.Tanh, scale=0.5)
                dve.wait(act.mark())
                fused(dve, out, out, 1.0, bank2, ALU.add, ALU.mult)
                return (dve.mark(),)

            mixed_w = mix_in(1)
            yield
            mixed_q = mix_in(0)
            yield
            b, projected = project(w_a, *mixed_w, GATERANK)
            act.wait(projected, *got("w", c - 1))
            activation(act, gate_low[:, :], b.buf[0:GATERANK, :], ACT.Tanh)
            b.read, low_done = (act.mark(),), act.mark()
            mixed_k = mix_in(2)
            yield
            b = front.take()
            pe.wait(low_done, *b.read)
            matmul(pe, b.buf, w_b[:, :], gate_low[:, :])
            done["w", c] = (pe.mark(),)
            act.wait(pe.mark(), *got("recurred", c - 2))
            activation(act, dec[:, 0:CHUNK], b.buf, ACT.Exp, bias=b_w[:, 0:1])
            b.read = (act.mark(),)
            act.wait(act.mark())
            activation(act, dec[:, 0:CHUNK], dec[:, 0:CHUNK], ACT.Exp, scale=-1.0)
            done["decay", c] = (act.mark(),)
            feature_major(*mixed_q, w_r, q0, "q")
            mixed_v = mix_in(3)
            yield
            feature_major(*mixed_k, w_k, k0, "k")
            mixed_g = mix_in(4)
            done["mus", c] = (pe.mark(),)
            yield
            levels = carry(c)
            for _ in token_major(*mixed_v, w_v, take_values):
                next(levels)
                yield
            done["v", c] = (act.mark(),)
            for _ in token_major(*mixed_g, w_g, take_gate):
                next(levels)
                yield
            done["gated", c] = done["mixed", c] = (dve.mark(),)
            yield from levels

        def carry(c):
            qs, ks, tots = q_up[c % 2], k_up[c % 2], totals[c % 2]
            ready = got("k", c) + got("q", c) + got("decay", c) + got("recurred", c - 2)
            for e in (dve, act, pool):
                e.wait(*ready)
            for l in range(TREE):
                blocks = lambda ap: ap.rearrange("p (n two m) -> p n two m", two=2, m=1 << l)
                tot = tots[l].rearrange("p (n two) -> p n two", two=2)
                tensor2(dve, blocks(qs[l + 1][:, :])[:, :, 1, :], blocks(qs[l][:, :])[:, :, 1, :],
                        spread(tot[:, :, 0], 1 << l), ALU.mult)
                tensor2(dve, tots[l + 1], tot[:, :, 0], tot[:, :, 1], ALU.mult)
                stepped = dve.mark()
                tensor2(pool, blocks(ks[l + 1][:, :])[:, :, 0, :], blocks(ks[l][:, :])[:, :, 0, :],
                        spread(tot[:, :, 1], 1 << l), ALU.mult)
                key = pool.mark()
                act_copy(act, blocks(qs[l + 1][:, :])[:, :, 0, :], blocks(qs[l][:, :])[:, :, 0, :])
                act_copy(act, blocks(ks[l + 1][:, :])[:, :, 1, :], blocks(ks[l][:, :])[:, :, 1, :])
                kept = act.mark()
                if l == TREE // 2:
                    turns = lambda ap, i: ap.rearrange("p (n two) -> p n two", two=2)[:, :, i]
                    for near, plain, scaled in ((q_near, qs[0], 0), (k_near, ks[0], 1)):
                        scalar1(pool, turns(near[c % 2][:, :], scaled), turns(plain[:, :], scaled), bonus[:, 0:1], ALU.mult)
                        act_copy(act, turns(near[c % 2][:, :], 1 - scaled), turns(plain[:, :], 1 - scaled))
                yield
                dve.wait(kept, stepped)
                pool.wait(kept, stepped, key)
                act.wait(stepped, key, kept)
            done["carried_up", c] = (stepped, key, kept)

        def recur(c):
            par, o = c % 2, o_bufs[c % 2]
            qs, ks = q_up[par], k_up[par]
            pe.wait(*got("carried_up", c), *got("v", c))

            def pair_products(i):
                tok = i * P
                pe.wait(*products.read)
                for part in range(DIAG):
                    kk, qq = (k_near[par], q_near[par]) if part == 0 else (ks[part], qs[part])
                    for j in range(P // SUB):
                        t0 = tok + j * SUB
                        for h in range(HEADS_A):
                            r = h * HK
                            matmul(pe, products.buf[j * SUB:(j + 1) * SUB, h, part * SUB:(part + 1) * SUB],
                                   kk[r:r + HK, t0:t0 + SUB], qq[r:r + HK, t0:t0 + SUB], tile=(r, j * SUB))
                off = DIAG * SUB
                for j in (0, 2):
                    t0 = tok + j * SUB
                    for h in range(HEADS_A):
                        r = h * HK
                        matmul(pe, products.buf[j * SUB:(j + 1) * SUB, h, off:off + SUB],
                               ks[5][r:r + HK, t0:t0 + SUB], qs[5][r:r + HK, t0 + SUB:t0 + C2], tile=(r, j * SUB))
                for h in range(HEADS_A):
                    r = h * HK
                    matmul(pe, products.buf[0:C2, h, off + SUB:off + SUB + C2],
                           ks[6][r:r + HK, tok:tok + C2], qs[6][r:r + HK, tok + C2:tok + P], tile=(r, 0))
                multiplied = pe.mark()
                b = back.take()
                pe.wait(*b.read)
                transpose(pe, b.buf[:, 0:P], ks[TREE][:, tok:tok + P], ident[:, :])
                turned, keys, s = pe.mark(), k_tok.take(), pair.take()
                dve.wait(multiplied, *got("summed", 0))
                tensor2(dve, masked[:, :, :], products.buf[:, :, 0:off],
                        mask[:, :].unsqueeze(1).to_broadcast([P, HEADS_A, off]), ALU.mult)
                act.wait(multiplied, dve.mark(), *s.read)
                act_copy(act, s.buf[0:SUB, :, SUB:C2], products.buf[0:SUB, :, off:off + SUB])
                act_copy(act, s.buf[C2:C2 + SUB, :, C2 + SUB:P], products.buf[C2:C2 + SUB, :, off:off + SUB])
                act_copy(act, s.buf[0:C2, :, C2:P], products.buf[0:C2, :, off + SUB:off + SUB + C2])
                products.read = (dve.mark(), act.mark())
                act.wait(turned, *keys.read)
                act_copy(act, keys.buf[:, :], b.buf[:, 0:P])
                b.read = (act.mark(),)
                k_turned = act.mark()
                dve.wait(dve.mark(), *got("placed", 0))
                reduce(dve, diag[:, :, :], masked[:, :, :].rearrange("p h (l t) -> p h t l", l=DIAG), ALU.add)
                done["summed", 0] = (dve.mark(),)
                act.wait(dve.mark())
                for j in range(P // SUB):
                    act_copy(act, s.buf[j * SUB:(j + 1) * SUB, :, j * SUB:(j + 1) * SUB],
                             diag[j * SUB:(j + 1) * SUB, :, :])
                done["placed", 0] = (act.mark(),)
                return keys, k_turned, s, act.mark()

            def advance(i, keys, k_turned, s, placed):
                tok = i * P
                first_of_sequence = (c * CT + i) % QB == 0
                now, then = (c * CT + i) % 2, (c * CT + i + 1) % 2
                b = back.take()
                pe.wait(k_turned, *b.read)
                for h in range(HEADS_A):
                    r = h * HK
                    matmul(pe, b.buf[r:r + HK, 0:HV], keys.buf[:, r:r + HK], v[par][:, i, h * HV:(h + 1) * HV],
                           tile=(0, r))
                keys.read = (pe.mark(),)
                kv_done, kv = pe.mark(), b
                b = back.take()
                pe.wait(*b.read, *got("state", 0))
                if not first_of_sequence:
                    matmul(pe, b.buf[:, 0:VD], qs[TREE][:, tok:tok + P], state[now][:, :], True, False)
                dve.wait(kv_done, *got("state_read", 0), *got("state", 0))
                for h in range(HEADS_A):
                    r, cols = h * HK, slice(h * HV, (h + 1) * HV)
                    if first_of_sequence:
                        copy(dve, state[then][r:r + HK, cols], kv.buf[r:r + HK, 0:HV])
                    else:
                        fused(dve, state[then][r:r + HK, cols], state[now][r:r + HK, cols],
                              totals[par][TREE][r:r + HK, i:i + 1], kv.buf[r:r + HK, 0:HV], ALU.mult, ALU.add)
                kv.read = (dve.mark(),)
                done["state", 0] = (dve.mark(),)
                pe.wait(placed)
                for h in range(HEADS_A):
                    matmul(pe, b.buf[:, h * HV:(h + 1) * HV], s.buf[:, h, :], v[par][:, i, h * HV:(h + 1) * HV],
                           first_of_sequence, first_of_sequence or h == HEADS_A - 1)
                s.read = done["state_read", 0] = (pe.mark(),)
                act.wait(pe.mark(), *got("o_read", c - 2))
                act_copy(act, o[:, i, :], b.buf[:, 0:VD])
                b.read = (act.mark(),)

            ahead = pair_products(0)
            yield
            for i in range(CT):
                current = ahead
                if i + 1 < CT:
                    ahead = pair_products(i + 1)
                    yield
                advance(i, *current)
                yield
            done["o", c] = (act.mark(),)
            done["recurred", c] = (pe.mark(), dve.mark(), act.mark())

        def finish(c):
            o, x = o_bufs[c % 2], xs[c % X_BUFS]
            groups = lambda ap: ap.rearrange("p t (h n) -> p (t h) n", n=HV)
            dve.wait(*got("o", c), *got("rstd_read", c - 1))
            reduce(dve, sums[:, :], groups(o[:, :, :]), ALU.add)
            dve.wait(dve.mark())
            scalar1(dve, sums[:, :], sums[:, :], 1.0 / HV, ALU.mult)
            dve.wait(dve.mark())
            tensor2(dve, groups(o[:, :, :]), groups(o[:, :, :]), spread(sums[:, :], HV), ALU.subtract)
            act.wait(dve.mark(), *got("projected", c - 1))
            activation(act, o_sq, o[:, :, :], ACT.Square)
            yield
            dve.wait(act.mark(), *got("rstd_read", c - 1))
            reduce(dve, rstd[:, :], groups(o_sq), ALU.add)
            done["squares", c] = (dve.mark(),)
            pool.wait(dve.mark())
            scalar2(pool, rstd[:, :], rstd[:, :], 1.0 / HV, EPS, ALU.mult, ALU.add)
            pool.wait(pool.mark())
            tensor2(pool, rstd[:, :], rstd[:, :], half[:, :], ALU.pow)
            rstd_done = pool.mark()
            yield
            dve.wait(rstd_done)
            tensor2(dve, groups(o[:, :, :]), groups(o[:, :, :]), spread(rstd[:, :], HV), ALU.mult)
            done["rstd_read", c] = (dve.mark(),)
            yield
            wide = lambda ap: ap.unsqueeze(1).to_broadcast([P, CT, VD])
            dve.wait(dve.mark(), *got("gated", c))
            tensor2(dve, o[:, :, :], o[:, :, :], wide(gn_w[:, :]), ALU.mult)
            yield
            dve.wait(dve.mark())
            tensor2(dve, o[:, :, :], o[:, :, :], wide(gn_b[:, :]), ALU.add)
            dve.wait(dve.mark())
            fused(dve, o[:, :, :], o[:, :, :], 0.5, gate[c % 3][:, :, :], ALU.mult, ALU.mult)
            done["gate_read", c] = (dve.mark(),)
            out_ready = dve.mark()
            yield
            yield
            yield
            pe.wait(out_ready)
            for kt in range(KT):
                b = back.take()
                pe.wait(*b.read)
                for i in range(CT):
                    transpose(pe, b.buf[:, i * P:(i + 1) * P], o[:, i, kt * P:(kt + 1) * P], ident[:, :])
                act.wait(pe.mark(), *got("squares", c))
                act_copy(act, o_t[:, kt, :], b.buf)
                b.read = (act.mark(),)
            done["o_read", c] = (pe.mark(),)
            turned = act.mark()
            yield
            for i in range(CT):
                b = back.take()
                pe.wait(turned, *b.read)
                for kt in range(KT):
                    matmul(pe, b.buf[:, 0:DIM], o_t[:, kt, i * P:(i + 1) * P], w_o[:, kt, :], kt == 0, kt == KT - 1)
                dve.wait(pe.mark())
                tensor2(dve, x[:, i, :], x[:, i, :], b.buf[:, 0:DIM], ALU.add)
                b.read = (dve.mark(),)
                yield
            done["projected", c] = (pe.mark(),)
            sp.wait(dve.mark())
            done["stored", c] = (stores[c % X_BUFS].start(sp, token_tiles(x_out)[:, c * CT:(c + 1) * CT, :], x[:, :, :]),)

        pipeline = Pipeline()
        for c in range(-2, CHUNKS + 1):
            pipeline.together(("recur", recur(c)) if 0 <= c < CHUNKS else None,
                              ("finish", finish(c - 1)) if c > 0 else None,
                              ("prepare", prepare(c + 1)) if 0 <= c + 1 < CHUNKS else None,
                              ("normalize", normalize(c + 2)) if c + 2 < CHUNKS else None)
        for s in stores:
            sp.wait((s.sem, s.count))
        core.run()


def feed_forward(core, x_in, x_out, d, tag):
    nc, pe, act, dve, pool, sp, banks = core.nc, core.pe, core.act, core.dve, core.pool, core.sp, core.banks
    with ExitStack() as ctx:
        sb = lambda n, s, dt=F32: ctx.enter_context(nc.sbuf_tensor(f"{tag}_{n}", s, dt))
        lane = lambda n: Lane(ctx.enter_context(nc.semaphore(f"{tag}_{n}")))
        COPIES = 3
        ROWS = COPIES * SUB
        ident = sb("ident", [P, P])
        fc = sb("fc", [P, HT, DIM])
        proj = sb("proj", [P, KT, HIDDEN])
        u, v, fast_b = sb("u", [P, HT, RANK]), sb("v", [RANK, DIM]), sb("fast_b", [RANK, RANK])
        gate = sb("gate", [P, 1])
        fc_t, proj_t = sb("fc_t", [P, KT, HIDDEN], F32R), sb("proj_t", [P, HT, DIM], F32R)
        scale_fc, gate_fc = sb("scale_fc", [P, HT]), sb("gate_fc", [P, HT])
        scale_proj, scale_row = sb("scale_proj", [P, KT]), sb("scale_row", [P, DIM])
        upper, lower = sb("upper", [P, HT]), sb("lower", [P, HT])
        below = Ring([sb(f"below{i}", [P, HIDDEN]) for i in range(2)])
        tern = Ring([sb(f"tern{i}", [P, HIDDEN]) for i in range(2)])
        ones, diagonal = sb("ones", [P, P]), sb("diagonal", [P, P])
        u3 = sb("u3", [P, HT, ROWS])
        u3_t = sb("u3_t", [ROWS, HIDDEN], F32R)
        low_in = sb("low_in", [P, KT, ROWS])
        low_hi, low_lo = sb("low_hi", [P, KT, ROWS], F32R), sb("low_lo", [P, KT, ROWS], F32R)

        X_BUFS = 5
        xs = [sb(f"x{i}", [P, CT, DIM]) for i in range(X_BUFS)]
        xn = Ring([sb(f"xn{i}", [P, DIM]) for i in range(4)])
        x_hi_bufs = [sb(f"x_hi{i}", [P, KT, CHUNK], F32R) for i in range(2)]
        x_lo_bufs = [sb(f"x_lo{i}", [P, KT, CHUNK], F32R) for i in range(2)]
        low_bufs = [sb(f"low{i}", [ROWS, CHUNK], F32R) for i in range(2)]
        relu = Ring([sb(f"relu{i}", [P, CHUNK]) for i in range(2)])
        square = Ring([sb(f"square{i}", [P, CHUNK]) for i in range(2)])
        r_hi = [sb(f"r_hi{i}", [P, HT, CHUNK], F32R) for i in range(2)]
        r_lo = [sb(f"r_lo{i}", [P, HT, CHUNK], F32R) for i in range(2)]
        scaled_out = Ring([sb(f"scaled_out{i}", [P, DIM]) for i in range(2)])

        bank = lambda i: banks[:, i, :]
        front, back = Ring([bank(i) for i in range(5)]), Ring([bank(i) for i in range(5, 8)])
        norm = Normalizer(core, sb, "norm", CT)

        first, weights = lane("first"), lane("weights")
        first.start(sp, fc[:, :, :], d["w_fc"].rearrange("(m p) n -> p m n", p=P))
        first_loaded = first.start(sp, ident[:, :], d["c_ident"])
        weights.start(sp, proj[:, :, :], d["w_proj"].rearrange("(m p) n -> p m n", p=P))
        weights.start(sp, u[:, :, :], d["u"].rearrange("(m p) n -> p m n", p=P))
        weights.start(sp, v[:, :], d["v"])
        weights.start(sp, fast_b[:, :], d["fast_b"])
        loaded = weights.start(sp, gate[:, :], d["gate"].to_broadcast([P, 1]))
        memset(pool, ones[:, :], 1.0)
        memset(pool, u3[:, :, :], 0.0)
        memset(pool, low_in[:, :, :], 0.0)
        zeroed = pool.mark()
        for e in (pe, act, dve, pool):
            e.wait(first_loaded, zeroed)

        def ternary(w, rows, cols, scale, out_t):
            reduce(dve, scale[:, 0:rows], w[:, :, :], ALU.add, absolute=True)
            dve.wait(dve.mark())
            scalar2(dve, scale[:, 0:rows], scale[:, 0:rows], 1.0 / (cols * P), 1e-5, ALU.mult, ALU.max)
            dve.wait(dve.mark())
            scalar1(dve, upper[:, 0:rows], scale[:, 0:rows], 0.5, ALU.mult)
            scalar1(dve, lower[:, 0:rows], scale[:, 0:rows], -0.5, ALU.mult)
            dve.wait(dve.mark())
            pool.wait(dve.mark())
            for m in range(rows):
                lt, s, width = below.take(), tern.take(), cols * P
                pool.wait(*lt.read)
                scalar1(pool, lt.buf[:, 0:width], w[:, m, :], lower[:, m:m + 1], ALU.is_lt)
                dve.wait(pool.mark(), *s.read)
                fused(dve, s.buf[:, 0:width], w[:, m, :], upper[:, m:m + 1], lt.buf[:, 0:width], ALU.is_gt, ALU.subtract)
                lt.read, made = (dve.mark(),), dve.mark()
                for n in range(0, cols, CT):
                    b, count = front.take(), min(CT, cols - n)
                    pe.wait(made, *b.read)
                    for i in range(count):
                        transpose(pe, b.buf[:, i * P:(i + 1) * P], s.buf[:, (n + i) * P:(n + i + 1) * P], ident[:, :])
                    s.read = (pe.mark(),)
                    act.wait(pe.mark())
                    act_copy(act, out_t[:, n:n + count, m * P:(m + 1) * P],
                             b.buf[:, 0:count * P].rearrange("p (i n) -> p i n", n=P))
                    b.read = (act.mark(),)

        ternary(fc, HT, KT, scale_fc, fc_t)
        for e in (pe, act, dve, pool):
            e.wait(loaded)
        dve.do(lambda e: e.reciprocal(gate_fc[:, :], scale_fc[:, :]))
        dve.wait(dve.mark())
        scalar1(dve, gate_fc[:, :], gate_fc[:, :], gate[:, 0:1], ALU.mult)
        dve.wait(dve.mark())
        tensor2(dve, u[:, :, :], u[:, :, :], spread(gate_fc[:, :], RANK), ALU.mult)
        dve.wait(dve.mark())
        for i in range(COPIES):
            copy(dve, u3[:, :, i * SUB:i * SUB + RANK], u[:, :, :])
        u3_done = dve.mark()
        for m in range(HT):
            b, cols = front.take(), slice(m * P, (m + 1) * P)
            pe.wait(u3_done, *b.read)
            transpose(pe, b.buf[0:ROWS, 0:P], u3[:, m, :], ident[:, :])
            dve.wait(pe.mark())
            copy(dve, u3_t[:, cols], b.buf[0:ROWS, 0:P])
            dve.wait(dve.mark())
            last = slice(ROWS - SUB, ROWS)
            tensor2(dve, u3_t[last, cols], b.buf[last, 0:P], u3_t[last, cols].bitcast(F32), ALU.subtract)
            b.read = (dve.mark(),)
        for kt in range(KT):
            b = front.take()
            pe.wait(*b.read)
            matmul(pe, b.buf[:, 0:RANK], v[:, kt * P:(kt + 1) * P], fast_b[:, :])
            dve.wait(pe.mark())
            for i in range(COPIES):
                copy(dve, low_in[:, kt, i * SUB:i * SUB + RANK], b.buf[:, 0:RANK])
            b.read = (dve.mark(),)
        dve.wait(dve.mark())
        copy(dve, low_hi[:, :, :], low_in[:, :, :])
        dve.wait(dve.mark())
        tensor2(dve, low_lo[:, :, :], low_in[:, :, :], low_hi[:, :, :].bitcast(F32), ALU.subtract)
        ternary(proj, KT, HT, scale_proj, proj_t)
        for kt in range(KT):
            b = front.take()
            dve.wait(*(() if kt == 0 else (pe.mark(),)))
            scalar1(dve, diagonal[:, :], ident[:, :], scale_proj[:, kt:kt + 1], ALU.mult)
            pe.wait(dve.mark(), *b.read)
            matmul(pe, b.buf[:, 0:P], ones[:, :], diagonal[:, :])
            act.wait(pe.mark())
            act_copy(act, scale_row[:, kt * P:(kt + 1) * P], b.buf[:, 0:P])
            b.read = (act.mark(),)
        pe.wait(act.mark(), dve.mark())
        dve.wait(act.mark())

        done = {}
        got = lambda what, c: done.get((what, c), ())
        loads, stores = [lane(f"load{i}") for i in range(X_BUFS)], [lane(f"store{i}") for i in range(X_BUFS)]

        def load_x(c):
            if c < CHUNKS:
                sp.wait(*got("stored", c - X_BUFS))
                done["x", c] = (loads[c % X_BUFS].start(sp, xs[c % X_BUFS][:, :, :],
                                                        token_tiles(x_in)[:, c * CT:(c + 1) * CT, :]),)

        def normalize(c):
            x, x_hi, x_lo, low = xs[c % X_BUFS], x_hi_bufs[c % 2], x_lo_bufs[c % 2], low_bufs[c % 2]
            load_x(c + 2)
            rstd_done = norm.statistics(x, got("x", c))
            yield
            dve.wait(rstd_done)
            slots = []
            for i in range(CT):
                s = xn.take()
                dve.wait(*s.read)
                norm.scale(s.buf[:, :], x, i)
                slots.append((s, dve.mark()))
            norm.applied = (dve.mark(),)
            yield
            for kt in range(KT):
                b = front.take()
                pe.wait(*b.read)
                for i, (s, scaled) in enumerate(slots):
                    pe.wait(scaled)
                    transpose(pe, b.buf[:, i * P:(i + 1) * P], s.buf[:, kt * P:(kt + 1) * P], ident[:, :])
                    s.read = (pe.mark(),)
                act.wait(pe.mark(), *got("x_read", c - 2))
                act_copy(act, x_hi[:, kt, :], b.buf)
                dve.wait(act.mark(), *got("x_read", c - 2))
                tensor2(dve, x_lo[:, kt, :], b.buf, x_hi[:, kt, :].bitcast(F32), ALU.subtract)
                b.read = (dve.mark(),)
                yield
            x_done = dve.mark()
            yield
            b = front.take()
            pe.wait(x_done, *b.read)
            passes = [(kt, w, s) for kt in range(KT) for w, s in ((low_hi, x_hi), (low_hi, x_lo), (low_lo, x_hi))]
            for n, (kt, w, s) in enumerate(passes):
                matmul(pe, b.buf[0:ROWS, :], w[:, kt, :], s[:, kt, :], n == 0, n == len(passes) - 1)
            act.wait(pe.mark(), *got("x_read", c - 2))
            act_copy(act, low[:, :], b.buf[0:ROWS, :])
            dve.wait(act.mark())
            tensor2(dve, low[SUB:2 * SUB, :], b.buf[SUB:2 * SUB, :], low[SUB:2 * SUB, :].bitcast(F32), ALU.subtract)
            b.read = (dve.mark(),)
            done["x_parts", c] = (dve.mark(),)

        def up(c):
            par, x_hi, x_lo, low = c % 2, x_hi_bufs[c % 2], x_lo_bufs[c % 2], low_bufs[c % 2]
            pe.wait(*got("x_parts", c))
            for m in range(HT):
                b, cols = front.take(), slice(m * P, (m + 1) * P)
                pe.wait(*b.read)
                for kt in range(KT):
                    matmul(pe, b.buf, fc_t[:, kt, cols], x_hi[:, kt, :], kt == 0, False)
                    matmul(pe, b.buf, fc_t[:, kt, cols], x_lo[:, kt, :], False, False)
                matmul(pe, b.buf, u3_t[:, cols], low[:, :], False, True)
                r, sq = relu.take(), square.take()
                act.wait(pe.mark(), *r.read)
                activation(act, r.buf[:, :], b.buf, ACT.Relu, scale=scale_fc[:, m:m + 1])
                b.read = (act.mark(),)
                act.wait(act.mark(), *sq.read)
                activation(act, sq.buf[:, :], r.buf[:, :], ACT.Square)
                dve.wait(act.mark(), *got("down", c - 2))
                copy(dve, r_hi[par][:, m, :], sq.buf[:, :])
                dve.wait(dve.mark())
                tensor2(dve, r_lo[par][:, m, :], sq.buf[:, :], r_hi[par][:, m, :].bitcast(F32), ALU.subtract)
                sq.read = (dve.mark(),)
                yield
            done["x_read", c] = (pe.mark(),)
            done["up", c] = (dve.mark(),)

        def down(c):
            par, x = c % 2, xs[c % X_BUFS]
            pe.wait(*got("up", c))
            for i in range(CT):
                b = back.take()
                pe.wait(*b.read)
                for m in range(HT):
                    for r in (r_hi, r_lo):
                        matmul(pe, b.buf[:, 0:DIM], r[par][:, m, i * P:(i + 1) * P], proj_t[:, m, :],
                               m == 0 and r is r_hi, m == HT - 1 and r is r_lo)
                    if m == HT // 2:
                        yield
                s = scaled_out.take()
                dve.wait(pe.mark(), *s.read)
                tensor2(dve, s.buf[:, :], b.buf[:, 0:DIM], scale_row[:, :], ALU.mult)
                b.read = (dve.mark(),)
                pool.wait(dve.mark())
                tensor2(pool, x[:, i, :], x[:, i, :], s.buf[:, :], ALU.add)
                s.read = (pool.mark(),)
                yield
            done["down", c] = (pe.mark(),)
            sp.wait(pool.mark())
            done["stored", c] = (stores[c % X_BUFS].start(sp, token_tiles(x_out)[:, c * CT:(c + 1) * CT, :], x[:, :, :]),)

        load_x(0)
        load_x(1)
        pipeline = Pipeline()
        for c in range(-2, CHUNKS):
            pipeline.together(("down", down(c)) if c >= 0 else None,
                              ("up", up(c + 1)) if 0 <= c + 1 < CHUNKS else None,
                              ("normalize", normalize(c + 2)) if c + 2 < CHUNKS else None)
        for s in stores:
            sp.wait((s.sem, s.count))
        core.run()


def attention(core, x_in, x_out, d):
    nc, pe, act, dve, pool, sp, banks = core.nc, core.pe, core.act, core.dve, core.pool, core.sp, core.banks
    with ExitStack() as ctx:
        sb = lambda n, s, dt=F32: ctx.enter_context(nc.sbuf_tensor("b_" + n, s, dt))
        lane = lambda n: Lane(ctx.enter_context(nc.semaphore("b_" + n)))
        GW = GROUP * HD
        VW = HD + 1
        SLOT = P // GROUP

        ident, ident_b = sb("ident", [P, P]), sb("ident_b", [P, P], BF16)
        tables = sb("tables", [P, HEADS, P], BF16)
        w_qk = sb("w_qk", [P, KT, GROUPS, 2 * GW])
        w_v, w_out = sb("w_v", [P, KT, DIM]), sb("w_out", [P, KT, DIM])
        b_qk, scale_qk = sb("b_qk", [P, GROUPS]), sb("scale_qk", [P, 1])
        b_v, b_out = sb("b_v", [P, DIM]), sb("b_out", [P, DIM])
        SETS = 3
        q_stack = sb("q_stack", [STACK, SETS * GROUP, SEQ], F32R)
        k_stack = sb("k_stack", [STACK, SETS * GROUP, SEQ], F32R)
        X_BUFS = 2
        AHEAD = 1.15
        xs = [sb(f"x{i}", [P, QB, DIM]) for i in range(X_BUFS)]
        xn = Ring([sb(f"xn{i}", [P, DIM]) for i in range(2)])
        xn_ts = [sb(f"xn_t{i}", [P, KT, SEQ]) for i in range(2)]
        qk = Ring([sb("qk", [P, BANK])])
        qk_hi, qk_lo = sb("qk_hi", [P, SEQ], F32R), sb("qk_lo", [P, SEQ], F32R)
        vs = [sb(f"v{i}", [P, QB, HEADS, VW]) for i in range(2)]
        half_max = sb("half_max", [P, GROUP * QB, HALVES])
        row_max = sb("row_max", [P, 2, GROUP * QB])
        shift = sb("shift", [2 * GROUP * QB, P], F32R)
        p_t = Ring([sb(f"p_t{i}", [P, 2, BANK]) for i in range(4)])
        pv = sb("pv", [P, BANK])
        recip = sb("recip", [P, CT * GROUP])
        att = sb("att", [P, QB, DIM])
        att_t = Ring([sb(f"att_t{i}", [P, KT, P]) for i in range(2)])
        shift_dram = [nc.dram_tensor(f"b_shift_dram{i}", (2, GROUP, SEQ), F32R, kind="Internal").ap() for i in range(2)]

        scores = Ring([banks[:, 0:2, :], banks[:, 2:4, :]])
        values = Slot(banks[:, 4, :])
        misc = Ring([banks[:, i, :] for i in (5, 6, 7)])
        norm = Normalizer(core, sb, "norm", QB)

        done = {}
        got = lambda what, g: done.get((what, g), ())
        stack_lane = [lane(f"stack{i}") for i in range(SETS)]
        shift_out, shift_in = lane("shift_out"), [lane(f"shift_in{i}") for i in range(2)]

        loads, stores = [lane(f"load{i}") for i in range(X_BUFS)], [lane(f"store{i}") for i in range(X_BUFS)]

        def load_x(b):
            if b < BATCH:
                sp.wait(*got("stored", b - X_BUFS))
                done["x", b] = (loads[b % X_BUFS].start(sp, xs[b % X_BUFS][:, :, :],
                                                        token_tiles(x_in)[:, b * QB:(b + 1) * QB, :]),)

        weights, bias_lane, tables_lane = lane("weights"), lane("bias"), lane("tables")
        first = lane("first")
        k_bias = nc.dram_tensor("b_k_bias", (HEADS, BIASROWS, SEQ), F32R, kind="Internal").ap()
        bias_cast = bias_lane.start(pool, k_bias, d["c_kbias"])
        every_slot = lambda ap: ap.unsqueeze(1).to_broadcast([ap.shape[0], SETS * GROUP, SEQ])
        tables_lane.start(pool, q_stack[MAIN:SHIFTROW, :, :], every_slot(d["c_qrows"]))
        tables_lane.start(pool, k_stack[MAIN + BIASROWS:STACK, :, :], every_slot(d["c_krows"]))
        tables_cast = tables_lane.start(pool, tables[:, :, :], d["c_block"])
        ident_loaded = first.start(sp, ident[:, :], d["c_ident"])
        load_x(0)
        for kt in range(KT):
            rows = d["Wqkv"][kt * P:(kt + 1) * P, :]
            for part in range(2):
                weights.start(sp, w_qk[:, kt, :, part * GW:(part + 1) * GW],
                              rows[:, part * DIM:(part + 1) * DIM].rearrange("p (g n) -> p g n", g=GROUPS))
            weights.start(sp, w_v[:, kt, :], rows[:, 2 * DIM:3 * DIM])
        weights.start(sp, w_out[:, :, :], d["Wout"].rearrange("(k p) n -> p k n", p=P))
        for g in range(GROUPS):
            for part in range(2):
                lo = part * DIM + g * GW
                weights.start(sp, b_qk[part * GW:(part + 1) * GW, g:g + 1],
                              d["bqkv"][lo:lo + GW].rearrange("(p a) -> p a", a=1))
        weights.start(sp, b_v[:, :], d["bqkv"][2 * DIM:3 * DIM].partition_broadcast(P))
        weights.start(sp, scale_qk[:, :], d["c_qkscale"])
        loaded = weights.start(sp, b_out[:, :], d["bout"].partition_broadcast(P))
        for v in vs:
            memset(dve, v[:, :, :, HD:VW], 1.0)
        filled = pool.mark()
        memset(dve, values.buf, 0.0)
        for e in (pe, act, dve, pool):
            e.wait(ident_loaded, filled, dve.mark())
        copy(dve, ident_b[:, :], ident[:, :])
        pe.wait(dve.mark())

        def add_block_bias(out, h):
            matmul(pe, out, ident_b[:, :], tables[:, h, :], False, True)

        def normalize(b):
            x, xn_t = xs[b % X_BUFS], xn_ts[b % 2]
            rstd_done = norm.statistics(x, got("x", b))
            dve.wait(rstd_done)
            yield
            for i in range(0, QB, 2):
                scaled = []
                for j in range(2):
                    s = xn.take()
                    dve.wait(*s.read)
                    norm.scale(s.buf[:, :], x, i + j)
                    scaled.append((s, dve.mark()))
                yield
                m = misc.take()
                pe.wait(*m.read)
                for j, (s, done_scaling) in enumerate(scaled):
                    pe.wait(done_scaling)
                    for kt in range(KT):
                        at = (kt * 2 + j) * P
                        transpose(pe, m.buf[:, at:at + P], s.buf[:, kt * P:(kt + 1) * P], ident[:, :])
                    s.read = (pe.mark(),)
                act.wait(pe.mark(), *got("projected", b - 2), *got("v_made", b - 2))
                act_copy(act, xn_t[:, :, i * P:(i + 2) * P], m.buf.rearrange("p (k n) -> p k n", k=KT))
                m.read = (act.mark(),)
                yield
            norm.applied = (dve.mark(),)
            done["xn", b] = (act.mark(),)

        def make_values(b):
            xn_t, v = xn_ts[b % 2], vs[b % 2]
            by_head = lambda ap: ap.rearrange("p (h n) -> p h n", n=HD)
            pe.wait(loaded, *got("xn", b))
            dve.wait(loaded)
            for i in range(QB):
                m = misc.take()
                pe.wait(*m.read)
                for kt in range(KT):
                    matmul(pe, m.buf[:, 0:DIM], xn_t[:, kt, i * P:(i + 1) * P], w_v[:, kt, :],
                           kt == 0, kt == KT - 1)
                dve.wait(pe.mark(), *got("weighed", (b - 1) * GROUPS - 1))
                tensor2(dve, v[:, i, :, 0:HD], by_head(m.buf[:, 0:DIM]), by_head(b_v[:, :]), ALU.add)
                m.read = (dve.mark(),)
                yield
            done["v_made", b] = (pe.mark(), dve.mark())

        def make_stacks(g):
            b, hg, slot0 = g // GROUPS, g % GROUPS, g % SETS * GROUP
            xn_t = xn_ts[b % 2]
            pe.wait(loaded, *got("xn", b))
            dve.wait(loaded)
            for half in range(HALVES):
                m, s, cols = misc.take(), qk.take(), slice(half * BANK, (half + 1) * BANK)
                pe.wait(*m.read)
                for kt in range(KT):
                    matmul(pe, m.buf, w_qk[:, kt, hg, :], xn_t[:, kt, cols], kt == 0, kt == KT - 1)
                dve.wait(pe.mark(), *s.read)
                scalar2(dve, s.buf[:, :], m.buf, b_qk[:, hg:hg + 1], scale_qk[:, 0:1], ALU.add, ALU.mult)
                m.read = (dve.mark(),)
                act.wait(dve.mark(), *got("stacked", g - 1))
                act_copy(act, qk_hi[:, cols], s.buf[:, :])
                pool.wait(act.mark(), *got("stacked", g - 1))
                tensor2(pool, qk_lo[:, cols], s.buf[:, :], qk_hi[:, cols].bitcast(F32), ALU.subtract)
                s.read = (pool.mark(),)
                yield
            done["qk", g] = (pe.mark(),)
            if hg == GROUPS - 1:
                done["projected", b] = (pe.mark(),)
            sp.wait(bias_cast, act.mark(), pool.mark(), *got("scored", g - SETS))
            for i in range(GROUP):
                s, rows_q = slot0 + i, slice(i * HD, (i + 1) * HD)
                rows_k = slice(GW + i * HD, GW + (i + 1) * HD)
                for at, (qpart, kpart) in enumerate(((qk_hi, qk_hi), (qk_hi, qk_lo), (qk_lo, qk_hi))):
                    to = slice(at * HD, (at + 1) * HD)
                    stack_lane[g % SETS].start(sp, words(q_stack[to, s, :]), words(qpart[rows_q, :]))
                    stack_lane[g % SETS].start(sp, words(k_stack[to, s, :]), words(kpart[rows_k, :]))
                stacked = stack_lane[g % SETS].start(sp, words(k_stack[MAIN:MAIN + BIASROWS, s, :]), words(k_bias[hg * GROUP + i]))
            done["stacked", g] = (stacked,)

        def find_maxima(g):
            hg, slot0 = g % GROUPS, g % SETS * GROUP
            pe.wait(tables_cast, *got("stacked", g))
            for i in range(GROUP):
                for qb in range(QB):
                    s = slot0 + i
                    for half in range(HALVES):
                        m = misc.take()
                        pe.wait(*m.read)
                        here = qb // CT == half
                        matmul(pe, m.buf, q_stack[0:SHIFTROW, s, qb * P:(qb + 1) * P],
                               k_stack[0:SHIFTROW, s, half * BANK:(half + 1) * BANK], True, not here)
                        if here:
                            at = qb % CT * P
                            add_block_bias(m.buf[:, at:at + P], hg * GROUP + i)
                        dve.wait(pe.mark(), *got("max", g - 1))
                        reduce(dve, half_max[:, i * QB + qb, half:half + 1], m.buf, ALU.max, negate=True)
                        m.read = (dve.mark(),)
                    yield
            dve.wait(dve.mark(), *got("turned", g - 1))
            reduce(dve, row_max[:, 0, :], half_max[:, :, :], ALU.min)
            done["max", g] = (dve.mark(),)
            dve.wait(dve.mark())
            copy(dve, row_max[:, 1, :], row_max[:, 0, :])
            m = misc.take()
            pe.wait(dve.mark(), *m.read)
            rows = 2 * GROUP * QB
            transpose(pe, m.buf[0:rows, 0:P], row_max[:, :, :].rearrange("p a n -> p (a n)"), ident[:, :])
            done["turned", g] = (pe.mark(),)
            act.wait(pe.mark(), *got("shift_out", g - 1))
            act_copy(act, shift[:, :], m.buf[0:rows, 0:P])
            dve.wait(act.mark())
            lo = slice(rows // 2, rows)
            tensor2(dve, shift[lo, :], m.buf[lo, 0:P], shift[lo, :].bitcast(F32), ALU.subtract)
            m.read = (dve.mark(),)
            sp.wait(dve.mark(), *got("shift_in", g - 2))
            out = shift_out.start(sp, words(shift_dram[g % 2].rearrange("a h (b n) -> (a h b) n", n=P)), words(shift[:, :]))
            done["shift_out", g] = (out,)
            sp.wait(out)
            done["shift_in", g] = (shift_in[g % 2].start(sp, words(q_stack[SHIFTROW:STACK, slot0:slot0 + GROUP, :]), words(shift_dram[g % 2])),)

        weighing, tails = [], []

        def weigh():
            g, half, kb, made = weighing.pop(0)
            hg, v = g % GROUPS, vs[g // GROUPS % 2]
            if kb == 0:
                pe.wait(*values.read)
            pe.wait(*(exponentials for _, exponentials in made))
            for i in range(GROUP):
                slot = made[i % 2][0]
                matmul(pe, values.buf[i * SLOT:i * SLOT + VW, :], v[:, kb, hg * GROUP + i, :],
                       slot.buf[:, i // 2, :], kb == 0, kb == QB - 1, tile=(0, i * SLOT))
            for slot, _ in made:
                slot.read = (pe.mark(),)
            if kb == QB - 1:
                done["weighed", g] = (pe.mark(),)
                act.wait(pe.mark(), *got("pv_read", 0))
                act_copy(act, pv[:, :], values.buf)
                values.read = (act.mark(),)
                tails.append(conclude(g, half, act.mark()))

        def advance_tail():
            if tails and next(tails[0], tails) is tails:
                tails.pop(0)

        def conclude(g, half, copied):
            b, hg = g // GROUPS, g % GROUPS
            m = misc.take()
            pe.wait(copied, *m.read)
            for i in range(CT):
                transpose(pe, m.buf[:, i * P:(i + 1) * P], pv[:, i * P:(i + 1) * P], ident[:, :])
            done["pv_read", 0] = (pe.mark(),)
            slots = m.buf.rearrange("p (t h n) -> p t h n", t=CT, h=GROUP)
            dve.wait(pe.mark(), *got("att_read", b - 1), *got("normalized", 0))
            dve.do(lambda e: e.reciprocal(recip[:, :].rearrange("p (t h) -> p t h", t=CT), slots[:, :, :, HD]))
            dve.wait(dve.mark())
            tensor2(dve, att[:, half * CT:(half + 1) * CT, hg * GW:(hg + 1) * GW].rearrange("p t (h n) -> p t h n", n=HD),
                    slots[:, :, :, 0:HD], spread(recip[:, :].rearrange("p (t h) -> p t h", t=CT), HD), ALU.mult)
            m.read = done["normalized", 0] = (dve.mark(),)
            yield
            if (hg, half) != (GROUPS - 1, HALVES - 1):
                return
            pe.wait(*done["normalized", 0])
            turned = []
            for i in range(QB + 1):
                if i < QB:
                    m, t = misc.take(), att_t.take()
                    pe.wait(*m.read)
                    for kt in range(KT):
                        transpose(pe, m.buf[:, kt * P:(kt + 1) * P], att[:, i, kt * P:(kt + 1) * P], ident[:, :])
                    act.wait(pe.mark(), *t.read)
                    act_copy(act, t.buf[:, :, :], m.buf[:, 0:DIM].rearrange("p (k n) -> p k n", k=KT))
                    m.read = (act.mark(),)
                    done["att_read", b] = (pe.mark(),)
                    turned.append((t, act.mark()))
                    if i == 0:
                        continue
                t, copied = turned[i - 1]
                m = misc.take()
                pe.wait(copied, *m.read)
                for kt in range(KT):
                    matmul(pe, m.buf[:, 0:DIM], t.buf[:, kt, :], w_out[:, kt, :], kt == 0, kt == KT - 1)
                t.read = (pe.mark(),)
                tile = xs[b % X_BUFS][:, i - 1, :]
                dve.wait(pe.mark())
                tensor2(dve, tile, tile, m.buf[:, 0:DIM], ALU.add)
                m.read = (dve.mark(),)
                pool.wait(dve.mark())
                tensor2(pool, tile, tile, b_out[:, :], ALU.add)
                yield
            sp.wait(pool.mark())
            done["stored", b] = (stores[b % X_BUFS].start(sp, token_tiles(x_out)[:, b * QB:(b + 1) * QB, :],
                                                          xs[b % X_BUFS][:, :, :]),)
            load_x(b + 2)

        def attend(g):
            b, hg, slot0 = g // GROUPS, g % GROUPS, g % SETS * GROUP
            pe.wait(*got("shift_in", g), *got("v_made", b))
            for half in range(HALVES):
                qcols = slice(half * BANK, (half + 1) * BANK)
                for kb in range(QB):
                    made = []
                    for pair in range(2):
                        sc = scores.take()
                        pe.wait(*sc.read)
                        for j in range(2):
                            i = pair + 2 * j
                            here = kb // CT == half
                            matmul(pe, sc.buf[:, j, :], k_stack[0:STACK, slot0 + i, kb * P:(kb + 1) * P],
                                   q_stack[0:STACK, slot0 + i, qcols], True, not here)
                            if here:
                                at = kb % CT * P
                                add_block_bias(sc.buf[:, j, at:at + P], hg * GROUP + i)
                        s = p_t.take()
                        act.wait(pe.mark(), *s.read)
                        activation(act, s.buf[:, :, :], sc.buf, ACT.Exp, scale=slopes()[pair][0])
                        sc.read = (act.mark(),)
                        made.append((s, act.mark()))
                        if pair == 0:
                            yield
                    if weighing:
                        weigh()
                    weighing.append((g, half, kb, made))
                    yield
                    advance_tail()
            done["scored", g] = (pe.mark(),)

        load_x(1)
        groups = BATCH * GROUPS
        pipeline = Pipeline()
        for g in range(1 - GROUPS, groups):
            b, last = (g - 1) // GROUPS + 1, g % GROUPS == GROUPS - 1
            pipeline.together(
                ("attend", attend(g)) if g >= 0 else None,
                ("maxima", find_maxima(g + 1), AHEAD) if 0 <= g + 1 < groups else None,
                ("stacks", make_stacks(g + 2), 3 * AHEAD) if 0 <= g + 2 < groups else None,
                ("values", make_values(b)) if last and b < BATCH else None,
                ("normalize", normalize(b)) if g % GROUPS == 1 and b < BATCH else None)
        weigh()
        while tails:
            advance_tail()
        for s in stores:
            sp.wait((s.sem, s.count))
        core.run()


def build(nc, d, out):
    with ExitStack() as ctx:
        core = Core(nc, ctx)
        between = [nc.dram_tensor(f"x{i}", (BATCH, SEQ, DIM), F32, kind="Internal").ap() for i in range(3)]
        recurrent_mixer(core, d["hidden_states"], between[0], d)
        feed_forward(core, between[0], between[1], d, "ffn1")
        attention(core, between[1], between[2], d)
        feed_forward(core, between[2], out, d, "ffn2")


BY_PARTITION = ("mu_x", "x_bias")
TRANSPOSED = ("W_x1", "W_x2", "W_r", "W_k", "W_v", "W_g", "A_w", "B_w", "W_o", "fast_b")


def lay_out(name, a):
    a = np.asarray(a)
    if name in TRANSPOSED:
        a = a.T
    if name in BY_PARTITION:
        a = np.moveaxis(a.reshape(a.shape[:-1] + (-1, P)), -1, 0)
    return np.ascontiguousarray(a.reshape(1, 1) if a.ndim == 0 else a)


def kernel(**inputs):
    import concourse.bacc as bacc
    from concourse.bass_utils import run_bass_kernel_spmd

    nc = bacc.Bacc("TRN2", target_bir_lowering=False, num_devices=1)
    arrays, d = {}, {}
    for name, a in list(inputs.items()) + list(constants().items()):
        short = name.replace("L0_attn_a_", "").replace("L0_attn_b_", "").replace("L0_ffn_", "")
        a = lay_out(short, a)
        arrays[short] = a
        d[short] = nc.dram_tensor(short, a.shape, mybir.dt.from_np(a.dtype), kind="ExternalInput").ap()
    out = nc.dram_tensor("out", (BATCH, SEQ, DIM), F32, kind="ExternalOutput").ap()
    build(nc, d, out)
    return run_bass_kernel_spmd(nc, [arrays], core_ids=[0]).results[0]["out"]
```
